# Optimizing a Trainium2 kernel written in Bass

```python
import numpy as np
import jax
import jax.numpy as jnp

def _softmax(x, axis=-1):
    return jax.nn.softmax(x, axis=axis)

def _gelu(x):
    return jax.nn.gelu(x, approximate=True)

def _silu(x):
    return jax.nn.silu(x)

def _sigmoid(x):
    return jax.nn.sigmoid(x)

def _layernorm(x, axis=-1, eps=1e-05):
    m = jnp.mean(x, axis=axis, keepdims=True)
    v = jnp.var(x, axis=axis, keepdims=True)
    return (x - m) / jnp.sqrt(v + eps)

def _scatter_add(tgt, idx, src, axis=0):
    return tgt.at[idx].add(src)

def _segment_sum(src, seg, n):
    return jax.ops.segment_sum(src, seg, n)
kernel_name = 'mk_conv_attn_hybrid_d4_conv_nchw256_r2_f30335'

def setup_inputs(seed: int=0):
    np.random.seed(seed)
    _w = jnp.asarray

    def _rec_inputs():
        import jax
        import jax.numpy as jnp
        _gk = jax.random.key(seed)
        x = 7.22e-05 + 1 * jax.random.normal(jax.random.fold_in(_gk, 1), (8, 128, 32, 32), jnp.float32)
        return x
    x = _rec_inputs()

    def _L0_conv_setup():
        import jax, jax.numpy as jnp
        import numpy as np
        from jax import lax
        K = 3
        STRIDE = 1
        PAD = 1
        DIL = 1

        def _bilinear_gather(x, py, px):
            B, C, H, W = x.shape
            y0 = jnp.floor(py)
            x0 = jnp.floor(px)
            ly = py - y0
            lx = px - x0
            xf = x.reshape(B, C, H * W)

            def corner(yi, xi, wgt):
                valid = (yi >= 0) & (yi < H) & (xi >= 0) & (xi < W)
                yc = jnp.clip(yi, 0, H - 1).astype(jnp.int32)
                xc = jnp.clip(xi, 0, W - 1).astype(jnp.int32)
                idx = (yc * W + xc).reshape(B, 1, -1)
                v = jnp.take_along_axis(xf, idx, axis=2)
                return v * (wgt * valid.astype(x.dtype)).reshape(B, 1, -1)
            acc = corner(y0, x0, (1 - ly) * (1 - lx)) + corner(y0, x0 + 1, (1 - ly) * lx) + corner(y0 + 1, x0, ly * (1 - lx)) + corner(y0 + 1, x0 + 1, ly * lx)
            return acc.reshape(B, C, py.shape[1], py.shape[2], py.shape[3])

        def deform_conv2d(x, offset_w, offset_b, weight, bias):
            B, C, H, W = x.shape
            off = lax.conv_general_dilated(x, offset_w, window_strides=(STRIDE, STRIDE), padding=[(PAD, PAD), (PAD, PAD)], rhs_dilation=(DIL, DIL))
            off = off + offset_b[None, :, None, None]
            Ho, Wo = (off.shape[2], off.shape[3])
            off = off.reshape(B, K * K, 2, Ho, Wo)
            dy = off[:, :, 0].transpose(0, 2, 3, 1)
            dx = off[:, :, 1].transpose(0, 2, 3, 1)
            ki, kj = jnp.meshgrid(jnp.arange(K), jnp.arange(K), indexing='ij')
            base_y = (jnp.arange(Ho) * STRIDE - PAD)[:, None, None] + (ki.reshape(-1) * DIL)[None, None, :]
            base_x = (jnp.arange(Wo) * STRIDE - PAD)[None, :, None] + (kj.reshape(-1) * DIL)[None, None, :]
            py = base_y[None].astype(x.dtype) + dy
            px = base_x[None].astype(x.dtype) + dx
            sampled = _bilinear_gather(x, py, px)
            Oc = weight.shape[0]
            out = jnp.einsum('bchwk,ock->bohw', sampled, weight.reshape(Oc, C, K * K))
            return out + bias[None, :, None, None]
        key = jax.random.key(seed)
        k1, k2, k3 = jax.random.split(key, 3)
        B, C, H, W = (8, 128, 32, 32)
        Oc = 128
        return {'x': jax.random.normal(k1, (B, C, H, W), dtype=jnp.float32), 'offset_w': jax.random.normal(k2, (2 * K * K, C, K, K), dtype=jnp.float32) * 0.01, 'offset_b': jnp.zeros((2 * K * K,), dtype=jnp.float32), 'weight': jax.random.normal(k3, (Oc, C, K, K), dtype=jnp.float32) * (1.0 / np.sqrt(C * K * K)), 'bias': jnp.zeros((Oc,), dtype=jnp.float32)}
    _L0_conv_all = _L0_conv_setup()
    _L0_conv_in = {k: v for k, v in _L0_conv_all.items() if k in ('offset_w', 'offset_b', 'weight', 'bias')}
    del _L0_conv_all

    def _L1_conv_setup():
        import jax, jax.numpy as jnp
        import numpy as np
        B, C, H, W = (4, 128, 32, 32)
        C8 = C // 8
        key = jax.random.key(seed)
        ks = jax.random.split(key, 9)
        s_in = 1.0 / np.sqrt(C)
        return {'x': jax.random.normal(ks[0], (B, C, H, W), dtype=jnp.float32), 'Wq': jax.random.normal(ks[1], (C8, C), dtype=jnp.float32) * s_in, 'bq': jax.random.normal(ks[2], (C8,), dtype=jnp.float32) * 0.01, 'Wk': jax.random.normal(ks[3], (C8, C), dtype=jnp.float32) * s_in, 'bk': jax.random.normal(ks[4], (C8,), dtype=jnp.float32) * 0.01, 'Wv': jax.random.normal(ks[5], (C, C), dtype=jnp.float32) * s_in, 'bv': jax.random.normal(ks[6], (C,), dtype=jnp.float32) * 0.01, 'Wo': jax.random.normal(ks[7], (C, C), dtype=jnp.float32) * s_in, 'bo': jax.random.normal(ks[8], (C,), dtype=jnp.float32) * 0.01}
    _L1_conv_all = _L1_conv_setup()
    _L1_conv_in = {k: v for k, v in _L1_conv_all.items() if k in ('Wq', 'bq', 'Wk', 'bk', 'Wv', 'bv', 'Wo', 'bo')}
    del _L1_conv_all

    def _L2_attn_setup():
        import jax, jax.numpy as jnp
        import numpy as np
        B, S, D = (4, 2048, 128)
        HURST = 0.1

        def _fractional_log_bias(seq_len):
            idx = jnp.arange(seq_len, dtype=jnp.float32)
            time_diffs = jnp.abs(idx[:, None] - idx[None, :]) + 1e-09
            kernel = time_diffs ** (HURST - 1.5)
            kernel = kernel / jnp.sum(kernel, axis=-1, keepdims=True)
            return jnp.log(kernel + 1e-09)
        key = jax.random.key(seed)
        ks = jax.random.split(key, 4)
        scale = 1.0 / np.sqrt(D)
        return {'x': jax.random.normal(ks[0], (B, S, D), dtype=jnp.float32), 'Wq': jax.random.normal(ks[1], (D, D), dtype=jnp.float32) * scale, 'bq': jnp.zeros((D,), dtype=jnp.float32), 'Wk': jax.random.normal(ks[2], (D, D), dtype=jnp.float32) * scale, 'bk': jnp.zeros((D,), dtype=jnp.float32), 'Wv': jax.random.normal(ks[3], (D, D), dtype=jnp.float32) * scale, 'bv': jnp.zeros((D,), dtype=jnp.float32)}
    _L2_attn_all = _L2_attn_setup()
    _L2_attn_in = {k: v for k, v in _L2_attn_all.items() if k in ('Wq', 'bq', 'Wk', 'bk', 'Wv', 'bv')}
    del _L2_attn_all

    def _L2_ffn_setup():
        import jax, jax.numpy as jnp
        import numpy as np
        B, T, D, H, E = (16, 2048, 128, 256, 8)
        key = jax.random.key(seed)
        ks = jax.random.split(key, 5)
        x = jax.random.normal(ks[0], (B, T, D), dtype=jnp.float32)
        gate_w = jax.random.normal(ks[1], (D, E), dtype=jnp.float32) * 0.02
        gate_b = jnp.zeros((E,), dtype=jnp.float32)
        W1 = jax.random.normal(ks[2], (E, D, H), dtype=jnp.float32) * 0.02
        b1 = jnp.zeros((E, H), dtype=jnp.float32)
        W2 = jax.random.normal(ks[3], (E, H, D), dtype=jnp.float32) * 0.02
        b2 = jnp.zeros((E, D), dtype=jnp.float32)
        return {'x': x, 'gate_w': gate_w, 'gate_b': gate_b, 'W1': W1, 'b1': b1, 'W2': W2, 'b2': b2}
    _L2_ffn_all = _L2_ffn_setup()
    _L2_ffn_in = {k: v for k, v in _L2_ffn_all.items() if k in ('gate_w', 'gate_b', 'W1', 'b1', 'W2', 'b2')}
    del _L2_ffn_all

    def _L3_attn_setup():
        import jax, jax.numpy as jnp
        import numpy as np
        MIDC = 128
        HEADS = 16
        HEADC = MIDC // HEADS
        EPS = 1e-05

        def _layernorm(x, w, b):
            mean = jnp.mean(x, axis=-1, keepdims=True)
            std = jnp.std(x, axis=-1, keepdims=True, ddof=1)
            return w * (x - mean) / (std + EPS) + b
        key = jax.random.key(seed)
        ks = jax.random.split(key, 3)
        B, HW = (8, 8192)
        x = jax.random.normal(ks[0], (B, HW, MIDC), dtype=jnp.float32)
        W_qkv = jax.random.normal(ks[1], (3 * MIDC, MIDC), dtype=jnp.float32) * 0.02
        b_qkv = jnp.zeros((3 * MIDC,), dtype=jnp.float32)
        kln_w = jnp.ones((HEADS, 1, HEADC), dtype=jnp.float32)
        kln_b = jnp.zeros((HEADS, 1, HEADC), dtype=jnp.float32)
        vln_w = jnp.ones((HEADS, 1, HEADC), dtype=jnp.float32)
        vln_b = jnp.zeros((HEADS, 1, HEADC), dtype=jnp.float32)
        W_proj = jax.random.normal(ks[2], (MIDC, MIDC), dtype=jnp.float32) * 0.02
        b_proj = jnp.zeros((MIDC,), dtype=jnp.float32)
        return {'x': x, 'W_qkv': W_qkv, 'b_qkv': b_qkv, 'kln_w': kln_w, 'kln_b': kln_b, 'vln_w': vln_w, 'vln_b': vln_b, 'W_proj': W_proj, 'b_proj': b_proj}
    _L3_attn_all = _L3_attn_setup()
    _L3_attn_in = {k: v for k, v in _L3_attn_all.items() if k in ('W_qkv', 'b_qkv', 'kln_w', 'kln_b', 'vln_w', 'vln_b', 'W_proj', 'b_proj')}
    del _L3_attn_all

    def _L3_ffn_setup():
        import jax, jax.numpy as jnp
        import numpy as np
        B, T, D, H, E = (16, 2048, 128, 256, 8)
        key = jax.random.key(seed)
        ks = jax.random.split(key, 5)
        x = jax.random.normal(ks[0], (B, T, D), dtype=jnp.float32)
        gate_w = jax.random.normal(ks[1], (D, E), dtype=jnp.float32) * 0.02
        gate_b = jnp.zeros((E,), dtype=jnp.float32)
        W1 = jax.random.normal(ks[2], (E, D, H), dtype=jnp.float32) * 0.02
        b1 = jnp.zeros((E, H), dtype=jnp.float32)
        W2 = jax.random.normal(ks[3], (E, H, D), dtype=jnp.float32) * 0.02
        b2 = jnp.zeros((E, D), dtype=jnp.float32)
        return {'x': x, 'gate_w': gate_w, 'gate_b': gate_b, 'W1': W1, 'b1': b1, 'W2': W2, 'b2': b2}
    _L3_ffn_all = _L3_ffn_setup()
    _L3_ffn_in = {k: v for k, v in _L3_ffn_all.items() if k in ('gate_w', 'gate_b', 'W1', 'b1', 'W2', 'b2')}
    del _L3_ffn_all
    return {'x': x, 'L0_conv_offset_w': _L0_conv_in['offset_w'], 'L0_conv_offset_b': _L0_conv_in['offset_b'], 'L0_conv_weight': _L0_conv_in['weight'], 'L0_conv_bias': _L0_conv_in['bias'], 'L1_conv_Wq': _L1_conv_in['Wq'], 'L1_conv_bq': _L1_conv_in['bq'], 'L1_conv_Wk': _L1_conv_in['Wk'], 'L1_conv_bk': _L1_conv_in['bk'], 'L1_conv_Wv': _L1_conv_in['Wv'], 'L1_conv_bv': _L1_conv_in['bv'], 'L1_conv_Wo': _L1_conv_in['Wo'], 'L1_conv_bo': _L1_conv_in['bo'], 'L2_attn_Wq': _L2_attn_in['Wq'], 'L2_attn_bq': _L2_attn_in['bq'], 'L2_attn_Wk': _L2_attn_in['Wk'], 'L2_attn_bk': _L2_attn_in['bk'], 'L2_attn_Wv': _L2_attn_in['Wv'], 'L2_attn_bv': _L2_attn_in['bv'], 'L2_ffn_gate_w': _L2_ffn_in['gate_w'], 'L2_ffn_gate_b': _L2_ffn_in['gate_b'], 'L2_ffn_W1': _L2_ffn_in['W1'], 'L2_ffn_b1': _L2_ffn_in['b1'], 'L2_ffn_W2': _L2_ffn_in['W2'], 'L2_ffn_b2': _L2_ffn_in['b2'], 'L3_attn_W_qkv': _L3_attn_in['W_qkv'], 'L3_attn_b_qkv': _L3_attn_in['b_qkv'], 'L3_attn_kln_w': _L3_attn_in['kln_w'], 'L3_attn_kln_b': _L3_attn_in['kln_b'], 'L3_attn_vln_w': _L3_attn_in['vln_w'], 'L3_attn_vln_b': _L3_attn_in['vln_b'], 'L3_attn_W_proj': _L3_attn_in['W_proj'], 'L3_attn_b_proj': _L3_attn_in['b_proj'], 'L3_ffn_gate_w': _L3_ffn_in['gate_w'], 'L3_ffn_gate_b': _L3_ffn_in['gate_b'], 'L3_ffn_W1': _L3_ffn_in['W1'], 'L3_ffn_b1': _L3_ffn_in['b1'], 'L3_ffn_W2': _L3_ffn_in['W2'], 'L3_ffn_b2': _L3_ffn_in['b2']}

def reference(x, L0_conv_offset_w, L0_conv_offset_b, L0_conv_weight, L0_conv_bias, L1_conv_Wq, L1_conv_bq, L1_conv_Wk, L1_conv_bk, L1_conv_Wv, L1_conv_bv, L1_conv_Wo, L1_conv_bo, L2_attn_Wq, L2_attn_bq, L2_attn_Wk, L2_attn_bk, L2_attn_Wv, L2_attn_bv, L2_ffn_gate_w, L2_ffn_gate_b, L2_ffn_W1, L2_ffn_b1, L2_ffn_W2, L2_ffn_b2, L3_attn_W_qkv, L3_attn_b_qkv, L3_attn_kln_w, L3_attn_kln_b, L3_attn_vln_w, L3_attn_vln_b, L3_attn_W_proj, L3_attn_b_proj, L3_ffn_gate_w, L3_ffn_gate_b, L3_ffn_W1, L3_ffn_b1, L3_ffn_W2, L3_ffn_b2):
    import jax
    import jax.numpy as jnp

    def _L0_conv_ref(x, offset_w, offset_b, weight, bias):
        import jax, jax.numpy as jnp
        import numpy as np
        from jax import lax
        K = 3
        STRIDE = 1
        PAD = 1
        DIL = 1

        def _bilinear_gather(x, py, px):
            B, C, H, W = x.shape
            y0 = jnp.floor(py)
            x0 = jnp.floor(px)
            ly = py - y0
            lx = px - x0
            xf = x.reshape(B, C, H * W)

            def corner(yi, xi, wgt):
                valid = (yi >= 0) & (yi < H) & (xi >= 0) & (xi < W)
                yc = jnp.clip(yi, 0, H - 1).astype(jnp.int32)
                xc = jnp.clip(xi, 0, W - 1).astype(jnp.int32)
                idx = (yc * W + xc).reshape(B, 1, -1)
                v = jnp.take_along_axis(xf, idx, axis=2)
                return v * (wgt * valid.astype(x.dtype)).reshape(B, 1, -1)
            acc = corner(y0, x0, (1 - ly) * (1 - lx)) + corner(y0, x0 + 1, (1 - ly) * lx) + corner(y0 + 1, x0, ly * (1 - lx)) + corner(y0 + 1, x0 + 1, ly * lx)
            return acc.reshape(B, C, py.shape[1], py.shape[2], py.shape[3])

        def deform_conv2d(x, offset_w, offset_b, weight, bias):
            B, C, H, W = x.shape
            off = lax.conv_general_dilated(x, offset_w, window_strides=(STRIDE, STRIDE), padding=[(PAD, PAD), (PAD, PAD)], rhs_dilation=(DIL, DIL))
            off = off + offset_b[None, :, None, None]
            Ho, Wo = (off.shape[2], off.shape[3])
            off = off.reshape(B, K * K, 2, Ho, Wo)
            dy = off[:, :, 0].transpose(0, 2, 3, 1)
            dx = off[:, :, 1].transpose(0, 2, 3, 1)
            ki, kj = jnp.meshgrid(jnp.arange(K), jnp.arange(K), indexing='ij')
            base_y = (jnp.arange(Ho) * STRIDE - PAD)[:, None, None] + (ki.reshape(-1) * DIL)[None, None, :]
            base_x = (jnp.arange(Wo) * STRIDE - PAD)[None, :, None] + (kj.reshape(-1) * DIL)[None, None, :]
            py = base_y[None].astype(x.dtype) + dy
            px = base_x[None].astype(x.dtype) + dx
            sampled = _bilinear_gather(x, py, px)
            Oc = weight.shape[0]
            out = jnp.einsum('bchwk,ock->bohw', sampled, weight.reshape(Oc, C, K * K))
            return out + bias[None, :, None, None]
        return deform_conv2d(x, offset_w, offset_b, weight, bias)

    def _L1_conv_ref(x, Wq, bq, Wk, bk, Wv, bv, Wo, bo):
        import jax, jax.numpy as jnp
        import numpy as np
        B, C, H, W = (4, 128, 32, 32)
        C8 = C // 8
        b, c, h, w = x.shape
        n = h * w
        xf = x.reshape(b, c, n)
        q = jnp.einsum('bcn,dc->bnd', xf, Wq) + bq
        k = jnp.einsum('bcn,dc->bdn', xf, Wk) + bk[:, None]
        v = jnp.einsum('bcn,dc->bdn', xf, Wv) + bv[:, None]
        energy = jnp.einsum('bnd,bdm->bnm', q, k)
        attn = jax.nn.softmax(energy, axis=-1)
        out = jnp.einsum('bcj,bij->bci', v, attn)
        out = out.reshape(b, c, h, w) + x
        out = jnp.einsum('bchw,dc->bdhw', out, Wo) + bo[None, :, None, None]
        return out

    def _L2_attn_ref(x, Wq, bq, Wk, bk, Wv, bv):
        import jax, jax.numpy as jnp
        import numpy as np
        B, S, D = (4, 2048, 128)
        HURST = 0.1

        def _fractional_log_bias(seq_len):
            idx = jnp.arange(seq_len, dtype=jnp.float32)
            time_diffs = jnp.abs(idx[:, None] - idx[None, :]) + 1e-09
            kernel = time_diffs ** (HURST - 1.5)
            kernel = kernel / jnp.sum(kernel, axis=-1, keepdims=True)
            return jnp.log(kernel + 1e-09)
        d = x.shape[-1]
        q = jnp.einsum('bsd,ed->bse', x, Wq) + bq
        k = jnp.einsum('bsd,ed->bse', x, Wk) + bk
        v = jnp.einsum('bsd,ed->bse', x, Wv) + bv
        scores = jnp.einsum('bqd,bkd->bqk', q, k) / np.sqrt(d).astype(np.float32)
        log_bias = _fractional_log_bias(x.shape[1])
        attn = jax.nn.softmax(scores + log_bias, axis=-1)
        return jnp.einsum('bqk,bkd->bqd', attn, v)

    def _L2_ffn_ref(x, gate_w, gate_b, W1, b1, W2, b2):
        import jax, jax.numpy as jnp
        import numpy as np
        B, T, D, H, E = (16, 2048, 128, 256, 8)
        Bb, Tt, Dd = x.shape
        Ee = gate_w.shape[1]
        xf = x.reshape(-1, Dd)
        N = xf.shape[0]
        logits = xf @ gate_w + gate_b
        probs = jax.nn.softmax(logits, axis=-1)
        top2_vals, top2_idx = jax.lax.top_k(probs, 2)
        cw = jnp.zeros((N, Ee), dtype=xf.dtype).at[jnp.arange(N)[:, None], top2_idx].add(top2_vals)

        def step(acc, params):
            w1, bb1, w2, bb2, we = params
            h = jax.nn.gelu(xf @ w1 + bb1, approximate=False)
            y = h @ w2 + bb2
            return (acc + we[:, None] * y, None)
        out, _ = jax.lax.scan(step, jnp.zeros_like(xf), (W1, b1, W2, b2, cw.T))
        return out.reshape(Bb, Tt, Dd)

    def _L3_attn_ref(x, W_qkv, b_qkv, kln_w, kln_b, vln_w, vln_b, W_proj, b_proj):
        import jax, jax.numpy as jnp
        import numpy as np
        MIDC = 128
        HEADS = 16
        HEADC = MIDC // HEADS
        EPS = 1e-05

        def _layernorm(x, w, b):
            mean = jnp.mean(x, axis=-1, keepdims=True)
            std = jnp.std(x, axis=-1, keepdims=True, ddof=1)
            return w * (x - mean) / (std + EPS) + b
        B, HW, C = x.shape
        bias = x
        qkv = jnp.einsum('bnc,oc->bno', x, W_qkv) + b_qkv
        qkv = qkv.reshape(B, HW, HEADS, 3 * HEADC).transpose(0, 2, 1, 3)
        q, k, v = jnp.split(qkv, 3, axis=-1)
        k = _layernorm(k, kln_w, kln_b)
        v = _layernorm(v, vln_w, vln_b)
        kv = jnp.einsum('bhnd,bhne->bhde', k, v) / HW
        out = jnp.einsum('bhnd,bhde->bhne', q, kv)
        out = out.transpose(0, 2, 1, 3).reshape(B, HW, C)
        ret = out + bias
        proj = jnp.einsum('bnc,oc->bno', ret, W_proj) + b_proj
        return jax.nn.gelu(proj, approximate=False) + bias

    def _L3_ffn_ref(x, gate_w, gate_b, W1, b1, W2, b2):
        import jax, jax.numpy as jnp
        import numpy as np
        B, T, D, H, E = (16, 2048, 128, 256, 8)
        Bb, Tt, Dd = x.shape
        Ee = gate_w.shape[1]
        xf = x.reshape(-1, Dd)
        N = xf.shape[0]
        logits = xf @ gate_w + gate_b
        probs = jax.nn.softmax(logits, axis=-1)
        top2_vals, top2_idx = jax.lax.top_k(probs, 2)
        cw = jnp.zeros((N, Ee), dtype=xf.dtype).at[jnp.arange(N)[:, None], top2_idx].add(top2_vals)

        def step(acc, params):
            w1, bb1, w2, bb2, we = params
            h = jax.nn.gelu(xf @ w1 + bb1, approximate=False)
            y = h @ w2 + bb2
            return (acc + we[:, None] * y, None)
        out, _ = jax.lax.scan(step, jnp.zeros_like(xf), (W1, b1, W2, b2, cw.T))
        return out.reshape(Bb, Tt, Dd)

    def _gn(v, G=32, eps=1e-05):
        B_, C_, H_, W_ = v.shape
        g = v.reshape(B_, G, C_ // G, H_, W_)
        m = jnp.mean(g, axis=(2, 3, 4), keepdims=True)
        s = jnp.var(g, axis=(2, 3, 4), keepdims=True)
        return ((g - m) / jnp.sqrt(s + eps)).reshape(v.shape)

    def _ln_c(v, eps=1e-06):
        m = jnp.mean(v, axis=1, keepdims=True)
        s = jnp.var(v, axis=1, keepdims=True)
        return (v - m) / jnp.sqrt(s + eps)

    def _ln_t(v, eps=1e-05):
        m = jnp.mean(v, axis=-1, keepdims=True)
        s = jnp.var(v, axis=-1, keepdims=True)
        return (v - m) / jnp.sqrt(s + eps)

    def _to_tokens(v):
        B_, C_, H_, W_ = v.shape
        return v.reshape(B_, C_, H_ * W_).transpose(0, 2, 1)

    def _from_tokens(t, like):
        B_, C_, H_, W_ = like.shape
        return t.transpose(0, 2, 1).reshape(B_, C_, H_, W_)
    x = x + _L0_conv_ref(_gn(x), L0_conv_offset_w, L0_conv_offset_b, L0_conv_weight, L0_conv_bias)
    x = x + _L1_conv_ref(_gn(x), L1_conv_Wq, L1_conv_bq, L1_conv_Wk, L1_conv_bk, L1_conv_Wv, L1_conv_bv, L1_conv_Wo, L1_conv_bo)
    t = _to_tokens(x)
    t = t + _L2_attn_ref(_ln_t(t), L2_attn_Wq, L2_attn_bq, L2_attn_Wk, L2_attn_bk, L2_attn_Wv, L2_attn_bv)
    t = t + _L2_ffn_ref(_ln_t(t), L2_ffn_gate_w, L2_ffn_gate_b, L2_ffn_W1, L2_ffn_b1, L2_ffn_W2, L2_ffn_b2)
    t = t + _L3_attn_ref(_ln_t(t), L3_attn_W_qkv, L3_attn_b_qkv, L3_attn_kln_w, L3_attn_kln_b, L3_attn_vln_w, L3_attn_vln_b, L3_attn_W_proj, L3_attn_b_proj)
    t = t + _L3_ffn_ref(_ln_t(t), L3_ffn_gate_w, L3_ffn_gate_b, L3_ffn_W1, L3_ffn_b1, L3_ffn_W2, L3_ffn_b2)
    x = _from_tokens(t, x)
    return x

_drawn_inputs = setup_inputs


def setup_inputs(seed=0):
    import zlib

    import numpy as np

    out = dict(_drawn_inputs(seed))
    spreads = {'L0_conv_offset_b': (0.0, 0.1),
     'L0_conv_bias': (0.0, 0.1),
     'L2_attn_bq': (0.0, 0.8),
     'L2_attn_bk': (0.0, 0.8),
     'L2_attn_bv': (0.0, 0.1),
     'L2_ffn_gate_b': (0.0, 0.799),
     'L2_ffn_b1': (0.0, 0.8),
     'L2_ffn_b2': (0.0, 0.617),
     'L3_attn_b_qkv': (0.0, 0.8),
     'L3_attn_kln_w': (1.0, 0.6),
     'L3_attn_kln_b': (0.0, 0.8),
     'L3_attn_vln_w': (1.0, 0.6),
     'L3_attn_vln_b': (0.0, 0.8),
     'L3_attn_b_proj': (0.0, 0.412),
     'L3_ffn_gate_b': (0.0, 0.8),
     'L3_ffn_b1': (0.0, 0.8),
     'L3_ffn_b2': (0.0, 0.8)}
    factors = {'L1_conv_bq': 8.0,
     'L1_conv_bk': 8.0,
     'L1_conv_bv': 7.91,
     'L1_conv_bo': 8.0,
     'L2_attn_Wq': 8.0,
     'L2_attn_Wk': 8.0,
     'L2_ffn_gate_w': 5.263,
     'L2_ffn_W1': 8.0,
     'L2_ffn_W2': 8.0,
     'L3_attn_W_qkv': 8.0,
     'L3_ffn_gate_w': 7.886,
     'L3_ffn_W1': 8.0,
     'L3_ffn_W2': 8.0}
    for name, (base, spread) in spreads.items():
        noise = np.random.default_rng([zlib.crc32(name.encode()), seed]).standard_normal(out[name].shape)
        drawn = base * np.exp(spread * noise) if base else spread * noise
        out[name] = jnp.asarray(drawn.astype(out[name].dtype))
    for name, factor in factors.items():
        out[name] = (out[name] * factor).astype(out[name].dtype)
    return out
```

```python
from contextlib import ExitStack

import concourse.bass as bass
from concourse import mybir

F32 = mybir.dt.float32
BF16 = mybir.dt.bfloat16
ALU = mybir.AluOpType
ACT = mybir.ActivationFunctionType
AX = mybir.AxisListType

P = 128
B = 8
HW = 32
N = HW * HW
NT = N // P
C = 128
TAPS = 9
NOFF = 2 * TAPS
D1 = C // 8
E = 8
HID = 256
HC = HID // P
HEADC = 8
SLOTS = 2
ROWS = P // HW
GN_EPS, LN_EPS, HEAD_EPS = 1e-5, 1e-5, 1e-5
TOEP = N + (NT - 1) * P
LIMIT = 384


def near_pieces():
    return [(c, max(0, P * (c - 1)), min(N, P * (c + 2))) for c in range(NT)]


def far_pieces():
    out = []
    for c, lo, hi in near_pieces():
        for a, b in ((0, lo), (hi, N)):
            while a < b:
                out.append((c, a, min(b, a + LIMIT)))
                a += LIMIT
    return out


PASSES = [near_pieces(), far_pieces()]
PIECES = TAPS * sum(len(p) for p in PASSES)
RING = 4


def layout():
    early = dict(ident=(P, P), grp=(P, P), kvmask=(P, P), base=(NOFF, N), yneg=(P, NT), xneg=(P, 1),
                 offw=(C, TAPS * NOFF), offb=(NOFF, 1), w0=(C, TAPS * C), b0=(C, 1),
                 wq1=(C, D1), wk1=(C, D1), bq1=(D1, 1), bk1=(D1, 1), wv1=(C, C), bv1=(P, C), wo1=(C, C), bo1=(P, C))
    late = dict(wq2=(C, C), wk2=(C, C), bq2=(C, 1), bk2=(C, 1), wv2=(C, C), bv2=(P, C), toep=(P, TOEP),
                low=(P, E * E),
                wq3=(C, C), bq3=(C, 1), wkv3=(C, 2 * C), bkv3=(P, 2 * C), lnw3=(P, 2 * C), lnb3=(P, 2 * C),
                wp3=(C, C), bp3=(P, C))
    for f in "ab":
        late.update({"gw" + f: (C, E), "gb" + f: (P, E), "w1" + f: (C, E * HID), "b1" + f: (P, E * HC),
                     "w2" + f: (P, E * HC * C), "b2" + f: (NT * E, NT * C)})
    return early, late


def columns(part):
    at, out = 0, {}
    for name, (p, n) in part.items():
        out[name] = (at, p, n)
        at += n
    return out, at


def build(nc, x, sel_in, early_in, late_in, out):
    early, late = layout()
    ecols, en = columns(early)
    lcols, ln = columns(late)
    with ExitStack() as ctx:
        def sb(name, shape, dt=F32):
            return ctx.enter_context(nc.sbuf_tensor(name, shape, dt))

        sems = {}

        def sem(name):
            if name not in sems:
                sems[name] = ctx.enter_context(nc.semaphore(name))
            return sems[name]

        early_sb, late_sb = sb("early_sb", [P, en]), sb("late_sb", [P, ln])

        def const(name):
            tile, cols = (early_sb, ecols) if name in ecols else (late_sb, lcols)
            at, p, n = cols[name]
            return tile[0:p, at:at + n]

        ident, grp = const("ident"), const("grp")
        sel = sb("sel_sb", [96, NOFF * P], BF16)
        xc = [sb(f"xc{s}", [P, N]) for s in range(SLOTS)]
        xn = [sb(f"xn{s}", [P, N]) for s in range(SLOTS)]
        xpad = sb("xpad", [P, HW + 2, HW + 2])
        tok = [sb(f"tok{s}", [P, NT, C]) for s in range(SLOTS)]
        tn = [sb(f"tn{s}", [P, NT, C]) for s in range(SLOTS)]
        tnT = [sb(f"tnT{s}", [P, N]) for s in range(SLOTS)]
        qT = [sb(f"qT{s}", [P, N]) for s in range(SLOTS)]
        kT = [sb(f"kT{s}", [P, N]) for s in range(SLOTS)]
        vt = [sb(f"vt{s}", [P, NT, C]) for s in range(SLOTS)]
        hx = [vt[s][:].rearrange("p a b -> p (a b)") for s in range(SLOTS)]
        offs = sb("offs", [96, N], BF16)
        offcut = [tnT[n][0:NOFF, 0:N // 2].bitcast(BF16) for n in range(2)]
        big = sb("big", [P, NT * TAPS * C])
        z = big[:, :].rearrange("p (c k o) -> p c k o", c=NT, k=TAPS)
        kv = [big[:, 2 * N * s:2 * N * (s + 1)] for s in range(SLOTS)]
        hid = [big[:, (4 + r) * N:(5 + r) * N] for r in range(4)]
        prob = sb("prob", [P, 2 * N])
        pr = [prob[:, r * N:(r + 1) * N] for r in range(2)]
        pos, rest = prob[0:NOFF, 0:N], prob[0:NOFF, N:2 * N]
        dist = sb("dist", [P, 2 * RING * LIMIT])
        ay = [dist[:, r * LIMIT:(r + 1) * LIMIT] for r in range(RING)]
        hat = [dist[:, (RING + r) * LIMIT:(RING + r + 1) * LIMIT] for r in range(RING)]
        prT = [dist[:, r * N:(r + 1) * N].rearrange("p (a b) -> p a b", a=NT) for r in range(2)]
        mhalf = sb("mhalf", [P, NT])
        bst = [sb(f"bst{s}", [P, NT * 6]) for s in range(SLOTS)]
        mv = [sb(f"mv{s}", [P, NT, 2]) for s in range(SLOTS)]
        gst = [sb(f"gst{s}", [P, 4]) for s in range(SLOTS)]
        var = [sb(f"var{s}", [P, NT]) for s in range(SLOTS)]
        rstd = [sb(f"rstd{s}", [P, NT]) for s in range(SLOTS)]
        nmr = [sb(f"nmr{s}", [P, NT]) for s in range(SLOTS)]
        nmax = [sb(f"nmax{s}", [P, NT]) for s in range(SLOTS)]
        rsum = [sb(f"rsum{s}", [P, NT]) for s in range(SLOTS)]
        rinv = [sb(f"rinv{s}", [P, NT]) for s in range(SLOTS)]
        lg = [sb(f"lg{s}", [P, NT, E]) for s in range(SLOTS)]
        gmx = [sb(f"gmx{s}", [P, NT]) for s in range(SLOTS)]
        gsum = [sb(f"gsum{s}", [P, NT]) for s in range(SLOTS)]
        cw = [sb(f"cw{s}", [P, NT, E]) for s in range(SLOTS)]
        cwT = [sb(f"cwT{s}", [NT * E, P]) for s in range(SLOTS)]
        wins, ties = (prob[:, r * NT * E * E:(r + 1) * NT * E * E].rearrange("p (a b c) -> p a b c", a=NT, b=E)
                      for r in range(2))
        bqs = sb("bqs", [P, 1])
        hm = [sb(f"hm{s}", [P, NT * 32]) for s in range(SLOTS)]
        kvm = [sb(f"kvm{s}", [P, P]) for s in range(SLOTS)]
        xo = qT

        pair = [ctx.enter_context(nc.psum_tensor(f"pair{i}", [P, N], F32)) for i in range(4)]
        BANKS = ("0", "1", "2", "3a", "3b")
        p3 = {"3a": pair[3][:, 0:512], "3b": pair[3][:, 512:1024]}

        def released(ins, bank):
            return ins.then_inc(sem("free" + bank), 1)

        def at(i, s, k, c):
            return i * (SLOTS * k) + (s * k + c)

        def at4(i, inst, k, c):
            return i * (4 * k) + (inst * k + c)

        UNITS = E * HC
        block = ctx.enter_context(nc.Block())

        @block.sync
        def _(sp):
            sp.dma_start(early_sb[:, :], early_in).then_inc(sem("early_loaded"), 16)
            sp.dma_start(sel[:, :], sel_in).then_inc(sem("early_loaded"), 16)
            with sp.Fori(0, B // SLOTS) as i:
                for s in range(SLOTS):
                    sp.wait_ge(sem(f"x_used{s}"), i + 1)
                    sp.dma_start(xc[s][:, :], x[i * SLOTS + s].rearrange("c h w -> c (h w)")).then_inc(sem(f"x_loaded{s}"), 16)

        @block.gpsimd
        def _(pool):
            pool.memset(mhalf[:, :], -0.5).then_inc(sem("mhalf_set"), 1)
            pool.memset(xpad[:, :, :], 0.0)
            pool.drain().then_inc(sem("pads_zero"), 1)
            pool.wait_ge(sem("mhalf_set"), 1)

            def rsqrt(i, s, which, width):
                pool.wait_ge(sem(which + "_var"), at(i, s, 1, 1))
                pool.tensor_tensor(rstd[s][:, 0:width], var[s][:, 0:width], mhalf[:, 0:width],
                                   ALU.pow).then_inc(sem(which + "_rstd"), 1)

            with pool.Fori(0, B // SLOTS) as i:
                for which, width in (("gn0", 1), ("gn1", 1), ("ln2", NT), ("lnf2", NT), ("ln3", NT), ("lnf3", NT)):
                    for s in range(SLOTS):
                        rsqrt(i, s, which, width)
                        if which == "ln3":
                            pool.wait_ge(sem("ln3_tn"), at(i, s, 1, 1))
                            pool.tensor_tensor(tok[s][:, :, :], tok[s][:, :, :], tn[s][:, :, :],
                                               ALU.add).then_inc(sem("tok3_res"), 1)

        @block.tensor
        def _(pe):
            uses = dict.fromkeys(BANKS, 0)
            totals = {"0": 60, "1": 92, "2": 108, "3a": 70, "3b": 60}

            def claim(i, bank):
                uses[bank] += 1
                pe.wait_ge(sem("free" + bank), i * totals[bank] + uses[bank])

            def gn(i, s, which):
                for c in range(2):
                    pe.wait_ge(sem(which + "_stat"), at(i, s, 2, c + 1))
                    claim(i, "3a")
                    pe.matmul(p3["3a"][:, 0:1], grp, gst[s][:, c:c + 1], start=True, stop=True)\
                        .then_inc(sem(which + "_group"), 1)

            def l0(i, s):
                pe.wait_ge(sem("xpad_set"), at(i, s, 1, 1))
                claim(i, "2")
                for h in range(2):
                    for k in range(TAPS):
                        ky, kx = divmod(k, 3)
                        last = pe.matmul(pair[2][0:NOFF, h * 512:h * 512 + 512], const("offw")[:, k * NOFF:(k + 1) * NOFF],
                                         xpad[:, ky + 16 * h:ky + 16 * h + 16, kx:kx + HW],
                                         start=(k == 0), stop=(k == TAPS - 1))
                last.then_inc(sem("off_ready"), 1)
                for g in range(3 * NT):
                    c, third = divmod(g, 3)
                    bank = ("3a", "3b")[g % 2]
                    claim(i, bank)
                    pe.matmul(p3[bank][:, 0:384], xn[s][:, c * P:(c + 1) * P],
                              const("w0")[:, third * 384:(third + 1) * 384], start=True, stop=True)\
                        .then_inc(sem("z_ready"), 1)
                pe.wait_ge(sem("offs_split"), at(i, s, 3, 3))

                def spread(k):
                    for bank, r in ((1, 2 * k + 1), (2, 2 * k)):
                        claim(i, str(bank))
                        for h in range(2):
                            last = pe.matmul(pair[bank][:, h * 512:(h + 1) * 512], sel[:, r * P:(r + 1) * P],
                                             offs[:, h * 512:(h + 1) * 512], start=True, stop=True)
                        last.then_inc(sem("spread"), 1)

                order = [(p, k) for p in range(len(PASSES)) for k in range(TAPS)]
                spread(0)
                claim(i, "0")
                pe.wait_ge(sem("z_kept"), at(i, s, 3 * NT, 3 * NT))
                n = 0
                opened = set()
                for m, (p, k) in enumerate(order):
                    for q, (c, lo, hi) in enumerate(PASSES[p]):
                        if q == len(PASSES[p]) - 2 * RING and m + 1 < len(order):
                            spread(order[m + 1][1])
                        pe.wait_ge(sem("hat_ready"), at(i, s, PIECES, n + 1) + RING)
                        for a, b in ((lo, min(hi, 512)), (max(lo, 512), hi)):
                            if a < b:
                                bank = a // 512
                                last = pe.matmul(pair[0][:, a:b], z[:, c, k, :], hat[n % RING][:, a - lo:b - lo],
                                                 start=bank not in opened, stop=m == len(order) - 1,
                                                 skip_group_check=True)
                                opened.add(bank)
                        last.then_inc(sem("hat_used"), 1)
                        n += 1

            def project(i, s, bank, w, src, m, done):
                claim(i, str(bank))
                for h in range(2):
                    last = pe.matmul(pair[bank][0:m, h * 512:(h + 1) * 512], w, src[:, h * 512:(h + 1) * 512],
                                     start=True, stop=True)
                last.then_inc(sem(done), 1)

            def tiles(i, s, bank, src, w, done):
                claim(i, str(bank))
                for j in range(NT):
                    last = pe.matmul(pair[bank][:, j * P:(j + 1) * P], src[:, j * P:(j + 1) * P], w, start=True, stop=True)
                last.then_inc(sem(done), 1)

            def transposes(i, s, bank, src, done):
                claim(i, str(bank))
                for j in range(NT):
                    last = pe.transpose(pair[bank][:, j * P:(j + 1) * P], src[:, j, :], ident)
                last.then_inc(sem(done), 1)

            def core(i, s, inst, rows):
                for j in range(NT + 2):
                    if j < NT:
                        bank = j % 2
                        claim(i, str(bank))
                        for h in range(2):
                            last = pe.matmul(pair[bank][:, h * 512:(h + 1) * 512], qT[s][0:rows, j * P:(j + 1) * P],
                                             kT[s][0:rows, h * 512:(h + 1) * 512], start=True, stop=True)
                        last.then_inc(sem("energy"), 1)
                    if 1 <= j <= NT:
                        jj = j - 1
                        if inst < 2:
                            pe.wait_ge(sem("prob_exp"), at4(i, inst, NT, jj + 1))
                        else:
                            pe.wait_ge(sem("prob_biased"), at(i, s, NT, jj + 1))
                        transposes(i, s, 2, pr[jj % 2].rearrange("p (a b) -> p a b", a=NT), "prob_T")
                    if j >= 2:
                        jj = j - 2
                        bank = ("3a", "3b")[jj % 2]
                        pe.wait_ge(sem("probT_kept"), at4(i, inst, NT, jj + 1))
                        claim(i, bank)
                        for m in range(NT):
                            last = pe.matmul(p3[bank][:, 0:P], prT[jj % 2][:, m, :], vt[s][:, m, :],
                                             start=(m == 0), stop=(m == NT - 1))
                        last.then_inc(sem("pv"), 1)

            def l1(i, s):
                pe.wait_ge(sem("gn1_xn"), at(i, s, 1, 1))
                project(i, s, 0, const("wq1"), xn[s], D1, "proj1")
                project(i, s, 1, const("wk1"), xn[s], D1, "proj1")
                tiles(i, s, 2, xn[s], const("wv1"), "proj1")
                pe.wait_ge(sem("qk1_kept"), at(i, s, 2, 2))
                pe.wait_ge(sem("v1_kept"), at(i, s, 1, 1))
                core(i, s, s, D1)

            def l1_out(i, s):
                pe.wait_ge(sem("o_kept"), at4(i, s, NT, NT))
                transposes(i, s, 2, tn[s], "att1_T")
                pe.wait_ge(sem("y1_kept"), at(i, s, 1, 1))
                claim(i, "0")
                for j in range(NT):
                    pe.matmul(pair[0][:, j * P:(j + 1) * P], xn[s][:, j * P:(j + 1) * P], const("wo1"), start=True, stop=False)
                    last = pe.matmul(pair[0][:, j * P:(j + 1) * P], xc[s][:, j * P:(j + 1) * P], ident, start=False, stop=True)
                last.then_inc(sem("tok1"), 1)

            def ln_T(i, s, which):
                pe.wait_ge(sem(which + "_tn"), at(i, s, 1, 1))
                transposes(i, s, 2, tn[s], which + "_T")
                pe.wait_ge(sem(which + "_tnT"), at(i, s, 1, 1))

            def l2(i, s):
                ln_T(i, s, "ln2")
                project(i, s, 0, const("wq2"), tnT[s], C, "proj2")
                project(i, s, 1, const("wk2"), tnT[s], C, "proj2")
                tiles(i, s, 2, tnT[s], const("wv2"), "proj2")
                pe.wait_ge(sem("qk2_kept"), at(i, s, 2, 2))
                pe.wait_ge(sem("v2_kept"), at(i, s, 1, 1))
                core(i, s, 2 + s, C)

            def ffn(i, s, inst, which, f):
                ln_T(i, s, which)
                claim(i, "3a")
                for j in range(NT):
                    last = pe.matmul(p3["3a"][:, j * E:(j + 1) * E], tnT[s][:, j * P:(j + 1) * P], const("gw" + f),
                                     start=True, stop=True)
                last.then_inc(sem("gate"), 1)

                def hidden(e):
                    for h in range(HC):
                        col = e * HID + h * P
                        project(i, s, (HC * e + h) % 2, const("w1" + f)[:, col:col + P], tnT[s], P, "hidden")

                def pair_claim(q):
                    if q % 2:
                        claim(i, "3a")
                        claim(i, "3b")
                    else:
                        claim(i, "2")
                    return pair[2 + q % 2]

                def back(e, q):
                    pe.wait_ge(sem("gelu"), at4(i, inst, UNITS, HC * (e + 1)))
                    dst = pair_claim(q)
                    for j in range(NT):
                        for h in range(HC):
                            w = (e * HC + h) * C
                            last = pe.matmul(dst[:, j * P:(j + 1) * P], hid[(HC * e + h) % 4][:, j * P:(j + 1) * P],
                                             const("w2" + f)[:, w:w + C], start=(h == 0), stop=(h == HC - 1))
                    last.then_inc(sem("expert"), 1)

                hidden(0)
                hidden(1)
                pe.wait_ge(sem("cw"), at4(i, inst, 1, 1))
                claim(i, "3b")
                pe.matmul(p3["3b"][0:NT * E, 0:P], cw[s][:, :, :].rearrange("p a b -> p (a b)"), ident, start=True, stop=True)\
                    .then_inc(sem("cw_T"), 1)
                back(0, 0)
                hidden(2)
                pe.wait_ge(sem("cwT_kept"), at4(i, inst, 1, 1))
                dst = pair_claim(1)
                for j in range(NT):
                    last = pe.matmul(dst[:, j * P:(j + 1) * P], cwT[s][:, :], const("b2" + f)[:, j * C:(j + 1) * C],
                                     start=True, stop=True)
                last.then_inc(sem("bias2"), 1)
                for e in range(1, E):
                    back(e, e + 1)
                    if e + 2 < E:
                        hidden(e + 2)

            def l3(i, s):
                ln_T(i, s, "ln3")
                project(i, s, 0, const("wq3"), tnT[s], C, "q3")
                for g in range(2):
                    claim(i, str(1 + g))
                    for j in range(4):
                        t0 = (4 * g + j) * P
                        last = pe.matmul(pair[1 + g][:, j * 256:(j + 1) * 256], tnT[s][:, t0:t0 + P], const("wkv3"),
                                         start=True, stop=True)
                    last.then_inc(sem("kv3"), 1)

            def l3_out(i, s):
                kvs = kv[s].rearrange("p (a b) -> p a b", a=NT)
                pe.wait_ge(sem("kv3_normed"), at(i, s, 1, 1))
                claim(i, "3a")
                for j in range(NT):
                    last = pe.matmul(p3["3a"][:, 0:P], kvs[:, j, 0:C], kvs[:, j, C:2 * C], start=(j == 0), stop=(j == NT - 1))
                last.then_inc(sem("state3"), 1)
                pe.wait_ge(sem("state3_kept"), at(i, s, 1, 1))
                pe.wait_ge(sem("q3_kept"), at(i, s, 1, 1))
                project(i, s, 0, kvm[s][:, :], qT[s], P, "read3")
                pe.wait_ge(sem("ret3_kept"), at(i, s, 1, 1))
                tiles(i, s, 1, kT[s], const("wp3"), "proj3")

            def finish(i, s):
                pe.wait_ge(sem("tok_final"), at(i, s, 1, 1))
                transposes(i, s, 2, tok[s], "final_T")

            pe.wait_ge(sem("early_loaded"), 32)
            with pe.Fori(0, B // SLOTS) as i:
                for s in range(SLOTS):
                    gn(i, s, "gn0")
                for s in range(SLOTS):
                    l0(i, s)
                for s in range(SLOTS):
                    gn(i, s, "gn1")
                for s in range(SLOTS):
                    l1(i, s)
                for s in range(SLOTS):
                    l1_out(i, s)
                pe.wait_ge(sem("late_loaded"), 16)
                for s in range(SLOTS):
                    l2(i, s)
                for s in range(SLOTS):
                    ffn(i, s, s, "lnf2", "a")
                for s in range(SLOTS):
                    l3(i, s)
                for s in range(SLOTS):
                    l3_out(i, s)
                for s in range(SLOTS):
                    ffn(i, s, 2 + s, "lnf3", "b")
                for s in range(SLOTS):
                    finish(i, s)
            assert uses == totals, uses

        @block.scalar
        def _(act):
            def copy_out(i, s, bank, dst, ready, value, done, **kw):
                act.wait_ge(sem(ready), value)
                src = pair[bank][0:dst.shape[0], :]
                released(act.activation(dst, src, ACT.Identity if kw else ACT.Copy, **kw), str(bank))
                return act.drain().then_inc(sem(done), 1)

            def l0(i, s):
                act.wait_ge(sem("gn0_xn"), at(i, s, 1, 1))
                act.activation(xpad[:, 1:HW + 1, 1:HW + 1], xn[s][:, :].rearrange("p (a b) -> p a b", a=HW),
                               ACT.Copy).then_inc(sem("xpad_set"), 1)
                for g in range(0, 3 * NT, 2):
                    c, third = divmod(g, 3)
                    act.wait_ge(sem("z_ready"), at(i, s, 3 * NT, g + 1))
                    released(act.activation(z[:, c, 3 * third:3 * third + 3, :],
                                            p3["3a"][:, 0:384].rearrange("p (a b) -> p a b", a=3), ACT.Copy), "3a")
                act.drain().then_inc(sem("z_kept"), 3 * NT // 2)
                for part in (1, 2):
                    act.wait_ge(sem("offs_cut"), at(i, s, 2, part))
                    src = offcut[part - 1]
                    act.activation(offs[32 * part:32 * part + NOFF, :], src, ACT.Copy).then_inc(sem("offs_split"), 1)
                n = 0
                m = 0
                for p in range(len(PASSES)):
                    for k in range(TAPS):
                        act.wait_ge(sem("spread"), at(i, s, 4 * TAPS, 2 * m + 1))
                        released(act.activation(hx[m % 2], pair[1][:, :], ACT.Abs, bias=const("xneg")), "1")
                        act.wait_ge(sem("spread"), at(i, s, 4 * TAPS, 2 * m + 2))
                        for c, lo, hi in PASSES[p]:
                            act.wait_ge(sem("hat_ready"), at(i, s, PIECES, n + 1))
                            act.activation(ay[n % RING][:, 0:hi - lo], pair[2][:, lo:hi], ACT.Abs,
                                           bias=const("yneg")[:, c:c + 1]).then_inc(sem("ay_ready"), 1)
                            n += 1
                        act.drain().then_inc(sem("free2"), 1)
                        m += 1

            def core(i, s, inst):
                for j in range(NT + 1):
                    if j < NT:
                        act.wait_ge(sem("nmax"), at4(i, inst, NT, j + 1))
                        act.activation(pr[j % 2], pair[j % 2][:, :], ACT.Exp, bias=nmax[s][:, j:j + 1],
                                       accum_out=rsum[s][:, j:j + 1]).then_inc(sem(f"free{j % 2}"), 1)
                        act.drain().then_inc(sem("prob_exp"), 1)
                    if j >= 1:
                        jj = j - 1
                        act.wait_ge(sem("prob_T"), at4(i, inst, NT, jj + 1))
                        act.wait_ge(sem("pv"), at4(i, inst, NT, jj + 1))
                        released(act.activation(prT[jj % 2].rearrange("p a b -> p (a b)"), pair[2][:, :], ACT.Copy), "2")
                        act.drain().then_inc(sem("probT_kept"), 1)

            def l1(i, s):
                for n, (dst, bias) in enumerate(((qT, "bq1"), (kT, "bk1"))):
                    copy_out(i, s, n, dst[s][0:D1, :], "proj1", at(i, s, 3, n + 1), "qk1_kept", bias=const(bias))
                core(i, s, s)

            def ln_T(i, s, which):
                copy_out(i, s, 2, tnT[s][:, :], which + "_T", at(i, s, 1, 1), which + "_tnT")

            def l2(i, s):
                ln_T(i, s, "ln2")
                copy_out(i, s, 0, qT[s][:, :], "proj2", at(i, s, 3, 1), "qk2_kept", bias=bqs[:, 0:1], scale=float(C) ** -0.5)
                copy_out(i, s, 1, kT[s][:, :], "proj2", at(i, s, 3, 2), "qk2_kept", bias=const("bk2"))
                core(i, s, 2 + s)

            def ffn(i, s, inst, which, f):
                ln_T(i, s, which)

                def gelu(u):
                    if u % HC == 0:
                        act.wait_ge(sem("expert"), at4(i, inst, E, u // HC + 1))
                    act.wait_ge(sem("hidden"), at4(i, inst, UNITS, u + 1))
                    act.activation(hid[u % 4], pair[u % 2][:, :], ACT.Gelu, bias=const("b1" + f)[:, u:u + 1])\
                        .then_inc(sem(f"free{u % 2}"), 1)
                    act.drain().then_inc(sem("gelu"), 1)

                for u in range(4):
                    gelu(u)
                act.wait_ge(sem("logits"), at4(i, inst, 1, 1))
                act.activation(lg[s][:, :, :], lg[s][:, :, :], ACT.Exp).then_inc(sem("gate_exp"), 1)
                for u in range(4, UNITS):
                    gelu(u)

            def l3(i, s):
                ln_T(i, s, "ln3")
                copy_out(i, s, 0, qT[s][:, :], "q3", at(i, s, 1, 1), "q3_kept", bias=const("bq3"))

            def l3_norm(i, s):
                act.wait_ge(sem("kv3_centred"), at(i, s, 1, 1))
                act.activation(prob[:, :], kv[s], ACT.Square).then_inc(sem("kv3_squared"), 1)
                act.wait_ge(sem("kv3_sumsq"), at(i, s, 1, 1))
                act.activation(hm[s][:, :], hm[s][:, :], ACT.Sqrt, scale=1.0 / (HEADC - 1)).then_inc(sem("kv3_std"), 1)

            def l3_gelu(i, s):
                act.wait_ge(sem("p3_biased"), at(i, s, 1, 1))
                act.activation(tn[s][:, :, :], tn[s][:, :, :], ACT.Gelu).then_inc(sem("p3_gelu"), 1)

            def finish(i, s):
                act.wait_ge(sem("final_T"), at(i, s, 1, 1))
                released(act.activation(xo[s][:, :], pair[2][:, :], ACT.Copy), "2")
                act.drain().then_inc(sem("xo_ready"), 1)
                act.wait_ge(sem("xo_ready"), at(i, s, 1, 1))
                act.dma_start(out[i * SLOTS + s].rearrange("c h w -> c (h w)"), xo[s][:, :]).then_inc(sem(f"stored{s}"), 16)

            act.dma_start(late_sb[:, :], late_in).then_inc(sem("late_loaded"), 16)
            act.wait_ge(sem("early_loaded"), 32)
            act.wait_ge(sem("pads_zero"), 1)
            act.wait_ge(sem("seeded"), 1)
            with act.Fori(0, B // SLOTS) as i:
                for s in range(SLOTS):
                    l0(i, s)
                for s in range(SLOTS):
                    l1(i, s)
                act.wait_ge(sem("late_loaded"), 16)
                act.mul(bqs[:, :], const("bq2"), float(C) ** -0.5)
                act.drain()
                for s in range(SLOTS):
                    l2(i, s)
                for s in range(SLOTS):
                    ffn(i, s, s, "lnf2", "a")
                for s in range(SLOTS):
                    l3(i, s)
                for s in range(SLOTS):
                    l3_norm(i, s)
                for s in range(SLOTS):
                    l3_gelu(i, s)
                for s in range(SLOTS):
                    ffn(i, s, 2 + s, "lnf3", "b")
                for s in range(SLOTS):
                    finish(i, s)
                for s in range(SLOTS):
                    act.wait_ge(sem(f"stored{s}"), 16 * i + 16)

        @block.vector
        def _(dve):
            def over_tiles(row, n=NT):
                return row.rearrange("p (a b) -> p a b", a=1).to_broadcast([row.shape[0], n, row.shape[1]])

            def inner(col, n):
                return col.rearrange("p (a b) -> p a b", b=1).to_broadcast([P, col.shape[1], n])

            def gn(i, s, which):
                for h in range(2):
                    dve.bn_stats(bst[s][:, 6 * h:6 * h + 6], xc[s][:, 512 * h:512 * h + 512])
                dve.drain()
                dve.bn_aggr(mv[s][:, 0, :], bst[s][:, 0:12])
                dve.drain()
                dve.tensor_copy(gst[s][:, 0:1], mv[s][:, 0, 0:1]).then_inc(sem(which + "_stat"), 1)
                dve.wait_ge(sem(which + "_group"), at(i, s, 2, 1))
                released(dve.tensor_copy(gst[s][:, 2:3], p3["3a"][:, 0:1]), "3a")
                dve.drain()
                dve.tensor_tensor(gst[s][:, 3:4], mv[s][:, 0, 0:1], gst[s][:, 2:3], ALU.subtract)
                dve.drain()
                dve.scalar_tensor_tensor(gst[s][:, 1:2], gst[s][:, 3:4], gst[s][:, 3:4], mv[s][:, 0, 1:2],
                                         ALU.mult, ALU.add).then_inc(sem(which + "_stat"), 1)
                dve.wait_ge(sem(which + "_group"), at(i, s, 2, 2))
                released(dve.tensor_scalar(var[s][:, 0:1], p3["3a"][:, 0:1], GN_EPS, None, ALU.add), "3a")
                dve.drain().then_inc(sem(which + "_var"), 1)
                dve.wait_ge(sem(which + "_rstd"), at(i, s, 1, 1))
                dve.scalar_tensor_tensor(nmr[s][:, 0:1], gst[s][:, 2:3], -1.0, rstd[s][:, 0:1], ALU.mult, ALU.mult)
                dve.drain()
                dve.tensor_scalar(xn[s][:, :], xc[s][:, :], rstd[s][:, 0:1], nmr[s][:, 0:1], ALU.mult, ALU.add)\
                    .then_inc(sem(which + "_xn"), 1)

            def l0(i, s):
                dve.wait_ge(sem("off_ready"), at(i, s, 1, 1))
                released(dve.scalar_tensor_tensor(pos, pair[2][0:NOFF, :], const("offb"), const("base"), ALU.add, ALU.add), "2")
                dve.drain()
                dve.tensor_copy(offs[0:NOFF, :], pos)
                dve.drain()
                dve.tensor_tensor(rest, pos, offs[0:NOFF, :], ALU.subtract)
                dve.drain().then_inc(sem("offs_split"), 1)
                dve.tensor_copy(offcut[0], rest)
                dve.drain().then_inc(sem("offs_cut"), 1)
                dve.tensor_tensor(offcut[1], rest, offcut[0], ALU.subtract)
                dve.drain().then_inc(sem("offs_cut"), 1)
                for g in range(1, 3 * NT, 2):
                    c, third = divmod(g, 3)
                    dve.wait_ge(sem("z_ready"), at(i, s, 3 * NT, g + 1))
                    released(dve.tensor_copy(z[:, c, 3 * third:3 * third + 3, :],
                                             p3["3b"][:, 0:384].rearrange("p (a b) -> p a b", a=3)), "3b")
                dve.drain().then_inc(sem("z_kept"), 3 * NT // 2)
                order = [(p, k, c, lo, hi) for p in range(len(PASSES)) for k in range(TAPS) for c, lo, hi in PASSES[p]]

                def cut(n):
                    p, k, c, lo, hi = order[n]
                    dve.wait_ge(sem("ay_ready"), at(i, s, PIECES, n + 1))
                    if n == 0 or order[n - 1][:2] != (p, k):
                        m = p * TAPS + k
                        dve.tensor_scalar(hx[m % 2], hx[m % 2], 1.0, 0.0, ALU.subtract, ALU.min)
                    dve.tensor_scalar(ay[n % RING][:, 0:hi - lo], ay[n % RING][:, 0:hi - lo], 1.0, 0.0, ALU.subtract, ALU.min)

                cut(0)
                for n, (p, k, c, lo, hi) in enumerate(order):
                    if n + 1 < len(order):
                        cut(n + 1)
                    dve.drain()
                    dve.wait_ge(sem("hat_used"), at(i, s, PIECES, n + 1))
                    m = p * TAPS + k
                    dve.tensor_tensor(hat[n % RING][:, 0:hi - lo], ay[n % RING][:, 0:hi - lo], hx[m % 2][:, lo:hi],
                                      ALU.mult).then_inc(sem("hat_ready"), 1)
                dve.wait_ge(sem("hat_used"), at(i, s, PIECES, PIECES) + RING)
                released(dve.scalar_tensor_tensor(xc[s][:, :], pair[0][:, :], const("b0"), xc[s][:, :], ALU.add, ALU.add), "0")
                dve.drain()

            def core(i, s, inst):
                for j in range(NT + 3):
                    if j < NT:
                        dve.wait_ge(sem("energy"), at4(i, inst, NT, j + 1))
                        dve.tensor_reduce(nmax[s][:, j:j + 1], pair[j % 2][:, :], AX.X, ALU.max, negate=True)\
                            .then_inc(sem("nmax"), 1)
                    if inst >= 2 and 1 <= j <= NT:
                        jj = j - 1
                        off = (NT - 1 - jj) * P
                        dve.wait_ge(sem("prob_exp"), at4(i, inst, NT, jj + 1))
                        dve.tensor_tensor_reduce(out=pr[jj % 2], in0=pr[jj % 2], in1=const("toep")[:, off:off + N],
                                                 scale=1.0, scalar=0.0, op0=ALU.mult, op1=ALU.add,
                                                 accum_out=rsum[s][:, jj:jj + 1])
                        dve.drain().then_inc(sem("prob_biased"), 1)
                    if j >= 3:
                        jj = j - 3
                        bank = ("3a", "3b")[jj % 2]
                        dve.wait_ge(sem("pv"), at4(i, inst, NT, jj + 1) + 2)
                        dve.reciprocal(rinv[s][:, jj:jj + 1], rsum[s][:, jj:jj + 1])
                        dve.drain()
                        if inst < 2:
                            ins = dve.tensor_scalar(tn[s][:, jj, :], p3[bank][:, 0:P], rinv[s][:, jj:jj + 1], None, ALU.mult)
                        else:
                            ins = dve.scalar_tensor_tensor(tok[s][:, jj, :], p3[bank][:, 0:P], rinv[s][:, jj:jj + 1],
                                                           tok[s][:, jj, :], ALU.mult, ALU.add)
                        released(ins, bank)
                        dve.drain().then_inc(sem("o_kept"), 1)

            def keep_v(i, s, ready, bias, done):
                dve.wait_ge(sem(ready), at(i, s, 3, 3))
                released(dve.tensor_tensor(vt[s][:, :, :], pair[2][:, :].rearrange("p (a b) -> p a b", a=NT),
                                           over_tiles(const(bias)), ALU.add), "2")
                dve.drain().then_inc(sem(done), 1)

            def l1_out(i, s):
                dve.wait_ge(sem("att1_T"), at(i, s, 1, 1))
                released(dve.tensor_tensor(xn[s][:, :], pair[2][:, :], xn[s][:, :], ALU.add), "2")
                dve.drain().then_inc(sem("y1_kept"), 1)
                dve.wait_ge(sem("tok1"), at(i, s, 1, 1))
                released(dve.tensor_tensor(tok[s][:, :, :], pair[0][:, :].rearrange("p (a b) -> p a b", a=NT),
                                           over_tiles(const("bo1")), ALU.add), "0")
                dve.drain().then_inc(sem(f"x_used{s}"), 1)

            def ln(i, s, which):
                for j in range(NT):
                    dve.bn_stats(bst[s][:, 6 * j:6 * j + 6], tok[s][:, j, :])
                dve.drain()
                for j in range(NT):
                    dve.bn_aggr(mv[s][:, j, :], bst[s][:, 6 * j:6 * j + 6])
                dve.drain()
                dve.tensor_scalar(var[s][:, :], mv[s][:, :, 1], LN_EPS, None, ALU.add).then_inc(sem(which + "_var"), 1)
                dve.wait_ge(sem(which + "_rstd"), at(i, s, 1, 1))
                dve.scalar_tensor_tensor(nmr[s][:, :], mv[s][:, :, 0], -1.0, rstd[s][:, :], ALU.mult, ALU.mult)
                dve.drain()
                for j in range(NT):
                    dve.tensor_scalar(tn[s][:, j, :], tok[s][:, j, :], rstd[s][:, j:j + 1], nmr[s][:, j:j + 1],
                                      ALU.mult, ALU.add)
                dve.drain().then_inc(sem(which + "_tn"), 1)

            def gate(i, s, inst, f):
                dve.wait_ge(sem("gate"), at4(i, inst, 1, 1))
                released(dve.tensor_tensor(lg[s][:, :, :], p3["3a"][:, 0:NT * E].rearrange("p (a b) -> p a b", a=NT),
                                           over_tiles(const("gb" + f)), ALU.add), "3a")
                dve.drain()
                dve.tensor_reduce(gmx[s][:, :], lg[s][:, :, :], AX.X, ALU.max)
                dve.drain()
                dve.tensor_tensor(lg[s][:, :, :], lg[s][:, :, :], inner(gmx[s][:, :], E), ALU.subtract)\
                    .then_inc(sem("logits"), 1)
                dve.wait_ge(sem("gate_exp"), at4(i, inst, 1, 1))
                dve.tensor_reduce(gsum[s][:, :], lg[s][:, :, :], AX.X, ALU.add)
                dve.drain()
                dve.reciprocal(gsum[s][:, :], gsum[s][:, :])
                dve.drain()
                dve.tensor_tensor(lg[s][:, :, :], lg[s][:, :, :], inner(gsum[s][:, :], E), ALU.mult)
                dve.drain()
                other = lg[s][:, :, :].rearrange("p a (o b) -> p a o b", o=1).to_broadcast([P, NT, E, E])
                own = lg[s][:, :, :].rearrange("p a (b o) -> p a b o", o=1).to_broadcast([P, NT, E, E])
                lower = const("low").rearrange("p (o b c) -> p o b c", o=1, b=E).to_broadcast([P, NT, E, E])
                dve.tensor_tensor(wins[:, :, :, :], other, own, ALU.is_gt)
                dve.tensor_tensor(ties[:, :, :, :], other, own, ALU.is_equal)
                dve.drain()
                dve.tensor_tensor(ties[:, :, :, :], ties[:, :, :, :], lower, ALU.mult)
                dve.drain()
                dve.tensor_tensor(wins[:, :, :, :], wins[:, :, :, :], ties[:, :, :, :], ALU.add)
                dve.drain()
                dve.tensor_reduce(cw[s][:, :, :], wins[:, :, :, :], AX.X, ALU.add)
                dve.drain()
                dve.scalar_tensor_tensor(cw[s][:, :, :], cw[s][:, :, :], 1.5, lg[s][:, :, :], ALU.is_lt, ALU.mult)\
                    .then_inc(sem("cw"), 1)
                dve.wait_ge(sem("cw_T"), at4(i, inst, 1, 1))
                released(dve.tensor_copy(cwT[s][:, :], p3["3b"][0:NT * E, 0:P]), "3b")
                dve.drain().then_inc(sem("cwT_kept"), 1)

            def ffn(i, s, inst, f):
                gate(i, s, inst, f)

                def take(e, q):
                    src = pair[2 + q % 2]
                    for j in range(NT):
                        ins = dve.scalar_tensor_tensor(tok[s][:, j, :], src[:, j * P:(j + 1) * P], cw[s][:, j, e:e + 1],
                                                       tok[s][:, j, :], ALU.mult, ALU.add)
                        if q % 2 and j in (NT // 2 - 1, NT - 1):
                            released(ins, "3a" if j < NT // 2 else "3b")
                    if q % 2 == 0:
                        released(ins, "2")
                    dve.drain()

                for e in range(E):
                    dve.wait_ge(sem("expert"), at4(i, inst, E, e + 1) + 2)
                    take(e, 0 if e == 0 else e + 1)
                    if e == 0:
                        dve.wait_ge(sem("bias2"), at4(i, inst, 1, 1))
                        for h, bank in enumerate(("3a", "3b")):
                            released(dve.tensor_tensor(tok[s][:, 4 * h:4 * h + 4, :],
                                                       p3[bank].rearrange("p (a b) -> p a b", a=4),
                                                       tok[s][:, 4 * h:4 * h + 4, :], ALU.add), bank)
                        dve.drain()

            def l3_norm(i, s):
                kvs = kv[s].rearrange("p (a b) -> p a b", a=NT)
                for g in range(2):
                    dve.wait_ge(sem("kv3"), at(i, s, 2, g + 1))
                    released(dve.tensor_tensor(kvs[:, 4 * g:4 * g + 4, :], pair[1 + g][:, :].rearrange("p (a b) -> p a b", a=4),
                                               over_tiles(const("bkv3"), 4), ALU.add), str(1 + g))
                dve.drain()
                heads = kv[s].rearrange("p (g d) -> p g d", d=HEADC)
                dve.tensor_reduce(hm[s][:, :], heads, AX.X, ALU.add)
                dve.drain()
                dve.tensor_scalar(hm[s][:, :], hm[s][:, :], 1.0 / HEADC, None, ALU.mult)
                dve.drain()
                dve.tensor_tensor(heads, heads, inner(hm[s][:, :], HEADC), ALU.subtract).then_inc(sem("kv3_centred"), 1)
                dve.wait_ge(sem("kv3_squared"), at(i, s, 1, 1))
                dve.tensor_reduce(hm[s][:, :], prob[:, :].rearrange("p (g d) -> p g d", d=HEADC), AX.X, ALU.add)\
                    .then_inc(sem("kv3_sumsq"), 1)
                dve.wait_ge(sem("kv3_std"), at(i, s, 1, 1))
                dve.tensor_scalar(hm[s][:, :], hm[s][:, :], HEAD_EPS, None, ALU.add)
                dve.drain()
                dve.reciprocal(hm[s][:, :], hm[s][:, :])
                dve.drain()
                dve.tensor_tensor(heads, heads, inner(hm[s][:, :], HEADC), ALU.mult)
                dve.drain()
                dve.tensor_tensor(kvs, kvs, over_tiles(const("lnw3")), ALU.mult)
                dve.drain()
                dve.tensor_tensor(kvs, kvs, over_tiles(const("lnb3")), ALU.add).then_inc(sem("kv3_normed"), 1)

            def l3_out(i, s):
                dve.wait_ge(sem("state3"), at(i, s, 1, 1))
                released(dve.tensor_tensor(kvm[s][:, :], p3["3a"][:, 0:P], const("kvmask"), ALU.mult), "3a")
                dve.drain().then_inc(sem("state3_kept"), 1)
                dve.wait_ge(sem("read3"), at(i, s, 1, 1))
                released(dve.tensor_tensor(kT[s][:, :], pair[0][:, :], tnT[s][:, :], ALU.add), "0")
                dve.drain().then_inc(sem("ret3_kept"), 1)
                dve.wait_ge(sem("tok3_res"), at(i, s, 1, 1))
                dve.wait_ge(sem("proj3"), at(i, s, 1, 1))
                released(dve.tensor_tensor(tn[s][:, :, :], pair[1][:, :].rearrange("p (a b) -> p a b", a=NT),
                                           over_tiles(const("bp3")), ALU.add), "1")
                dve.drain().then_inc(sem("p3_biased"), 1)

            def l3_add(i, s):
                dve.wait_ge(sem("p3_gelu"), at(i, s, 1, 1))
                dve.tensor_tensor(tok[s][:, :, :], tok[s][:, :, :], tn[s][:, :, :], ALU.add)
                dve.drain()

            dve.memset(offs[:, :], 0.0)
            for name, n in (("hat_ready", RING), ("hat_used", RING), ("pv", 2), ("expert", 2), ("seeded", 1),
                            *(("free" + b, 1) for b in BANKS), *((f"x_used{s}", 1) for s in range(SLOTS))):
                dve.drain().then_inc(sem(name), n)
            dve.wait_ge(sem("early_loaded"), 32)
            with dve.Fori(0, B // SLOTS) as i:
                for s in range(SLOTS):
                    dve.wait_ge(sem(f"x_loaded{s}"), i * 16 + 16)
                    gn(i, s, "gn0")
                for s in range(SLOTS):
                    l0(i, s)
                for s in range(SLOTS):
                    gn(i, s, "gn1")
                for s in range(SLOTS):
                    keep_v(i, s, "proj1", "bv1", "v1_kept")
                    core(i, s, s)
                for s in range(SLOTS):
                    l1_out(i, s)
                for s in range(SLOTS):
                    ln(i, s, "ln2")
                dve.wait_ge(sem("late_loaded"), 16)
                for s in range(SLOTS):
                    keep_v(i, s, "proj2", "bv2", "v2_kept")
                    core(i, s, 2 + s)
                    ln(i, s, "lnf2")
                for s in range(SLOTS):
                    ffn(i, s, s, "a")
                    ln(i, s, "ln3")
                for s in range(SLOTS):
                    l3_norm(i, s)
                for s in range(SLOTS):
                    l3_out(i, s)
                for s in range(SLOTS):
                    l3_add(i, s)
                    ln(i, s, "lnf3")
                for s in range(SLOTS):
                    ffn(i, s, 2 + s, "b")
                    dve.drain().then_inc(sem("tok_final"), 1)


def packed(part, arrays, np):
    cols, n = columns(part)
    out = np.zeros((P, n), np.float32)
    for name, (at, p, width) in cols.items():
        out[0:p, at:at + width] = arrays[name]
    return out


def kernel(**inputs):
    import ml_dtypes
    import numpy as np
    import concourse.bacc as bacc
    from concourse.bass_utils import run_bass_kernel_spmd

    w = {k: np.asarray(v) for k, v in inputs.items()}
    f = np.float32

    def rows(v):
        return np.broadcast_to(v.reshape(1, -1), (P, v.size))

    p, n = np.arange(P), np.arange(N)
    tap = np.arange(TAPS)
    base = np.stack([n // HW + (tap // 3)[:, None] - 1, n % HW + (tap % 3)[:, None] - 1], 1).reshape(NOFF, N)
    gap = np.abs(np.arange(TOEP)[None, :] - (NT - 1) * P - p[:, None]).astype(np.float64)
    decay = (gap + 1e-9) ** (0.1 - 1.5)
    toep = decay / 1e-9 ** (0.1 - 1.5) + 1e-9
    toep = np.where(gap == 0, 1.0 + 1e-9, toep)
    head = p // HEADC
    a = dict(ident=np.eye(P), grp=(p[:, None] // 4 == p // 4) / 4.0, kvmask=(head[:, None] == head) / float(N),
             base=base, yneg=-(ROWS * np.arange(NT)[None, :] + p[:, None] // HW), xneg=-(p[:, None] % HW), toep=toep,
             low=rows((np.arange(E)[None, :] < np.arange(E)[:, None]).astype(f)))
    a.update(offw=w["L0_conv_offset_w"].transpose(1, 2, 3, 0).reshape(C, -1), offb=w["L0_conv_offset_b"][:, None],
             w0=w["L0_conv_weight"].transpose(1, 2, 3, 0).reshape(C, -1), b0=w["L0_conv_bias"][:, None],
             wq1=w["L1_conv_Wq"].T, wk1=w["L1_conv_Wk"].T, bq1=w["L1_conv_bq"][:, None], bk1=w["L1_conv_bk"][:, None],
             wv1=w["L1_conv_Wv"].T, bv1=rows(w["L1_conv_bv"]), wo1=w["L1_conv_Wo"].T, bo1=rows(w["L1_conv_bo"]))
    a.update(wq2=w["L2_attn_Wq"].T, wk2=w["L2_attn_Wk"].T, bq2=w["L2_attn_bq"][:, None], bk2=w["L2_attn_bk"][:, None],
             wv2=w["L2_attn_Wv"].T, bv2=rows(w["L2_attn_bv"]))
    wqkv = w["L3_attn_W_qkv"].reshape(C // HEADC, 3, HEADC, C).transpose(1, 3, 0, 2).reshape(3, C, C)
    bqkv = w["L3_attn_b_qkv"].reshape(C // HEADC, 3, HEADC).transpose(1, 0, 2).reshape(3, C)
    a.update(wq3=wqkv[0], bq3=bqkv[0][:, None], wkv3=np.concatenate([wqkv[1], wqkv[2]], 1), bkv3=rows(bqkv[1:]),
             lnw3=rows(np.concatenate([w["L3_attn_kln_w"].reshape(-1), w["L3_attn_vln_w"].reshape(-1)])),
             lnb3=rows(np.concatenate([w["L3_attn_kln_b"].reshape(-1), w["L3_attn_vln_b"].reshape(-1)])),
             wp3=w["L3_attn_W_proj"].T, bp3=rows(w["L3_attn_b_proj"]))
    for name, layer in (("a", "L2_ffn_"), ("b", "L3_ffn_")):
        b2 = np.zeros((NT * E, NT * C), f)
        for j in range(NT):
            b2[j * E:(j + 1) * E, j * C:(j + 1) * C] = w[layer + "b2"]
        a["gw" + name] = w[layer + "gate_w"]
        a["gb" + name] = rows(w[layer + "gate_b"])
        a["w1" + name] = w[layer + "W1"].transpose(1, 0, 2).reshape(C, -1)
        a["b1" + name] = w[layer + "b1"].reshape(E * HC, P).T
        a["w2" + name] = w[layer + "W2"].reshape(E * HC, P, C).transpose(1, 0, 2).reshape(P, -1)
        a["b2" + name] = b2
    early, late = layout()
    sel = np.zeros((96, NOFF, P), ml_dtypes.bfloat16)
    for q in range(3):
        for r in range(NOFF):
            sel[32 * q + r, r, :] = 1
    arrays = dict(x=np.ascontiguousarray(w["x"]), sel=sel.reshape(96, -1), early=packed(early, a, np), late=packed(late, a, np))

    nc = bacc.Bacc("TRN2", target_bir_lowering=False, num_devices=1)
    args = [nc.dram_tensor(k, v.shape, mybir.dt.from_np(v.dtype), kind="ExternalInput").ap() for k, v in arrays.items()]
    result = nc.dram_tensor("result", (B, C, HW, HW), F32, kind="ExternalOutput").ap()
    build(nc, *args, result)
    r = run_bass_kernel_spmd(nc, [arrays], core_ids=[0])
    return r.results[0]["result"]
```

```python
from contextlib import ExitStack

import concourse.bass as bass
from concourse import mybir

F32 = mybir.dt.float32
BF16 = mybir.dt.bfloat16
ALU = mybir.AluOpType
ACT = mybir.ActivationFunctionType
AX = mybir.AxisListType

P = 128
B = 8
HW = 32
N = HW * HW
NT = N // P
C = 128
TAPS = 9
NOFF = 2 * TAPS
D1 = C // 8
E = 8
HID = 256
HC = HID // P
HEADC = 8
SLOTS = 2
ROWS = P // HW
GN_EPS, LN_EPS, HEAD_EPS = 1e-5, 1e-5, 1e-5
TOEP = N + (NT - 1) * P
REACH = 2
WIDE = 256


def near_pieces(k):
    ky = k // 3
    return [(c, HW * max(0, ROWS * c + 1 - REACH - ky), HW * min(HW, ROWS * (c + 1) + 1 + REACH - ky))
            for c in range(NT)]


def far_pieces(k):
    out = []
    for c, lo, hi in near_pieces(k):
        for a, b in ((0, lo), (hi, N)):
            while a < b:
                out.append((c, a, min(b, a + WIDE)))
                a += WIDE
    return out


NEAR = [(k, *p) for k in range(TAPS) for p in near_pieces(k)]
FAR = [(k, *p) for k in range(TAPS) for p in far_pieces(k)]
RING = 8


def layout():
    early = dict(ident=(P, P), grp=(P, P), kvmask=(P, P), base=(NOFF, N), yneg=(P, NT), xneg=(P, 1),
                 offw=(C, 3 * 96), offb=(NOFF, 1), isy=(NOFF, 1), ones=(NOFF, P), w0=(C, TAPS * C), b0=(C, 1),
                 wq1=(C, D1), wk1=(C, D1), bq1=(D1, 1), bk1=(D1, 1), wv1=(C, C), bv1=(P, C), wo1=(C, C), bo1=(P, C))
    late = dict(wq2=(C, C), wk2=(C, C), bq2=(C, 1), bk2=(C, 1), wv2=(C, C), bv2=(P, C), toep=(P, TOEP),
                low=(P, E * E),
                wq3=(C, C), bq3=(C, 1), wkv3=(C, 2 * C), bkv3=(P, 2 * C), lnw3=(P, 2 * C), lnb3=(P, 2 * C),
                wp3=(C, C), bp3=(P, C))
    for f in "ab":
        late.update({"gw" + f: (C, E), "gb" + f: (P, E), "w1" + f: (C, E * HID), "b1" + f: (P, E * HC),
                     "w2" + f: (P, E * HC * C), "b2" + f: (NT * E, NT * C)})
    return early, late


def columns(part):
    at, out = 0, {}
    for name, (p, n) in part.items():
        out[name] = (at, p, n)
        at += n
    return out, at


def build(nc, x, sel_in, early_in, late_in, out):
    early, late = layout()
    ecols, en = columns(early)
    lcols, ln = columns(late)
    with ExitStack() as ctx:
        def sb(name, shape, dt=F32):
            return ctx.enter_context(nc.sbuf_tensor(name, shape, dt))

        sems = {}

        def sem(name):
            if name not in sems:
                sems[name] = ctx.enter_context(nc.semaphore(name))
            return sems[name]

        early_sb, late_sb = sb("early_sb", [P, en]), sb("late_sb", [P, ln])

        def const(name):
            tile, cols = (early_sb, ecols) if name in ecols else (late_sb, lcols)
            at, p, n = cols[name]
            return tile[0:p, at:at + n]

        ident, grp = const("ident"), const("grp")
        sel = sb("sel_sb", [96, NOFF * P], BF16)
        xc = [sb(f"xc{s}", [P, N]) for s in range(SLOTS)]
        xrows = [sb(f"xrows{s}", [P, N + 2 * HW]) for s in range(SLOTS)]
        xn = [xrows[s][:, HW:HW + N] for s in range(SLOTS)]
        tok = [sb(f"tok{s}", [P, NT, C]) for s in range(SLOTS)]
        tn = [sb(f"tn{s}", [P, NT, C]) for s in range(SLOTS)]
        tnT = [sb(f"tnT{s}", [P, N]) for s in range(SLOTS)]
        qT = [sb(f"qT{s}", [P, N]) for s in range(SLOTS)]
        kT = [sb(f"kT{s}", [P, N]) for s in range(SLOTS)]
        vt = [sb(f"vt{s}", [P, NT, C]) for s in range(SLOTS)]
        hx = [vt[s][:].rearrange("p a b -> p (a b)") for s in range(SLOTS)]
        offs = sb("offs", [96, N], BF16)
        big = sb("big", [P, NT * TAPS * C])
        z = big[:, :].rearrange("p (c k o) -> p c k o", c=NT, k=TAPS)
        kv = [big[:, 2 * N * s:2 * N * (s + 1)] for s in range(SLOTS)]
        hid = [big[:, (4 + r) * N:(5 + r) * N] for r in range(4)]
        prob = sb("prob", [P, 2 * N])
        pr = [prob[:, r * N:(r + 1) * N] for r in range(2)]
        pos, rest = prob[0:NOFF, 0:N], prob[0:NOFF, N:2 * N]
        dist = sb("dist", [P, 2 * RING * WIDE])
        ay = [dist[:, r * WIDE:(r + 1) * WIDE] for r in range(RING)]
        hat = [dist[:, (RING + r) * WIDE:(RING + r + 1) * WIDE] for r in range(RING)]
        offcut = [dist[0:NOFF, n * N // 2:(n + 1) * N // 2].bitcast(BF16) for n in range(2)]
        dymax = sb("dymax", [NOFF, 1])
        dyok = sb("dyok", [NOFF, P])
        isfar = [sb(f"isfar{s}", [1, 1], mybir.dt.int32) for s in range(SLOTS)]
        prT = [dist[:, r * N:(r + 1) * N].rearrange("p (a b) -> p a b", a=NT) for r in range(2)]
        mhalf = sb("mhalf", [P, NT])
        bst = [sb(f"bst{s}", [P, NT * 6]) for s in range(SLOTS)]
        mv = [sb(f"mv{s}", [P, NT, 2]) for s in range(SLOTS)]
        gst = [sb(f"gst{s}", [P, 4]) for s in range(SLOTS)]
        var = [sb(f"var{s}", [P, NT]) for s in range(SLOTS)]
        rstd = [sb(f"rstd{s}", [P, NT]) for s in range(SLOTS)]
        nmr = [sb(f"nmr{s}", [P, NT]) for s in range(SLOTS)]
        nmax = [sb(f"nmax{s}", [P, NT]) for s in range(SLOTS)]
        rsum = [sb(f"rsum{s}", [P, NT]) for s in range(SLOTS)]
        rinv = [sb(f"rinv{s}", [P, NT]) for s in range(SLOTS)]
        lg = [sb(f"lg{s}", [P, NT, E]) for s in range(SLOTS)]
        gmx = [sb(f"gmx{s}", [P, NT]) for s in range(SLOTS)]
        gsum = [sb(f"gsum{s}", [P, NT]) for s in range(SLOTS)]
        cw = [sb(f"cw{s}", [P, NT, E]) for s in range(SLOTS)]
        cwT = [sb(f"cwT{s}", [NT * E, P]) for s in range(SLOTS)]
        wins, ties = (prob[:, r * NT * E * E:(r + 1) * NT * E * E].rearrange("p (a b c) -> p a b c", a=NT, b=E)
                      for r in range(2))
        bqs = sb("bqs", [P, 1])
        hm = [sb(f"hm{s}", [P, NT * 32]) for s in range(SLOTS)]
        kvm = [sb(f"kvm{s}", [P, P]) for s in range(SLOTS)]
        xo = qT

        pair = [ctx.enter_context(nc.psum_tensor(f"pair{i}", [P, N], F32)) for i in range(4)]
        BANKS = ("0", "1", "2", "3a", "3b")
        p3 = {"3a": pair[3][:, 0:512], "3b": pair[3][:, 512:1024]}

        def released(ins, bank):
            return ins.then_inc(sem("free" + bank), 1)

        def at(i, s, k, c):
            return i * (SLOTS * k) + (s * k + c)

        def at4(i, inst, k, c):
            return i * (4 * k) + (inst * k + c)

        UNITS = E * HC
        block = ctx.enter_context(nc.Block())

        @block.sync
        def _(sp):
            sp.dma_start(early_sb[:, :], early_in).then_inc(sem("early_loaded"), 16)
            sp.dma_start(sel[:, :], sel_in).then_inc(sem("early_loaded"), 16)
            with sp.Fori(0, B // SLOTS) as i:
                for s in range(SLOTS):
                    sp.wait_ge(sem(f"x_used{s}"), i + 1)
                    sp.dma_start(xc[s][:, :], x[i * SLOTS + s].rearrange("c h w -> c (h w)")).then_inc(sem(f"x_loaded{s}"), 16)

        @block.gpsimd
        def _(pool):
            pool.memset(mhalf[:, :], -0.5).then_inc(sem("mhalf_set"), 1)
            for s in range(SLOTS):
                pool.memset(xrows[s][:, :], 0.0)
            pool.drain().then_inc(sem("pads_zero"), 1)
            pool.wait_ge(sem("mhalf_set"), 1)

            def rsqrt(i, s, which, width):
                pool.wait_ge(sem(which + "_var"), at(i, s, 1, 1))
                pool.tensor_tensor(rstd[s][:, 0:width], var[s][:, 0:width], mhalf[:, 0:width],
                                   ALU.pow).then_inc(sem(which + "_rstd"), 1)

            with pool.Fori(0, B // SLOTS) as i:
                for which, width in (("gn0", 1), ("gn1", 1), ("ln2", NT), ("lnf2", NT), ("ln3", NT), ("lnf3", NT)):
                    for s in range(SLOTS):
                        rsqrt(i, s, which, width)
                        if which == "ln3":
                            pool.wait_ge(sem("ln3_tn"), at(i, s, 1, 1))
                            pool.tensor_tensor(tok[s][:, :, :], tok[s][:, :, :], tn[s][:, :, :],
                                               ALU.add).then_inc(sem("tok3_res"), 1)

        @block.tensor
        def _(pe):
            uses = dict.fromkeys(BANKS, 0)
            totals = {"0": 60, "1": 74, "2": 90, "3a": 70, "3b": 62}

            def claim(i, bank):
                uses[bank] += 1
                pe.wait_ge(sem("free" + bank), i * totals[bank] + uses[bank])

            def gn(i, s, which):
                for c in range(2):
                    pe.wait_ge(sem(which + "_stat"), at(i, s, 2, c + 1))
                    claim(i, "3a")
                    pe.matmul(p3["3a"][:, 0:1], grp, gst[s][:, c:c + 1], start=True, stop=True)\
                        .then_inc(sem(which + "_group"), 1)

            def l0(i, s):
                pe.wait_ge(sem("gn0_xn"), at(i, s, 1, 1))
                claim(i, "2")
                for h in range(2):
                    for ky in range(3):
                        last = pe.matmul(pair[2][0:96, h * 512:h * 512 + 512], const("offw")[:, ky * 96:(ky + 1) * 96],
                                         xrows[s][:, HW * ky + 512 * h:HW * ky + 512 * h + 512],
                                         start=(ky == 0), stop=(ky == 2))
                last.then_inc(sem("off_ready"), 1)
                for g in range(3 * NT):
                    c, third = divmod(g, 3)
                    bank = ("3a", "3b")[g % 2]
                    claim(i, bank)
                    pe.matmul(p3[bank][:, 0:384], xn[s][:, c * P:(c + 1) * P],
                              const("w0")[:, third * 384:(third + 1) * 384], start=True, stop=True)\
                        .then_inc(sem("z_ready"), 1)
                pe.wait_ge(sem("offs_split"), at(i, s, 3, 3))

                def spread(k):
                    for bank, r in ((1, 2 * k + 1), (2, 2 * k)):
                        claim(i, str(bank))
                        spread_row(bank, r).then_inc(sem("spread"), 1)

                def spread_far(k):
                    for bank, r in ((1, 2 * k + 1), (2, 2 * k)):
                        if k:
                            pe.wait_ge(sem(f"far_free{bank}"), at(i, s, TAPS, k))
                        spread_row(bank, r).then_inc(sem("far_spread"), 1)

                def spread_row(bank, r):
                    for h in range(2):
                        last = pe.matmul(pair[bank][:, h * 512:(h + 1) * 512], sel[:, r * P:(r + 1) * P],
                                         offs[:, h * 512:(h + 1) * 512], start=True, stop=True)
                    return last

                def sample(n, k, c, lo, hi, who, opened, final):
                    for a, b in ((lo, min(hi, 512)), (max(lo, 512), hi)):
                        if a < b:
                            bank = a // 512
                            last = pe.matmul(pair[0][:, a:b], z[:, c, k, :], hat[n % RING][:, a - lo:b - lo],
                                             start=bank not in opened, stop=final, skip_group_check=True)
                            opened.add(bank)
                    last.then_inc(sem(who + "hat_used"), 1)

                spread(0)
                claim(i, "3b")
                pe.wait_ge(sem("dy_checked"), at(i, s, 1, 1))
                pe.matmul(p3["3b"][:, 0:1], dyok[:, :], const("ones")[:, 0:1], start=True, stop=True)\
                    .then_inc(sem("dy_count"), 1)
                claim(i, "0")
                pe.wait_ge(sem("z_kept"), at(i, s, 3 * NT, 3 * NT))
                opened = set()
                for n, (k, c, lo, hi) in enumerate(NEAR):
                    if n % NT == 0 and k + 1 < TAPS:
                        spread(k + 1)
                    if n % 2 == 0:
                        pe.wait_ge(sem("hat_ready"), at(i, s, len(NEAR), n + 2) + RING)
                    if n == len(NEAR) - 1:
                        pe.wait_ge(sem("far_known"), at(i, s, 1, 1))
                    sample(n, k, c, lo, hi, "", opened, k == TAPS - 1)
                flag = pe.value_load(isfar[s][0:1, 0:1], min_val=0, max_val=1)
                with pe.If(flag > 0):
                    first = {k: min(n for n, p in enumerate(FAR) if p[0] == k) for k in range(TAPS)}
                    for n, (k, c, lo, hi) in enumerate(FAR):
                        if n == 0:
                            for bank in (1, 2):
                                pe.wait_ge(sem(f"free{bank}"), i * totals[str(bank)] + uses[str(bank)] + 1)
                            spread_far(0)
                        if k + 1 < TAPS and n == first[k + 1] - RING:
                            spread_far(k + 1)
                        pe.wait_ge(sem("far_hat_ready"), at(i, s, len(FAR), n + 1))
                        sample(n, k, c, lo, hi, "far_", opened, True)
                with pe.Else():
                    pe.drain().then_inc(sem("far_spread"), 2 * TAPS)
                    pe.drain().then_inc(sem("far_hat_used"), len(FAR))

            def project(i, s, bank, w, src, m, done):
                claim(i, str(bank))
                for h in range(2):
                    last = pe.matmul(pair[bank][0:m, h * 512:(h + 1) * 512], w, src[:, h * 512:(h + 1) * 512],
                                     start=True, stop=True)
                last.then_inc(sem(done), 1)

            def tiles(i, s, bank, src, w, done):
                claim(i, str(bank))
                for j in range(NT):
                    last = pe.matmul(pair[bank][:, j * P:(j + 1) * P], src[:, j * P:(j + 1) * P], w, start=True, stop=True)
                last.then_inc(sem(done), 1)

            def transposes(i, s, bank, src, done):
                claim(i, str(bank))
                for j in range(NT):
                    last = pe.transpose(pair[bank][:, j * P:(j + 1) * P], src[:, j, :], ident)
                last.then_inc(sem(done), 1)

            def core(i, s, inst, rows):
                for j in range(NT + 2):
                    if j < NT:
                        bank = j % 2
                        claim(i, str(bank))
                        for h in range(2):
                            last = pe.matmul(pair[bank][:, h * 512:(h + 1) * 512], qT[s][0:rows, j * P:(j + 1) * P],
                                             kT[s][0:rows, h * 512:(h + 1) * 512], start=True, stop=True)
                        last.then_inc(sem("energy"), 1)
                    if 1 <= j <= NT:
                        jj = j - 1
                        if inst < 2:
                            pe.wait_ge(sem("prob_exp"), at4(i, inst, NT, jj + 1))
                        else:
                            pe.wait_ge(sem("prob_biased"), at(i, s, NT, jj + 1))
                        transposes(i, s, 2, pr[jj % 2].rearrange("p (a b) -> p a b", a=NT), "prob_T")
                    if j >= 2:
                        jj = j - 2
                        bank = ("3a", "3b")[jj % 2]
                        pe.wait_ge(sem("probT_kept"), at4(i, inst, NT, jj + 1))
                        claim(i, bank)
                        for m in range(NT):
                            last = pe.matmul(p3[bank][:, 0:P], prT[jj % 2][:, m, :], vt[s][:, m, :],
                                             start=(m == 0), stop=(m == NT - 1))
                        last.then_inc(sem("pv"), 1)

            def l1(i, s):
                pe.wait_ge(sem("gn1_xn"), at(i, s, 1, 1))
                project(i, s, 0, const("wq1"), xn[s], D1, "proj1")
                project(i, s, 1, const("wk1"), xn[s], D1, "proj1")
                tiles(i, s, 2, xn[s], const("wv1"), "proj1")
                pe.wait_ge(sem("qk1_kept"), at(i, s, 2, 2))
                pe.wait_ge(sem("v1_kept"), at(i, s, 1, 1))
                core(i, s, s, D1)

            def l1_out(i, s):
                pe.wait_ge(sem("o_kept"), at4(i, s, NT, NT))
                transposes(i, s, 2, tn[s], "att1_T")
                pe.wait_ge(sem("y1_kept"), at(i, s, 1, 1))
                claim(i, "0")
                for j in range(NT):
                    pe.matmul(pair[0][:, j * P:(j + 1) * P], xn[s][:, j * P:(j + 1) * P], const("wo1"), start=True, stop=False)
                    last = pe.matmul(pair[0][:, j * P:(j + 1) * P], xc[s][:, j * P:(j + 1) * P], ident, start=False, stop=True)
                last.then_inc(sem("tok1"), 1)

            def ln_T(i, s, which):
                pe.wait_ge(sem(which + "_tn"), at(i, s, 1, 1))
                transposes(i, s, 2, tn[s], which + "_T")
                pe.wait_ge(sem(which + "_tnT"), at(i, s, 1, 1))

            def l2(i, s):
                ln_T(i, s, "ln2")
                project(i, s, 0, const("wq2"), tnT[s], C, "proj2")
                project(i, s, 1, const("wk2"), tnT[s], C, "proj2")
                tiles(i, s, 2, tnT[s], const("wv2"), "proj2")
                pe.wait_ge(sem("qk2_kept"), at(i, s, 2, 2))
                pe.wait_ge(sem("v2_kept"), at(i, s, 1, 1))
                core(i, s, 2 + s, C)

            def ffn(i, s, inst, which, f):
                ln_T(i, s, which)
                claim(i, "3a")
                for j in range(NT):
                    last = pe.matmul(p3["3a"][:, j * E:(j + 1) * E], tnT[s][:, j * P:(j + 1) * P], const("gw" + f),
                                     start=True, stop=True)
                last.then_inc(sem("gate"), 1)

                def hidden(e):
                    for h in range(HC):
                        col = e * HID + h * P
                        project(i, s, (HC * e + h) % 2, const("w1" + f)[:, col:col + P], tnT[s], P, "hidden")

                def pair_claim(q):
                    if q % 2:
                        claim(i, "3a")
                        claim(i, "3b")
                    else:
                        claim(i, "2")
                    return pair[2 + q % 2]

                def back(e, q):
                    pe.wait_ge(sem("gelu"), at4(i, inst, UNITS, HC * (e + 1)))
                    dst = pair_claim(q)
                    for j in range(NT):
                        for h in range(HC):
                            w = (e * HC + h) * C
                            last = pe.matmul(dst[:, j * P:(j + 1) * P], hid[(HC * e + h) % 4][:, j * P:(j + 1) * P],
                                             const("w2" + f)[:, w:w + C], start=(h == 0), stop=(h == HC - 1))
                    last.then_inc(sem("expert"), 1)

                hidden(0)
                hidden(1)
                pe.wait_ge(sem("cw"), at4(i, inst, 1, 1))
                claim(i, "3b")
                pe.matmul(p3["3b"][0:NT * E, 0:P], cw[s][:, :, :].rearrange("p a b -> p (a b)"), ident, start=True, stop=True)\
                    .then_inc(sem("cw_T"), 1)
                back(0, 0)
                hidden(2)
                pe.wait_ge(sem("cwT_kept"), at4(i, inst, 1, 1))
                dst = pair_claim(1)
                for j in range(NT):
                    last = pe.matmul(dst[:, j * P:(j + 1) * P], cwT[s][:, :], const("b2" + f)[:, j * C:(j + 1) * C],
                                     start=True, stop=True)
                last.then_inc(sem("bias2"), 1)
                for e in range(1, E):
                    back(e, e + 1)
                    if e + 2 < E:
                        hidden(e + 2)

            def l3(i, s):
                ln_T(i, s, "ln3")
                project(i, s, 0, const("wq3"), tnT[s], C, "q3")
                for g in range(2):
                    claim(i, str(1 + g))
                    for j in range(4):
                        t0 = (4 * g + j) * P
                        last = pe.matmul(pair[1 + g][:, j * 256:(j + 1) * 256], tnT[s][:, t0:t0 + P], const("wkv3"),
                                         start=True, stop=True)
                    last.then_inc(sem("kv3"), 1)

            def l3_out(i, s):
                kvs = kv[s].rearrange("p (a b) -> p a b", a=NT)
                pe.wait_ge(sem("kv3_normed"), at(i, s, 1, 1))
                claim(i, "3a")
                for j in range(NT):
                    last = pe.matmul(p3["3a"][:, 0:P], kvs[:, j, 0:C], kvs[:, j, C:2 * C], start=(j == 0), stop=(j == NT - 1))
                last.then_inc(sem("state3"), 1)
                pe.wait_ge(sem("state3_kept"), at(i, s, 1, 1))
                pe.wait_ge(sem("q3_kept"), at(i, s, 1, 1))
                project(i, s, 0, kvm[s][:, :], qT[s], P, "read3")
                pe.wait_ge(sem("ret3_kept"), at(i, s, 1, 1))
                tiles(i, s, 1, kT[s], const("wp3"), "proj3")

            def finish(i, s):
                pe.wait_ge(sem("tok_final"), at(i, s, 1, 1))
                transposes(i, s, 2, tok[s], "final_T")

            pe.wait_ge(sem("early_loaded"), 32)
            with pe.Fori(0, B // SLOTS) as i:
                for s in range(SLOTS):
                    gn(i, s, "gn0")
                for s in range(SLOTS):
                    l0(i, s)
                for s in range(SLOTS):
                    gn(i, s, "gn1")
                for s in range(SLOTS):
                    l1(i, s)
                for s in range(SLOTS):
                    l1_out(i, s)
                pe.wait_ge(sem("late_loaded"), 16)
                for s in range(SLOTS):
                    l2(i, s)
                for s in range(SLOTS):
                    ffn(i, s, s, "lnf2", "a")
                for s in range(SLOTS):
                    l3(i, s)
                for s in range(SLOTS):
                    l3_out(i, s)
                for s in range(SLOTS):
                    ffn(i, s, 2 + s, "lnf3", "b")
                for s in range(SLOTS):
                    finish(i, s)
            assert uses == totals, uses

        @block.scalar
        def _(act):
            def copy_out(i, s, bank, dst, ready, value, done, **kw):
                act.wait_ge(sem(ready), value)
                src = pair[bank][0:dst.shape[0], :]
                released(act.activation(dst, src, ACT.Identity if kw else ACT.Copy, **kw), str(bank))
                return act.drain().then_inc(sem(done), 1)

            def l0(i, s):
                for g in range(0, 3 * NT, 2):
                    c, third = divmod(g, 3)
                    act.wait_ge(sem("z_ready"), at(i, s, 3 * NT, g + 1))
                    released(act.activation(z[:, c, 3 * third:3 * third + 3, :],
                                            p3["3a"][:, 0:384].rearrange("p (a b) -> p a b", a=3), ACT.Copy), "3a")
                act.drain().then_inc(sem("z_kept"), 3 * NT // 2)
                for part in (1, 2):
                    act.wait_ge(sem("offs_cut"), at(i, s, 2, part))
                    src = offcut[part - 1]
                    act.activation(offs[32 * part:32 * part + NOFF, :], src, ACT.Copy).then_inc(sem("offs_split"), 1)
                def x_distance(k):
                    return act.activation(hx[k % 2], pair[1][:, :], ACT.Abs, bias=const("xneg"))

                def y_distance(n, c, lo, hi):
                    return act.activation(ay[n % RING][:, 0:hi - lo], pair[2][:, lo:hi], ACT.Abs, bias=const("yneg")[:, c:c + 1])

                for n, (k, c, lo, hi) in enumerate(NEAR):
                    if n % NT == 0:
                        act.wait_ge(sem("spread"), at(i, s, 2 * TAPS, 2 * k + 1))
                        released(x_distance(k), "1")
                        act.wait_ge(sem("spread"), at(i, s, 2 * TAPS, 2 * k + 2))
                    if n % 2 == 0:
                        act.wait_ge(sem("hat_ready"), at(i, s, len(NEAR), n + 2))
                    if n == len(NEAR) - 1:
                        act.wait_ge(sem("far_known"), at(i, s, 1, 1))
                    y_distance(n, c, lo, hi).then_inc(sem("ay_ready"), 1)
                    if n % NT == NT - 1:
                        act.drain().then_inc(sem("free2"), 1)
                flag = act.value_load(isfar[s][0:1, 0:1], min_val=0, max_val=1)
                with act.If(flag > 0):
                    act.wait_ge(sem("hat_ready"), at(i, s, len(NEAR), len(NEAR)) + RING)
                    for n, (k, c, lo, hi) in enumerate(FAR):
                        if n == 0 or FAR[n - 1][0] != k:
                            act.wait_ge(sem("far_spread"), at(i, s, 2 * TAPS, 2 * k + 1))
                            x_distance(k).then_inc(sem("far_free1"), 1)
                            act.wait_ge(sem("far_spread"), at(i, s, 2 * TAPS, 2 * k + 2))
                        if n >= RING:
                            act.wait_ge(sem("far_hat_ready"), at(i, s, len(FAR), n - RING + 1))
                        y_distance(n, c, lo, hi).then_inc(sem("far_ay_ready"), 1)
                        if n + 1 == len(FAR) or FAR[n + 1][0] != k:
                            act.drain().then_inc(sem("far_free2"), 1)
                with act.Else():
                    act.drain().then_inc(sem("far_free1"), TAPS)
                    act.drain().then_inc(sem("far_free2"), TAPS)
                    act.drain().then_inc(sem("far_ay_ready"), len(FAR))

            def core(i, s, inst):
                for j in range(NT + 1):
                    if j < NT:
                        act.wait_ge(sem("nmax"), at4(i, inst, NT, j + 1))
                        act.activation(pr[j % 2], pair[j % 2][:, :], ACT.Exp, bias=nmax[s][:, j:j + 1],
                                       accum_out=rsum[s][:, j:j + 1]).then_inc(sem(f"free{j % 2}"), 1)
                        act.drain().then_inc(sem("prob_exp"), 1)
                    if j >= 1:
                        jj = j - 1
                        act.wait_ge(sem("prob_T"), at4(i, inst, NT, jj + 1))
                        act.wait_ge(sem("pv"), at4(i, inst, NT, jj + 1))
                        released(act.activation(prT[jj % 2].rearrange("p a b -> p (a b)"), pair[2][:, :], ACT.Copy), "2")
                        act.drain().then_inc(sem("probT_kept"), 1)

            def l1(i, s):
                for n, (dst, bias) in enumerate(((qT, "bq1"), (kT, "bk1"))):
                    copy_out(i, s, n, dst[s][0:D1, :], "proj1", at(i, s, 3, n + 1), "qk1_kept", bias=const(bias))
                core(i, s, s)

            def ln_T(i, s, which):
                copy_out(i, s, 2, tnT[s][:, :], which + "_T", at(i, s, 1, 1), which + "_tnT")

            def l2(i, s):
                ln_T(i, s, "ln2")
                copy_out(i, s, 0, qT[s][:, :], "proj2", at(i, s, 3, 1), "qk2_kept", bias=bqs[:, 0:1], scale=float(C) ** -0.5)
                copy_out(i, s, 1, kT[s][:, :], "proj2", at(i, s, 3, 2), "qk2_kept", bias=const("bk2"))
                core(i, s, 2 + s)

            def ffn(i, s, inst, which, f):
                ln_T(i, s, which)

                def gelu(u):
                    if u % HC == 0:
                        act.wait_ge(sem("expert"), at4(i, inst, E, u // HC + 1))
                    act.wait_ge(sem("hidden"), at4(i, inst, UNITS, u + 1))
                    act.activation(hid[u % 4], pair[u % 2][:, :], ACT.Gelu, bias=const("b1" + f)[:, u:u + 1])\
                        .then_inc(sem(f"free{u % 2}"), 1)
                    act.drain().then_inc(sem("gelu"), 1)

                for u in range(4):
                    gelu(u)
                act.wait_ge(sem("logits"), at4(i, inst, 1, 1))
                act.activation(lg[s][:, :, :], lg[s][:, :, :], ACT.Exp).then_inc(sem("gate_exp"), 1)
                for u in range(4, UNITS):
                    gelu(u)

            def l3(i, s):
                ln_T(i, s, "ln3")
                copy_out(i, s, 0, qT[s][:, :], "q3", at(i, s, 1, 1), "q3_kept", bias=const("bq3"))

            def l3_norm(i, s):
                act.wait_ge(sem("kv3_centred"), at(i, s, 1, 1))
                act.activation(prob[:, :], kv[s], ACT.Square).then_inc(sem("kv3_squared"), 1)
                act.wait_ge(sem("kv3_sumsq"), at(i, s, 1, 1))
                act.activation(hm[s][:, :], hm[s][:, :], ACT.Sqrt, scale=1.0 / (HEADC - 1)).then_inc(sem("kv3_std"), 1)

            def l3_gelu(i, s):
                act.wait_ge(sem("p3_biased"), at(i, s, 1, 1))
                act.activation(tn[s][:, :, :], tn[s][:, :, :], ACT.Gelu).then_inc(sem("p3_gelu"), 1)

            def finish(i, s):
                act.wait_ge(sem("final_T"), at(i, s, 1, 1))
                released(act.activation(xo[s][:, :], pair[2][:, :], ACT.Copy), "2")
                act.drain().then_inc(sem("xo_ready"), 1)
                act.wait_ge(sem("xo_ready"), at(i, s, 1, 1))
                act.dma_start(out[i * SLOTS + s].rearrange("c h w -> c (h w)"), xo[s][:, :]).then_inc(sem(f"stored{s}"), 16)

            act.dma_start(late_sb[:, :], late_in).then_inc(sem("late_loaded"), 16)
            act.wait_ge(sem("early_loaded"), 32)
            act.wait_ge(sem("pads_zero"), 1)
            act.wait_ge(sem("seeded"), 1)
            with act.Fori(0, B // SLOTS) as i:
                for s in range(SLOTS):
                    l0(i, s)
                for s in range(SLOTS):
                    l1(i, s)
                act.wait_ge(sem("late_loaded"), 16)
                act.mul(bqs[:, :], const("bq2"), float(C) ** -0.5)
                act.drain()
                for s in range(SLOTS):
                    l2(i, s)
                for s in range(SLOTS):
                    ffn(i, s, s, "lnf2", "a")
                for s in range(SLOTS):
                    l3(i, s)
                for s in range(SLOTS):
                    l3_norm(i, s)
                for s in range(SLOTS):
                    l3_gelu(i, s)
                for s in range(SLOTS):
                    ffn(i, s, 2 + s, "lnf3", "b")
                for s in range(SLOTS):
                    finish(i, s)
                for s in range(SLOTS):
                    act.wait_ge(sem(f"stored{s}"), 16 * i + 16)

        @block.vector
        def _(dve):
            def over_tiles(row, n=NT):
                return row.rearrange("p (a b) -> p a b", a=1).to_broadcast([row.shape[0], n, row.shape[1]])

            def inner(col, n):
                return col.rearrange("p (a b) -> p a b", b=1).to_broadcast([P, col.shape[1], n])

            def gn(i, s, which):
                for h in range(2):
                    dve.bn_stats(bst[s][:, 6 * h:6 * h + 6], xc[s][:, 512 * h:512 * h + 512])
                dve.drain()
                dve.bn_aggr(mv[s][:, 0, :], bst[s][:, 0:12])
                dve.drain()
                dve.tensor_copy(gst[s][:, 0:1], mv[s][:, 0, 0:1]).then_inc(sem(which + "_stat"), 1)
                dve.wait_ge(sem(which + "_group"), at(i, s, 2, 1))
                released(dve.tensor_copy(gst[s][:, 2:3], p3["3a"][:, 0:1]), "3a")
                dve.drain()
                dve.tensor_tensor(gst[s][:, 3:4], mv[s][:, 0, 0:1], gst[s][:, 2:3], ALU.subtract)
                dve.drain()
                dve.scalar_tensor_tensor(gst[s][:, 1:2], gst[s][:, 3:4], gst[s][:, 3:4], mv[s][:, 0, 1:2],
                                         ALU.mult, ALU.add).then_inc(sem(which + "_stat"), 1)
                dve.wait_ge(sem(which + "_group"), at(i, s, 2, 2))
                released(dve.tensor_scalar(var[s][:, 0:1], p3["3a"][:, 0:1], GN_EPS, None, ALU.add), "3a")
                dve.drain().then_inc(sem(which + "_var"), 1)
                dve.wait_ge(sem(which + "_rstd"), at(i, s, 1, 1))
                dve.scalar_tensor_tensor(nmr[s][:, 0:1], gst[s][:, 2:3], -1.0, rstd[s][:, 0:1], ALU.mult, ALU.mult)
                dve.drain()
                dve.tensor_scalar(xn[s][:, :], xc[s][:, :], rstd[s][:, 0:1], nmr[s][:, 0:1], ALU.mult, ALU.add)\
                    .then_inc(sem(which + "_xn"), 1)

            def l0(i, s):
                dve.wait_ge(sem("off_ready"), at(i, s, 1, 1))
                dve.scalar_tensor_tensor(pos, pair[2][32:32 + NOFF, :], const("offb"), const("base"), ALU.add, ALU.add)
                grid = [v.rearrange("p (a b) -> p a b", a=HW) for v in (pos, pair[2][0:NOFF, :], pair[2][64:64 + NOFF, :])]
                dve.drain()
                dve.tensor_tensor(grid[0][:, :, 1:HW], grid[1][:, :, 0:HW - 1], grid[0][:, :, 1:HW], ALU.add)
                dve.drain()
                released(dve.tensor_tensor(grid[0][:, :, 0:HW - 1], grid[2][:, :, 1:HW], grid[0][:, :, 0:HW - 1], ALU.add), "2")
                dve.drain()
                dve.tensor_copy(offs[0:NOFF, :], pos)
                dve.drain()
                dve.tensor_tensor(rest, pos, offs[0:NOFF, :], ALU.subtract)
                dve.drain().then_inc(sem("offs_split"), 1)
                dve.tensor_copy(offcut[0], rest)
                dve.drain().then_inc(sem("offs_cut"), 1)
                dve.tensor_tensor(offcut[1], rest, offcut[0], ALU.subtract)
                dve.drain().then_inc(sem("offs_cut"), 1)
                for g in range(1, 3 * NT, 2):
                    c, third = divmod(g, 3)
                    dve.wait_ge(sem("z_ready"), at(i, s, 3 * NT, g + 1))
                    released(dve.tensor_copy(z[:, c, 3 * third:3 * third + 3, :],
                                             p3["3b"][:, 0:384].rearrange("p (a b) -> p a b", a=3)), "3b")
                dve.drain().then_inc(sem("z_kept"), 3 * NT // 2)
                dve.tensor_tensor(rest, pos, const("base"), ALU.subtract)
                dve.drain()
                dve.tensor_reduce(dymax[:, :], rest, AX.X, ALU.max, apply_absolute_value=True)
                dve.drain()
                dve.tensor_scalar(dymax[:, :], dymax[:, :], const("isy"), None, ALU.mult)
                dve.drain()
                dve.tensor_scalar(dyok[:, :], const("ones"), dymax[:, 0:1], float(REACH), ALU.mult, ALU.is_lt)\
                    .then_inc(sem("dy_checked"), 1)

                def x_hat(k):
                    dve.tensor_scalar(hx[k % 2], hx[k % 2], 1.0, 0.0, ALU.subtract, ALU.min)

                def y_hat(n, lo, hi):
                    dve.tensor_scalar(ay[n % RING][:, 0:hi - lo], ay[n % RING][:, 0:hi - lo], 1.0, 0.0, ALU.subtract, ALU.min)

                def product(n, k, lo, hi):
                    return dve.tensor_tensor(hat[n % RING][:, 0:hi - lo], ay[n % RING][:, 0:hi - lo], hx[k % 2][:, lo:hi],
                                             ALU.mult)

                def hats(n):
                    dve.wait_ge(sem("ay_ready"), at(i, s, len(NEAR), n + 2))
                    if n % NT == 0:
                        x_hat(NEAR[n][0])
                    for m in (n, n + 1):
                        y_hat(m, *NEAR[m][2:])

                hats(0)
                for n in range(0, len(NEAR), 2):
                    if n + 2 < len(NEAR):
                        hats(n + 2)
                    dve.drain()
                    dve.wait_ge(sem("hat_used"), at(i, s, len(NEAR), n + 2))
                    if n == len(NEAR) - 2:
                        dve.wait_ge(sem("far_known"), at(i, s, 1, 1))
                    for m in (n, n + 1):
                        k, c, lo, hi = NEAR[m]
                        product(m, k, lo, hi).then_inc(sem("hat_ready"), 1)
                    if n == 2 * NT:
                        dve.wait_ge(sem("dy_count"), at(i, s, 1, 1))
                        released(dve.tensor_scalar(isfar[s][:, :], p3["3b"][0:1, 0:1], NOFF - 0.5, None, ALU.is_lt), "3b")
                        dve.drain().then_inc(sem("far_known"), 1)
                flag = dve.value_load(isfar[s][0:1, 0:1], min_val=0, max_val=1)
                with dve.If(flag > 0):
                    dve.wait_ge(sem("hat_used"), at(i, s, len(NEAR), len(NEAR)) + RING)
                    for n, (k, c, lo, hi) in enumerate(FAR):
                        dve.wait_ge(sem("far_ay_ready"), at(i, s, len(FAR), n + 1))
                        if n == 0 or FAR[n - 1][0] != k:
                            x_hat(k)
                        y_hat(n, lo, hi)
                        dve.drain()
                        if n >= RING:
                            dve.wait_ge(sem("far_hat_used"), at(i, s, len(FAR), n - RING + 1))
                        product(n, k, lo, hi).then_inc(sem("far_hat_ready"), 1)
                with dve.Else():
                    dve.drain().then_inc(sem("far_hat_ready"), len(FAR))
                dve.wait_ge(sem("hat_used"), at(i, s, len(NEAR), len(NEAR)) + RING)
                dve.wait_ge(sem("far_hat_used"), at(i, s, len(FAR), len(FAR)))
                released(dve.scalar_tensor_tensor(xc[s][:, :], pair[0][:, :], const("b0"), xc[s][:, :], ALU.add, ALU.add), "0")
                dve.drain()

            def core(i, s, inst):
                for j in range(NT + 3):
                    if j < NT:
                        dve.wait_ge(sem("energy"), at4(i, inst, NT, j + 1))
                        dve.tensor_reduce(nmax[s][:, j:j + 1], pair[j % 2][:, :], AX.X, ALU.max, negate=True)\
                            .then_inc(sem("nmax"), 1)
                    if inst >= 2 and 1 <= j <= NT:
                        jj = j - 1
                        off = (NT - 1 - jj) * P
                        dve.wait_ge(sem("prob_exp"), at4(i, inst, NT, jj + 1))
                        dve.tensor_tensor_reduce(out=pr[jj % 2], in0=pr[jj % 2], in1=const("toep")[:, off:off + N],
                                                 scale=1.0, scalar=0.0, op0=ALU.mult, op1=ALU.add,
                                                 accum_out=rsum[s][:, jj:jj + 1])
                        dve.drain().then_inc(sem("prob_biased"), 1)
                    if j >= 3:
                        jj = j - 3
                        bank = ("3a", "3b")[jj % 2]
                        dve.wait_ge(sem("pv"), at4(i, inst, NT, jj + 1) + 2)
                        dve.reciprocal(rinv[s][:, jj:jj + 1], rsum[s][:, jj:jj + 1])
                        dve.drain()
                        if inst < 2:
                            ins = dve.tensor_scalar(tn[s][:, jj, :], p3[bank][:, 0:P], rinv[s][:, jj:jj + 1], None, ALU.mult)
                        else:
                            ins = dve.scalar_tensor_tensor(tok[s][:, jj, :], p3[bank][:, 0:P], rinv[s][:, jj:jj + 1],
                                                           tok[s][:, jj, :], ALU.mult, ALU.add)
                        released(ins, bank)
                        dve.drain().then_inc(sem("o_kept"), 1)

            def keep_v(i, s, ready, bias, done):
                dve.wait_ge(sem(ready), at(i, s, 3, 3))
                released(dve.tensor_tensor(vt[s][:, :, :], pair[2][:, :].rearrange("p (a b) -> p a b", a=NT),
                                           over_tiles(const(bias)), ALU.add), "2")
                dve.drain().then_inc(sem(done), 1)

            def l1_out(i, s):
                dve.wait_ge(sem("att1_T"), at(i, s, 1, 1))
                released(dve.tensor_tensor(xn[s][:, :], pair[2][:, :], xn[s][:, :], ALU.add), "2")
                dve.drain().then_inc(sem("y1_kept"), 1)
                dve.wait_ge(sem("tok1"), at(i, s, 1, 1))
                released(dve.tensor_tensor(tok[s][:, :, :], pair[0][:, :].rearrange("p (a b) -> p a b", a=NT),
                                           over_tiles(const("bo1")), ALU.add), "0")
                dve.drain().then_inc(sem(f"x_used{s}"), 1)

            def ln(i, s, which):
                for j in range(NT):
                    dve.bn_stats(bst[s][:, 6 * j:6 * j + 6], tok[s][:, j, :])
                dve.drain()
                for j in range(NT):
                    dve.bn_aggr(mv[s][:, j, :], bst[s][:, 6 * j:6 * j + 6])
                dve.drain()
                dve.tensor_scalar(var[s][:, :], mv[s][:, :, 1], LN_EPS, None, ALU.add).then_inc(sem(which + "_var"), 1)
                dve.wait_ge(sem(which + "_rstd"), at(i, s, 1, 1))
                dve.scalar_tensor_tensor(nmr[s][:, :], mv[s][:, :, 0], -1.0, rstd[s][:, :], ALU.mult, ALU.mult)
                dve.drain()
                for j in range(NT):
                    dve.tensor_scalar(tn[s][:, j, :], tok[s][:, j, :], rstd[s][:, j:j + 1], nmr[s][:, j:j + 1],
                                      ALU.mult, ALU.add)
                dve.drain().then_inc(sem(which + "_tn"), 1)

            def gate(i, s, inst, f):
                dve.wait_ge(sem("gate"), at4(i, inst, 1, 1))
                released(dve.tensor_tensor(lg[s][:, :, :], p3["3a"][:, 0:NT * E].rearrange("p (a b) -> p a b", a=NT),
                                           over_tiles(const("gb" + f)), ALU.add), "3a")
                dve.drain()
                dve.tensor_reduce(gmx[s][:, :], lg[s][:, :, :], AX.X, ALU.max)
                dve.drain()
                dve.tensor_tensor(lg[s][:, :, :], lg[s][:, :, :], inner(gmx[s][:, :], E), ALU.subtract)\
                    .then_inc(sem("logits"), 1)
                dve.wait_ge(sem("gate_exp"), at4(i, inst, 1, 1))
                dve.tensor_reduce(gsum[s][:, :], lg[s][:, :, :], AX.X, ALU.add)
                dve.drain()
                dve.reciprocal(gsum[s][:, :], gsum[s][:, :])
                dve.drain()
                dve.tensor_tensor(lg[s][:, :, :], lg[s][:, :, :], inner(gsum[s][:, :], E), ALU.mult)
                dve.drain()
                other = lg[s][:, :, :].rearrange("p a (o b) -> p a o b", o=1).to_broadcast([P, NT, E, E])
                own = lg[s][:, :, :].rearrange("p a (b o) -> p a b o", o=1).to_broadcast([P, NT, E, E])
                lower = const("low").rearrange("p (o b c) -> p o b c", o=1, b=E).to_broadcast([P, NT, E, E])
                dve.tensor_tensor(wins[:, :, :, :], other, own, ALU.is_gt)
                dve.tensor_tensor(ties[:, :, :, :], other, own, ALU.is_equal)
                dve.drain()
                dve.tensor_tensor(ties[:, :, :, :], ties[:, :, :, :], lower, ALU.mult)
                dve.drain()
                dve.tensor_tensor(wins[:, :, :, :], wins[:, :, :, :], ties[:, :, :, :], ALU.add)
                dve.drain()
                dve.tensor_reduce(cw[s][:, :, :], wins[:, :, :, :], AX.X, ALU.add)
                dve.drain()
                dve.scalar_tensor_tensor(cw[s][:, :, :], cw[s][:, :, :], 1.5, lg[s][:, :, :], ALU.is_lt, ALU.mult)\
                    .then_inc(sem("cw"), 1)
                dve.wait_ge(sem("cw_T"), at4(i, inst, 1, 1))
                released(dve.tensor_copy(cwT[s][:, :], p3["3b"][0:NT * E, 0:P]), "3b")
                dve.drain().then_inc(sem("cwT_kept"), 1)

            def ffn(i, s, inst, f):
                gate(i, s, inst, f)

                def take(e, q):
                    src = pair[2 + q % 2]
                    for j in range(NT):
                        ins = dve.scalar_tensor_tensor(tok[s][:, j, :], src[:, j * P:(j + 1) * P], cw[s][:, j, e:e + 1],
                                                       tok[s][:, j, :], ALU.mult, ALU.add)
                        if q % 2 and j in (NT // 2 - 1, NT - 1):
                            released(ins, "3a" if j < NT // 2 else "3b")
                    if q % 2 == 0:
                        released(ins, "2")
                    dve.drain()

                for e in range(E):
                    dve.wait_ge(sem("expert"), at4(i, inst, E, e + 1) + 2)
                    take(e, 0 if e == 0 else e + 1)
                    if e == 0:
                        dve.wait_ge(sem("bias2"), at4(i, inst, 1, 1))
                        for h, bank in enumerate(("3a", "3b")):
                            released(dve.tensor_tensor(tok[s][:, 4 * h:4 * h + 4, :],
                                                       p3[bank].rearrange("p (a b) -> p a b", a=4),
                                                       tok[s][:, 4 * h:4 * h + 4, :], ALU.add), bank)
                        dve.drain()

            def l3_norm(i, s):
                kvs = kv[s].rearrange("p (a b) -> p a b", a=NT)
                for g in range(2):
                    dve.wait_ge(sem("kv3"), at(i, s, 2, g + 1))
                    released(dve.tensor_tensor(kvs[:, 4 * g:4 * g + 4, :], pair[1 + g][:, :].rearrange("p (a b) -> p a b", a=4),
                                               over_tiles(const("bkv3"), 4), ALU.add), str(1 + g))
                dve.drain()
                heads = kv[s].rearrange("p (g d) -> p g d", d=HEADC)
                dve.tensor_reduce(hm[s][:, :], heads, AX.X, ALU.add)
                dve.drain()
                dve.tensor_scalar(hm[s][:, :], hm[s][:, :], 1.0 / HEADC, None, ALU.mult)
                dve.drain()
                dve.tensor_tensor(heads, heads, inner(hm[s][:, :], HEADC), ALU.subtract).then_inc(sem("kv3_centred"), 1)
                dve.wait_ge(sem("kv3_squared"), at(i, s, 1, 1))
                dve.tensor_reduce(hm[s][:, :], prob[:, :].rearrange("p (g d) -> p g d", d=HEADC), AX.X, ALU.add)\
                    .then_inc(sem("kv3_sumsq"), 1)
                dve.wait_ge(sem("kv3_std"), at(i, s, 1, 1))
                dve.tensor_scalar(hm[s][:, :], hm[s][:, :], HEAD_EPS, None, ALU.add)
                dve.drain()
                dve.reciprocal(hm[s][:, :], hm[s][:, :])
                dve.drain()
                dve.tensor_tensor(heads, heads, inner(hm[s][:, :], HEADC), ALU.mult)
                dve.drain()
                dve.tensor_tensor(kvs, kvs, over_tiles(const("lnw3")), ALU.mult)
                dve.drain()
                dve.tensor_tensor(kvs, kvs, over_tiles(const("lnb3")), ALU.add).then_inc(sem("kv3_normed"), 1)

            def l3_out(i, s):
                dve.wait_ge(sem("state3"), at(i, s, 1, 1))
                released(dve.tensor_tensor(kvm[s][:, :], p3["3a"][:, 0:P], const("kvmask"), ALU.mult), "3a")
                dve.drain().then_inc(sem("state3_kept"), 1)
                dve.wait_ge(sem("read3"), at(i, s, 1, 1))
                released(dve.tensor_tensor(kT[s][:, :], pair[0][:, :], tnT[s][:, :], ALU.add), "0")
                dve.drain().then_inc(sem("ret3_kept"), 1)
                dve.wait_ge(sem("tok3_res"), at(i, s, 1, 1))
                dve.wait_ge(sem("proj3"), at(i, s, 1, 1))
                released(dve.tensor_tensor(tn[s][:, :, :], pair[1][:, :].rearrange("p (a b) -> p a b", a=NT),
                                           over_tiles(const("bp3")), ALU.add), "1")
                dve.drain().then_inc(sem("p3_biased"), 1)

            def l3_add(i, s):
                dve.wait_ge(sem("p3_gelu"), at(i, s, 1, 1))
                dve.tensor_tensor(tok[s][:, :, :], tok[s][:, :, :], tn[s][:, :, :], ALU.add)
                dve.drain()

            dve.memset(offs[:, :], 0.0)
            for name, n in (("hat_ready", RING), ("hat_used", RING), ("pv", 2), ("expert", 2), ("seeded", 1),
                            *(("free" + b, 1) for b in BANKS), *((f"x_used{s}", 1) for s in range(SLOTS))):
                dve.drain().then_inc(sem(name), n)
            dve.wait_ge(sem("early_loaded"), 32)
            with dve.Fori(0, B // SLOTS) as i:
                for s in range(SLOTS):
                    dve.wait_ge(sem(f"x_loaded{s}"), i * 16 + 16)
                    gn(i, s, "gn0")
                for s in range(SLOTS):
                    l0(i, s)
                for s in range(SLOTS):
                    gn(i, s, "gn1")
                for s in range(SLOTS):
                    keep_v(i, s, "proj1", "bv1", "v1_kept")
                    core(i, s, s)
                for s in range(SLOTS):
                    l1_out(i, s)
                for s in range(SLOTS):
                    ln(i, s, "ln2")
                dve.wait_ge(sem("late_loaded"), 16)
                for s in range(SLOTS):
                    keep_v(i, s, "proj2", "bv2", "v2_kept")
                    core(i, s, 2 + s)
                    ln(i, s, "lnf2")
                for s in range(SLOTS):
                    ffn(i, s, s, "a")
                    ln(i, s, "ln3")
                for s in range(SLOTS):
                    l3_norm(i, s)
                for s in range(SLOTS):
                    l3_out(i, s)
                for s in range(SLOTS):
                    l3_add(i, s)
                    ln(i, s, "lnf3")
                for s in range(SLOTS):
                    ffn(i, s, 2 + s, "b")
                    dve.drain().then_inc(sem("tok_final"), 1)


def packed(part, arrays, np):
    cols, n = columns(part)
    out = np.zeros((P, n), np.float32)
    for name, (at, p, width) in cols.items():
        out[0:p, at:at + width] = arrays[name]
    return out


def kernel(**inputs):
    import ml_dtypes
    import numpy as np
    import concourse.bacc as bacc
    from concourse.bass_utils import run_bass_kernel_spmd

    w = {k: np.asarray(v) for k, v in inputs.items()}
    f = np.float32

    def rows(v):
        return np.broadcast_to(v.reshape(1, -1), (P, v.size))

    p, n = np.arange(P), np.arange(N)
    tap = np.arange(TAPS)
    base = np.stack([n // HW + (tap // 3)[:, None] - 1, n % HW + (tap % 3)[:, None] - 1], 1).reshape(NOFF, N)
    gap = np.abs(np.arange(TOEP)[None, :] - (NT - 1) * P - p[:, None]).astype(np.float64)
    decay = (gap + 1e-9) ** (0.1 - 1.5)
    toep = decay / 1e-9 ** (0.1 - 1.5) + 1e-9
    toep = np.where(gap == 0, 1.0 + 1e-9, toep)
    head = p // HEADC
    a = dict(ident=np.eye(P), grp=(p[:, None] // 4 == p // 4) / 4.0, kvmask=(head[:, None] == head) / float(N),
             base=base, yneg=-(ROWS * np.arange(NT)[None, :] + p[:, None] // HW), xneg=-(p[:, None] % HW), toep=toep,
             low=rows((np.arange(E)[None, :] < np.arange(E)[:, None]).astype(f)))
    offw = np.zeros((C, 3, 3, 32), f)
    offw[..., 0:NOFF] = w["L0_conv_offset_w"].transpose(1, 2, 3, 0)
    a.update(offw=offw.reshape(C, -1), isy=(np.arange(NOFF)[:, None] + 1) % 2, ones=np.ones((NOFF, P)), offb=w["L0_conv_offset_b"][:, None],
             w0=w["L0_conv_weight"].transpose(1, 2, 3, 0).reshape(C, -1), b0=w["L0_conv_bias"][:, None],
             wq1=w["L1_conv_Wq"].T, wk1=w["L1_conv_Wk"].T, bq1=w["L1_conv_bq"][:, None], bk1=w["L1_conv_bk"][:, None],
             wv1=w["L1_conv_Wv"].T, bv1=rows(w["L1_conv_bv"]), wo1=w["L1_conv_Wo"].T, bo1=rows(w["L1_conv_bo"]))
    a.update(wq2=w["L2_attn_Wq"].T, wk2=w["L2_attn_Wk"].T, bq2=w["L2_attn_bq"][:, None], bk2=w["L2_attn_bk"][:, None],
             wv2=w["L2_attn_Wv"].T, bv2=rows(w["L2_attn_bv"]))
    wqkv = w["L3_attn_W_qkv"].reshape(C // HEADC, 3, HEADC, C).transpose(1, 3, 0, 2).reshape(3, C, C)
    bqkv = w["L3_attn_b_qkv"].reshape(C // HEADC, 3, HEADC).transpose(1, 0, 2).reshape(3, C)
    a.update(wq3=wqkv[0], bq3=bqkv[0][:, None], wkv3=np.concatenate([wqkv[1], wqkv[2]], 1), bkv3=rows(bqkv[1:]),
             lnw3=rows(np.concatenate([w["L3_attn_kln_w"].reshape(-1), w["L3_attn_vln_w"].reshape(-1)])),
             lnb3=rows(np.concatenate([w["L3_attn_kln_b"].reshape(-1), w["L3_attn_vln_b"].reshape(-1)])),
             wp3=w["L3_attn_W_proj"].T, bp3=rows(w["L3_attn_b_proj"]))
    for name, layer in (("a", "L2_ffn_"), ("b", "L3_ffn_")):
        b2 = np.zeros((NT * E, NT * C), f)
        for j in range(NT):
            b2[j * E:(j + 1) * E, j * C:(j + 1) * C] = w[layer + "b2"]
        a["gw" + name] = w[layer + "gate_w"]
        a["gb" + name] = rows(w[layer + "gate_b"])
        a["w1" + name] = w[layer + "W1"].transpose(1, 0, 2).reshape(C, -1)
        a["b1" + name] = w[layer + "b1"].reshape(E * HC, P).T
        a["w2" + name] = w[layer + "W2"].reshape(E * HC, P, C).transpose(1, 0, 2).reshape(P, -1)
        a["b2" + name] = b2
    early, late = layout()
    sel = np.zeros((96, NOFF, P), ml_dtypes.bfloat16)
    for q in range(3):
        for r in range(NOFF):
            sel[32 * q + r, r, :] = 1
    arrays = dict(x=np.ascontiguousarray(w["x"]), sel=sel.reshape(96, -1), early=packed(early, a, np), late=packed(late, a, np))

    nc = bacc.Bacc("TRN2", target_bir_lowering=False, num_devices=1)
    args = [nc.dram_tensor(k, v.shape, mybir.dt.from_np(v.dtype), kind="ExternalInput").ap() for k, v in arrays.items()]
    result = nc.dram_tensor("result", (B, C, HW, HW), F32, kind="ExternalOutput").ap()
    build(nc, *args, result)
    r = run_bass_kernel_spmd(nc, [arrays], core_ids=[0])
    return r.results[0]["result"]
```

```python
from contextlib import ExitStack

import concourse.bass as bass
from concourse import mybir

F32 = mybir.dt.float32
F32R = mybir.dt.float32r
BF16 = mybir.dt.bfloat16
ALU = mybir.AluOpType
ACT = mybir.ActivationFunctionType
AX = mybir.AxisListType

P = 128
B = 8
HW = 32
N = HW * HW
NT = N // P
C = 128
TAPS = 9
NOFF = 2 * TAPS
D1 = C // 8
E = 8
HID = 256
HC = HID // P
HEADC = 8
SLOTS = 2
ROWS = P // HW
GN_EPS, LN_EPS, HEAD_EPS = 1e-5, 1e-5, 1e-5
TOEP = N + (NT - 1) * P
REACH = 2
WIDE = 256


def near_pieces(k):
    ky = k // 3
    return [(c, HW * max(0, ROWS * c + 1 - REACH - ky), HW * min(HW, ROWS * (c + 1) + 1 + REACH - ky))
            for c in range(NT)]


def far_pieces(k):
    out = []
    for c, lo, hi in near_pieces(k):
        for a, b in ((0, lo), (hi, N)):
            while a < b:
                out.append((c, a, min(b, a + WIDE)))
                a += WIDE
    return out


NEAR = [(k, *p) for k in range(TAPS) for p in near_pieces(k)]
FAR = [(k, *p) for k in range(TAPS) for p in far_pieces(k)]
RING = 8
SPREAD_X, SPREAD_Y = 5, 1
BODIES = B // SLOTS
STEPS = 17


def paced(steps, **pauses):
    out = []
    for step in range(steps):
        out += [None] * pauses.get(f"s{step}", 0) + [step]
    return out


START_PLACES = dict(
    pe={1: 4, 3: 9, 7: 15, 8: 17, 15: 30},
    dve={0: 1, 2: 7, 4: 12, 6: 14, 8: 19, 9: 21, 10: 23, 11: 25, 13: 28, 16: 34},
    act={12: 30, 13: 31}, pool={5: 12})
MID0_PLACES = dict(
    pe={1: 3, 3: 8, 7: 15, 11: 16, 15: 22, 19: 23, 23: 28, 25: 29},
    dve={0: 0, 2: 6, 4: 11, 6: 13, 12: 21, 16: 22, 20: 27, 24: 32, 26: 33},
    act={10: 20, 14: 21, 18: 27, 22: 28}, pool={5: 11})
MID0_ATTENTION_PACE = paced(27, s1=1, s3=2, s7=3)
MID1_PACE = paced(27, s10=1, s11=5)
GATING_ATTENTION_PACE = paced(18, s2=2, s3=5, s12=5, s14=1)
GATING_EXPERTS_PACE = paced(18, s0=2, s2=3, s3=7, s10=2, s12=6, s14=2)
BETWEEN_PACE = paced(48, s3=1, s18=1, s20=5, s33=3, s42=2)
NEXT_START_PACE = [None] * 6 + paced(17, s1=2, s3=2, s7=4, s15=6)


def placed(places):
    at = {n: step for step, n in places.items()}
    return [at.get(n) for n in range(max(at) + 1)]


def woven(work, pace):
    def side(i, n):
        if n < len(pace) and pace[n] is not None:
            work(i, pace[n])
    return side


def layout():
    early = dict(grp=(P, P), base=(NOFF, N), offw=(C, 3 * 96), offb=(NOFF, 1), isy=(NOFF, 1), ones=(NOFF, P),
                 ident=(P, P), kvmask=(P, P), yneg=(P, NT), xneg=(P, 1), w0=(C, TAPS * C), b0=(C, 1),
                 wq1=(C, P), wk1=(C, P), bq1=(P, 1), bk1=(P, 1), wv1=(C, C), bv1=(P, C), wo1=(C, C), bo1=(P, C),
                 wkv3=(C, 2 * C), bkv3=(P, 2 * C))
    late = dict(wq2=(C, C), wk2=(C, C), bq2=(C, 1), bk2=(C, 1), wv2=(C, C), bv2=(P, C), toep=(P, TOEP),
                low=(P, E * E),
                wq3=(C, C), bq3=(C, 1), lnw3=(P, 2 * C), lnb3=(P, 2 * C),
                wp3=(C, C), bp3=(P, C))
    for f in "ab":
        late.update({"gw" + f: (C, E), "gb" + f: (P, E), "w1" + f: (C, E * HID), "b1" + f: (P, E * HC),
                     "w2" + f: (P, E * HC * C), "b2" + f: (NT * E, NT * C)})
    return early, late


def columns(part):
    at, out = 0, {}
    for name, (p, n) in part.items():
        out[name] = (at, p, n)
        at += n
    return out, at


def build(nc, x, sel_in, early_in, late_in, out):
    early, late = layout()
    ecols, en = columns(early)
    lcols, ln = columns(late)
    with ExitStack() as ctx:
        def sb(name, shape, dt=F32):
            return ctx.enter_context(nc.sbuf_tensor(name, shape, dt))

        sems = {}

        def sem(name):
            if name not in sems:
                sems[name] = ctx.enter_context(nc.semaphore(name))
            return sems[name]

        early_sb, late_sb = sb("early_sb", [P, en]), sb("late_sb", [P, ln])

        def const(name):
            tile, cols = (early_sb, ecols) if name in ecols else (late_sb, lcols)
            at, p, n = cols[name]
            return tile[0:p, at:at + n]

        ident, grp = const("ident"), const("grp")
        start_cols = ecols["ident"][0]
        sel = sb("sel_sb", [96, NOFF * P], BF16)
        xc = [sb(f"xc{s}", [P, N]) for s in range(SLOTS)]
        tok = [xc[s][:, :].rearrange("p (a b) -> p a b", a=NT) for s in range(SLOTS)]
        xrows = [sb(f"xrows{s}", [P, N + 2 * HW]) for s in range(SLOTS)]
        xrows_end = nc.sbuf_base
        xn = [xrows[s][:, HW:HW + N] for s in range(SLOTS)]
        tn = [sb(f"tn{s}", [P, NT, C]) for s in range(SLOTS)]
        tnT = [sb(f"tnT{s}", [P, N]) for s in range(SLOTS)]
        qT = [sb(f"qT{s}", [P, N]) for s in range(SLOTS)]
        kT = [sb(f"kT{s}", [P, N]) for s in range(SLOTS)]
        qkT_end = nc.sbuf_base
        q1, k1 = ([nc.alloc_sbuf_tensor_at(f"{name}{s}", [P, N], F32R, offset=qkT_end - 4 * N * (2 * SLOTS - SLOTS * n - s))
                   for s in range(SLOTS)] for n, name in enumerate(("q1_", "k1_")))
        ximg = [k[:, :] for k in kT]
        vt = [sb(f"vt{s}", [P, NT, C]) for s in range(SLOTS)]
        vt_end = nc.sbuf_base
        tn_high = [nc.alloc_sbuf_tensor_at(f"tn_high{s}", [P, N], F32R, offset=vt_end - 4 * N * (SLOTS - s))
                   for s in range(SLOTS)]
        tn_low = [nc.alloc_sbuf_tensor_at(f"tn_low{s}", [P, N], F32R,
                                          offset=xrows_end - 4 * (N + 2 * HW) * (SLOTS - s) + 4 * HW)
                  for s in range(SLOTS)]
        hx = [tn[s][:].rearrange("p a b -> p (a b)") for s in range(SLOTS)]
        offs = [sb(f"offs{s}", [96, N], BF16) for s in range(SLOTS)]
        big = sb("big", [P, NT * TAPS * C])
        w1_split = nc.alloc_sbuf_tensor_at("w1_split", [P, 4 * HID], F32R, offset=nc.sbuf_base - 4 * 4 * HID)
        z = big[:, :].rearrange("p (c k o) -> p c k o", c=NT, k=TAPS)
        kv = [big[:, 2 * N * s:2 * N * (s + 1)] for s in range(SLOTS)]
        hid = [big[:, (4 + r) * N:(5 + r) * N] for r in range(4)]
        prob = sb("prob", [P, 3 * N])
        pr = [prob[:, r * N:(r + 1) * N] for r in range(3)]
        pos, rest = prob[0:NOFF, 0:N], prob[0:NOFF, N:2 * N]
        dist = sb("dist", [P, 2 * RING * WIDE])
        ay = [dist[:, r * WIDE:(r + 1) * WIDE] for r in range(RING)]
        hat = [dist[:, (RING + r) * WIDE:(RING + r + 1) * WIDE] for r in range(RING)]
        offcut = [[tnT[s][0:NOFF, n * N // 2:(n + 1) * N // 2].bitcast(BF16) for n in range(2)] for s in range(SLOTS)]
        dymax = sb("dymax", [NOFF, 1])
        dyok = sb("dyok", [NOFF, P])
        isfar = [sb(f"isfar{s}", [1, 1], mybir.dt.int32) for s in range(SLOTS)]
        prT = [dist[:, r * N:(r + 1) * N].rearrange("p (a b) -> p a b", a=NT) for r in range(2)]
        mhalf = sb("mhalf", [P, NT])
        zero = sb("zero", [P, 1])
        bst = [sb(f"bst{s}", [P, NT * 6]) for s in range(SLOTS)]
        mv = [sb(f"mv{s}", [P, NT, 2]) for s in range(SLOTS)]
        gst = [sb(f"gst{s}", [P, 4]) for s in range(SLOTS)]
        var = [sb(f"var{s}", [P, NT]) for s in range(SLOTS)]
        rstd = [sb(f"rstd{s}", [P, NT]) for s in range(SLOTS)]
        nmr = [sb(f"nmr{s}", [P, NT]) for s in range(SLOTS)]
        nmax = [sb(f"nmax{s}", [P, NT]) for s in range(SLOTS)]
        rsum = [sb(f"rsum{s}", [P, NT]) for s in range(SLOTS)]
        rinv = [sb(f"rinv{s}", [P, NT]) for s in range(SLOTS)]
        lg = [sb(f"lg{s}", [P, NT, E]) for s in range(SLOTS)]
        gmx = [sb(f"gmx{s}", [P, NT]) for s in range(SLOTS)]
        gsum = [sb(f"gsum{s}", [P, NT]) for s in range(SLOTS)]
        cw = [sb(f"cw{s}", [P, NT, E]) for s in range(SLOTS)]
        cwT = [sb(f"cwT{s}", [NT * E, P]) for s in range(SLOTS)]
        bqs = sb("bqs", [P, 1])
        hm = [dist[:, (2 * RING - 4 + s) * WIDE:(2 * RING - 3 + s) * WIDE] for s in range(SLOTS)]
        kvm = [dist[:, (2 * RING - 2 + s) * WIDE:(2 * RING - 2 + s) * WIDE + P] for s in range(SLOTS)]
        xo = [q[:, :] for q in qT]

        pair = [ctx.enter_context(nc.psum_tensor(f"pair{i}", [P, N], F32)) for i in range(4)]
        BANKS = ("0", "1", "2", "3a", "3b")
        p3 = {"3a": pair[3][:, 0:512], "3b": pair[3][:, 512:1024]}

        def released(ins, bank):
            return ins.then_inc(sem("free" + bank), 1)

        def qk1_full(s, n):
            place = (vt[s][:, :, :].rearrange("p a b -> p (a b)"), tnT[s][:, :])[n // 2]
            return place[:, 512 * (n % 2):512 * (n % 2) + 512]

        def mid0_bank(s, n):
            return ("3a", "3b")[n % 2] if s == 0 else "3b"

        def at(i, s, k, c):
            return i * (SLOTS * k) + (s * k + c)

        def at4(i, inst, k, c):
            return i * (4 * k) + (inst * k + c)

        UNITS = E * HC
        block = ctx.enter_context(nc.Block())

        @block.sync
        def _(sp):
            sp.dma_start(early_sb[:, 0:start_cols], early_in[:, 0:start_cols]).then_inc(sem("start_loaded"), 16)
            with sp.Fori(0, BODIES) as i:
                for s in range(SLOTS):
                    sp.wait_ge(sem(f"ximg_free{s}"), i + 1)
                    sp.dma_start(ximg[s][:, :], x[i * SLOTS + s].rearrange("c h w -> c (h w)"))\
                        .then_inc(sem(f"x_loaded{s}"), 16)

        @block.gpsimd
        def _(pool):
            pool.memset(mhalf[:, :], -0.5).then_inc(sem("mhalf_set"), 1)
            pool.memset(zero[:, :], 0.0)
            for s in range(SLOTS):
                pool.memset(xrows[s][:, :], 0.0)
            pool.drain().then_inc(sem("pads_zero"), 1)
            pool.wait_ge(sem("mhalf_set"), 1)

            def rsqrt(i, s, which, width):
                pool.wait_ge(sem(which + "_var"), at(i, s, 1, 1))
                pool.tensor_tensor(rstd[s][:, 0:width], var[s][:, 0:width], mhalf[:, 0:width],
                                   ALU.pow).then_inc(sem(which + "_rstd"), 1)

            def sampling(i, s, side):
                for n in range(1, len(NEAR), 2):
                    k, c, lo, hi = NEAR[n]
                    pool.wait_ge(sem("y_hats"), at(i, s, len(NEAR) // 2, n // 2 + 1))
                    pool.wait_ge(sem("hat_used"), at(i, s, len(NEAR), n + 1))
                    pool.tensor_tensor(hat[n % RING][:, 0:hi - lo], ay[n % RING][:, 0:hi - lo], hx[k % 2][:, lo:hi],
                                       ALU.mult).then_inc(sem("odd_hat_ready"), 1)
                    side(i, n // 2)

            def start(i, s, step):
                if step == 5:
                    rsqrt(i, s, "gn0", 1)

            def mid0(i, s, step):
                if step == 5:
                    rsqrt(i, s, "gn1", 1)

            def gating(i, s, which, step):
                if step == 1:
                    rsqrt(i, s, which, NT)

            def between1(i, s, step):
                if step == 1:
                    rsqrt(i, s, "ln3", NT)
                elif step == 4:
                    pool.wait_ge(sem("ln3_tn"), at(i, s, 1, 1))
                    pool.tensor_tensor(tok[s][:, :, :], tok[s][:, :, :], tn[s][:, :, :],
                                       ALU.add).then_inc(sem("tok3_res"), 1)
                elif step >= 30:
                    gating(i, s, "lnf3", step - 30)

            def experts(i, inst, f, side):
                def split(e):
                    high, low = (w1_split[:, 2 * HID * (e % 2) + HID * r:2 * HID * (e % 2) + HID * (r + 1)] for r in range(2))
                    w = const("w1" + f)[:, e * HID:(e + 1) * HID]
                    pool.tensor_tensor(high, w, zero[:, 0:1].to_broadcast([P, HID]), ALU.add)
                    pool.drain()
                    pool.tensor_tensor(low, w, high.bitcast(F32), ALU.subtract)
                    pool.drain().then_inc(sem("w1_split"), 1)

                for e in range(2):
                    split(e)
                for e in range(E):
                    pool.wait_ge(sem("hidden"), at4(i, inst, UNITS, HC * (e + 1)))
                    if e + 2 < E:
                        split(e + 2)
                    for n in range(8):
                        side(i, 8 * e + n)

            def body(i, more):
                sampling(i, 0, woven(lambda i, n: start(i, 1, n), placed(START_PLACES["pool"])))
                sampling(i, 1, woven(lambda i, n: mid0(i, 0, n), placed(MID0_PLACES["pool"])))
                rsqrt(i, 1, "gn1", 1)
                for s in range(SLOTS):
                    rsqrt(i, s, "ln2", NT)
                rsqrt(i, 0, "lnf2", NT)
                pool.wait_ge(sem("late_loaded"), 16)
                experts(i, 0, "a", woven(lambda i, n: gating(i, 1, "lnf2", n), GATING_EXPERTS_PACE))
                experts(i, 1, "a", woven(lambda i, n: between1(i, 0, n), BETWEEN_PACE))
                experts(i, 2, "b", woven(lambda i, n: between1(i, 1, n), BETWEEN_PACE))
                experts(i, 3, "b", woven(lambda i, n: start(i + 1, 0, n), NEXT_START_PACE if more else []))

            rsqrt(0, 0, "gn0", 1)
            with pool.Fori(0, BODIES - 1) as i:
                body(i, True)
            body(BODIES - 1, False)

        @block.tensor
        def _(pe):
            uses = dict.fromkeys(BANKS, 0)
            totals = {"0": 50, "1": 66, "2": 82, "3a": 79, "3b": 105}
            now = [0]

            def claim(bank):
                uses[bank] += 1
                pe.wait_ge(sem("free" + bank), now[0] * totals[bank] + uses[bank])

            def group(i, s, which, c):
                pe.wait_ge(sem(which + "_stat"), at(i, s, 2, c + 1))
                claim("3b")
                pe.matmul(p3["3b"][:, 0:1], grp, gst[s][:, c:c + 1], start=True, stop=True)\
                    .then_inc(sem(which + "_group"), 1)

            def half_product(i, bank, w, src, h, m, done):
                claim(bank)
                pe.matmul(p3[bank][0:m, :], w, src[:, h * 512:(h + 1) * 512], start=True, stop=True)\
                    .then_inc(sem(done), 1)

            def half_tiles(i, bank, src, w, h, done):
                claim(bank)
                for j in range(4):
                    t0 = (4 * h + j) * P
                    last = pe.matmul(p3[bank][:, j * P:(j + 1) * P], src[:, t0:t0 + P], w, start=True, stop=True)
                last.then_inc(sem(done), 1)

            def half_T(i, bank, src, h, done):
                claim(bank)
                for j in range(4):
                    last = pe.transpose(p3[bank][:, j * P:(j + 1) * P], src[:, 4 * h + j, :], ident)
                last.then_inc(sem(done), 1)

            def start(i, s, step):
                if step in (1, 3):
                    group(i, s, "gn0", step // 2)
                elif step in (7, 8):
                    h = step - 7
                    if h == 0:
                        pe.wait_ge(sem("gn0_xn"), at(i, s, 1, 1))
                    bank = ("3a", "3b")[h]
                    claim(bank)
                    for ky in range(3):
                        last = pe.matmul(p3[bank][0:96, :], const("offw")[:, ky * 96:(ky + 1) * 96],
                                         xrows[s][:, HW * ky + 512 * h:HW * ky + 512 * h + 512],
                                         start=(ky == 0), stop=(ky == 2))
                    last.then_inc(sem("off_ready"), 1)
                elif step == 15:
                    pe.wait_ge(sem("dy_checked"), at(i, s, 1, 1))
                    claim("3a")
                    pe.matmul(p3["3a"][:, 0:1], dyok[:, :], const("ones")[:, 0:1], start=True, stop=True)\
                        .then_inc(sem("dy_count"), 1)

            def mid0(i, s, step):
                if step in (1, 3):
                    group(i, s, "gn1", step // 2)
                elif step in (7, 11, 15, 19):
                    n = (step - 7) // 4
                    if n == 0:
                        pe.wait_ge(sem("gn1_xn"), at(i, s, 1, 1))
                    half_product(i, mid0_bank(s, n), const(("wq1", "wk1")[n // 2]), xn[s], n % 2, P, "proj1")
                elif step in (23, 25):
                    h = (step - 23) // 2
                    half_tiles(i, mid0_bank(s, h), xn[s], const("wv1"), h, "v1")

            def mid1(i, s, step):
                if step in (0, 2):
                    if step == 0:
                        pe.wait_ge(sem("o_kept"), at4(i, s, NT, NT))
                    half_T(i, "3b", tn[s], step // 2, "att1_T")
                elif step in (4, 6):
                    h = (step - 4) // 2
                    pe.wait_ge(sem("y1_kept"), at(i, s, 2, h + 1))
                    claim("3b")
                    for j in range(4):
                        t0 = (4 * h + j) * P
                        pe.matmul(p3["3b"][:, j * P:(j + 1) * P], xn[s][:, t0:t0 + P], const("wo1"), start=True, stop=False)
                        last = pe.matmul(p3["3b"][:, j * P:(j + 1) * P], xc[s][:, t0:t0 + P], ident, start=False, stop=True)
                    last.then_inc(sem("tok1"), 1)
                elif step in (11, 13):
                    if step == 11:
                        pe.wait_ge(sem("ln2_tn"), at(i, s, 1, 1))
                    half_T(i, "3b", tn[s], (step - 11) // 2, "ln2_T")
                elif step in (15, 17, 19, 21):
                    n = (step - 15) // 2
                    if n == 0:
                        pe.wait_ge(sem("ln2_tnT"), at(i, s, 2, 2))
                    half_product(i, "3b", const(("wq2", "wk2")[n // 2]), tnT[s], n % 2, C, "proj2")
                elif step in (23, 25):
                    half_tiles(i, "3b", tnT[s], const("wv2"), (step - 23) // 2, "v2")

            def gating(i, s, inst, which, f, step):
                if step in (3, 5):
                    if step == 3:
                        pe.wait_ge(sem(which + "_tn"), at(i, s, 1, 1))
                    half_T(i, "3b", tn[s], (step - 3) // 2, which + "_T")
                elif step == 7:
                    pe.wait_ge(sem(which + "_tnT"), at(i, s, 2, 2))
                    claim("3b")
                    for j in range(NT):
                        last = pe.matmul(p3["3b"][:, j * E:(j + 1) * E], tnT[s][:, j * P:(j + 1) * P], const("gw" + f),
                                         start=True, stop=True)
                    last.then_inc(sem("gate"), 1)
                elif step == 12:
                    pe.wait_ge(sem("cw"), at4(i, inst, 1, 1))
                    claim("3b")
                    pe.matmul(p3["3b"][0:NT * E, 0:P], cw[s][:, :, :].rearrange("p a b -> p (a b)"), ident,
                              start=True, stop=True).then_inc(sem("cw_T"), 1)
                elif step in (14, 16):
                    h = (step - 14) // 2
                    pe.wait_ge(sem("cwT_kept"), at4(i, inst, 1, 1))
                    claim("3b")
                    for j in range(4):
                        c0 = (4 * h + j) * C
                        last = pe.matmul(p3["3b"][:, j * P:(j + 1) * P], cwT[s][:, :], const("b2" + f)[:, c0:c0 + C],
                                         start=True, stop=True)
                    last.then_inc(sem("bias2"), 1)

            def layer3(i, s, step):
                if step in (3, 5):
                    if step == 3:
                        pe.wait_ge(sem("ln3_tn"), at(i, s, 1, 1))
                    half_T(i, ("3a", "3b")[step // 4], tn[s], (step - 3) // 2, "ln3_T")
                elif step in (7, 9):
                    if step == 7:
                        pe.wait_ge(sem("ln3_tnT"), at(i, s, 2, 2))
                    half_product(i, "3a", const("wq3"), tnT[s], (step - 7) // 2, C, "q3")
                elif step in (8, 10, 11, 12):
                    g = {8: 0, 10: 1, 11: 2, 12: 3}[step]
                    bank = ("3b", "3b", "3a", "3b")[g]
                    claim(bank)
                    for j in range(2):
                        t0 = (2 * g + j) * P
                        last = pe.matmul(p3[bank][:, j * 256:(j + 1) * 256], tnT[s][:, t0:t0 + P], const("wkv3"),
                                         start=True, stop=True)
                    last.then_inc(sem("kv3"), 1)
                elif step == 20:
                    kvs = kv[s].rearrange("p (a b) -> p a b", a=NT)
                    pe.wait_ge(sem("kv3_normed"), at(i, s, 1, 1))
                    claim("3a")
                    for j in range(NT):
                        last = pe.matmul(p3["3a"][:, 0:P], kvs[:, j, 0:C], kvs[:, j, C:2 * C],
                                         start=(j == 0), stop=(j == NT - 1))
                    last.then_inc(sem("state3"), 1)
                elif step in (22, 23):
                    if step == 22:
                        pe.wait_ge(sem("state3_kept"), at(i, s, 1, 1))
                        pe.wait_ge(sem("q3_kept"), at(i, s, 2, 2))
                    half_product(i, ("3a", "3b")[step - 22], kvm[s][:, :], qT[s], step - 22, P, "read3")
                elif step in (25, 26):
                    h = step - 25
                    pe.wait_ge(sem("ret3_kept"), at(i, s, 2, h + 1))
                    half_tiles(i, ("3a", "3b")[h], kT[s], const("wp3"), h, "proj3")

            def between1(i, s, step):
                if step < 30:
                    layer3(i, s, step)
                else:
                    gating(i, s, 2 + s, "lnf3", "b", step - 30)

            def finish(i, s, step):
                if step in (0, 1):
                    if step == 0:
                        pe.wait_ge(sem("tok_final"), at(i, s, 1, 1))
                    half_T(i, ("3a", "3b")[step], tok[s], step, "final_T")

            def chunks(i, s):
                for g in range(3 * NT):
                    c, third = divmod(g, 3)
                    bank = ("3a", "3b")[g % 2]
                    claim(bank)
                    pe.matmul(p3[bank][:, 0:384], xn[s][:, c * P:(c + 1) * P],
                              const("w0")[:, third * 384:(third + 1) * 384], start=True, stop=True)\
                        .then_inc(sem("z_ready"), 1)

            def sampling(i, s, side):
                pe.wait_ge(sem("offs_split"), at(i, s, 3, 3))

                def spread(k, bank):
                    claim(str(bank))
                    spread_row(bank, 2 * k + 2 - bank).then_inc(sem("spread"), 1)

                def spread_far(k):
                    for bank, r in ((1, 2 * k + 1), (2, 2 * k)):
                        if k:
                            pe.wait_ge(sem(f"far_free{bank}"), at(i, s, TAPS, k))
                        spread_row(bank, r).then_inc(sem("far_spread"), 1)

                def spread_row(bank, r):
                    for h in range(2):
                        last = pe.matmul(pair[bank][:, h * 512:(h + 1) * 512], sel[:, r * P:(r + 1) * P],
                                         offs[s][:, h * 512:(h + 1) * 512], start=True, stop=True)
                    return last

                def sample(n, k, c, lo, hi, who, opened, final):
                    for a, b in ((lo, min(hi, 512)), (max(lo, 512), hi)):
                        if a < b:
                            bank = a // 512
                            last = pe.matmul(pair[0][:, a:b], z[:, c, k, :], hat[n % RING][:, a - lo:b - lo],
                                             start=bank not in opened, stop=final, skip_group_check=True)
                            opened.add(bank)
                    last.then_inc(sem(who + "hat_used"), 1)

                spread(0, 1)
                spread(0, 2)
                claim("0")
                pe.wait_ge(sem("z_kept"), at(i, s, 3 * NT, 3 * NT))
                opened = set()
                for n, (k, c, lo, hi) in enumerate(NEAR):
                    if n == 0:
                        spread(1, 1)
                    if n % NT == SPREAD_Y and k + 1 < TAPS:
                        spread(k + 1, 2)
                    if n % NT == SPREAD_X and k + 2 < TAPS:
                        spread(k + 2, 1)
                    if n % 2 == 0:
                        pe.wait_ge(sem("even_hat_ready"), at(i, s, len(NEAR) // 2, n // 2 + 1) + RING // 2)
                        pe.wait_ge(sem("odd_hat_ready"), at(i, s, len(NEAR) // 2, n // 2 + 1) + RING // 2)
                    if n == len(NEAR) - 1:
                        pe.wait_ge(sem("far_known"), at(i, s, 1, 1))
                    sample(n, k, c, lo, hi, "", opened, k == TAPS - 1)
                    if n % 2:
                        side(i, n // 2)
                flag = pe.value_load(isfar[s][0:1, 0:1], min_val=0, max_val=1)
                with pe.If(flag > 0):
                    first = {k: min(n for n, p in enumerate(FAR) if p[0] == k) for k in range(TAPS)}
                    for n, (k, c, lo, hi) in enumerate(FAR):
                        if n == 0:
                            for bank in (1, 2):
                                pe.wait_ge(sem(f"free{bank}"), now[0] * totals[str(bank)] + uses[str(bank)] + 1)
                            spread_far(0)
                        if k + 1 < TAPS and n == first[k + 1] - RING:
                            spread_far(k + 1)
                        pe.wait_ge(sem("far_hat_ready"), at(i, s, len(FAR), n + 1))
                        sample(n, k, c, lo, hi, "far_", opened, True)
                with pe.Else():
                    pe.drain().then_inc(sem("far_spread"), 2 * TAPS)
                    pe.drain().then_inc(sem("far_hat_used"), len(FAR))

            def attention(i, s, inst, queries, keys, side):
                if inst < 2:
                    pe.wait_ge(sem("qk1_kept"), at(i, s, 4, 4))
                    pe.wait_ge(sem("v1_kept"), at(i, s, 2, 2))
                else:
                    pe.wait_ge(sem("qk2_kept"), at(i, s, 4, 4))
                    pe.wait_ge(sem("v2_kept"), at(i, s, 2, 2))
                for j in range(NT + 3):
                    if j < NT:
                        claim(str(j % 2))
                        for h in range(2):
                            last = pe.matmul(pair[j % 2][:, h * 512:(h + 1) * 512], queries[s][:, j * P:(j + 1) * P],
                                             keys[s][:, h * 512:(h + 1) * 512], start=True, stop=True)
                        last.then_inc(sem("energy"), 1)
                    side(i, 3 * j)
                    if 2 <= j < NT + 2:
                        jj = j - 2
                        if inst < 2:
                            pe.wait_ge(sem("prob_exp"), at4(i, inst, NT, jj + 1))
                        else:
                            pe.wait_ge(sem("prob_biased"), at(i, s, NT, jj + 1))
                        claim("2")
                        for m in range(NT):
                            last = pe.transpose(pair[2][:, m * P:(m + 1) * P], pr[jj % 3][:, m * P:(m + 1) * P], ident)
                        last.then_inc(sem("prob_T"), 1)
                    side(i, 3 * j + 1)
                    if j >= 3:
                        jj = j - 3
                        pe.wait_ge(sem("probT_kept"), at4(i, inst, NT, jj + 1))
                        claim("3a")
                        for m in range(NT):
                            last = pe.matmul(p3["3a"][:, 0:P], prT[jj % 2][:, m, :], vt[s][:, m, :],
                                             start=(m == 0), stop=(m == NT - 1))
                        last.then_inc(sem("pv"), 1)
                    side(i, 3 * j + 2)

            def experts(i, s, inst, which, f, side):
                pe.wait_ge(sem(which + "_tn_split"), at(i, s, 2, 2))

                def hidden(u, h):
                    e, part = divmod(u, HC)
                    if h == 0:
                        if part == 0:
                            pe.wait_ge(sem("w1_split"), at4(i, inst, E, e + 1))
                        claim(str(u % 2))
                    w0 = 2 * HID * (e % 2) + part * P
                    w_high, w_low = w1_split[:, w0:w0 + P], w1_split[:, w0 + HID:w0 + HID + P]
                    cols = slice(h * 512, (h + 1) * 512)
                    pe.matmul(pair[u % 2][:, cols], w_high, tn_high[s][:, cols], start=True, stop=False)
                    pe.matmul(pair[u % 2][:, cols], w_high, tn_low[s][:, cols], start=False, stop=False)
                    last = pe.matmul(pair[u % 2][:, cols], w_low, tn_high[s][:, cols], start=False, stop=True)
                    if h:
                        last.then_inc(sem("hidden"), 1)

                for u in range(HC):
                    for h in range(2):
                        hidden(u, h)
                for e in range(E):
                    for n in range(4):
                        if e + 1 < E:
                            hidden(HC * (e + 1) + n // 2, n % 2)
                        side(i, 8 * e + n)
                    pe.wait_ge(sem("gelu"), at4(i, inst, UNITS, HC * (e + 1)))
                    claim("2")
                    for n in range(4):
                        for j in (2 * n, 2 * n + 1):
                            for h in range(HC):
                                w = (e * HC + h) * C
                                last = pe.matmul(pair[2][:, j * P:(j + 1) * P], hid[(HC * e + h) % 4][:, j * P:(j + 1) * P],
                                                 const("w2" + f)[:, w:w + C], start=(h == 0), stop=(h == HC - 1))
                        if n % 2:
                            last.then_inc(sem("expert"), 1)
                        side(i, 8 * e + 4 + n)

            def body(i, more):
                chunks(i, 0)
                sampling(i, 0, woven(lambda i, n: start(i, 1, n), placed(START_PLACES["pe"])))
                chunks(i, 1)
                sampling(i, 1, woven(lambda i, n: mid0(i, 0, n), placed(MID0_PLACES["pe"])))
                attention(i, 0, 0, q1, k1, woven(lambda i, n: mid0(i, 1, n), MID0_ATTENTION_PACE))
                pe.wait_ge(sem("late_loaded"), 16)
                attention(i, 1, 1, q1, k1, woven(lambda i, n: mid1(i, 0, n), MID1_PACE))
                attention(i, 0, 2, qT, kT, woven(lambda i, n: mid1(i, 1, n), MID1_PACE))
                attention(i, 1, 3, qT, kT, woven(lambda i, n: gating(i, 0, 0, "lnf2", "a", n), GATING_ATTENTION_PACE))
                experts(i, 0, 0, "lnf2", "a", woven(lambda i, n: gating(i, 1, 1, "lnf2", "a", n), GATING_EXPERTS_PACE))
                experts(i, 1, 1, "lnf2", "a", woven(lambda i, n: between1(i, 0, n), BETWEEN_PACE))
                experts(i, 0, 2, "lnf3", "b", woven(lambda i, n: between1(i, 1, n), BETWEEN_PACE))

                next_start = woven(lambda i, n: start(i + 1, 0, n), NEXT_START_PACE)

                def last_side(i, n):
                    if n < 4:
                        finish(i, 0, n)
                    elif more:
                        next_start(i, n)

                experts(i, 1, 3, "lnf3", "b", last_side)
                for step in range(2):
                    finish(i, 1, step)

            pe.wait_ge(sem("start_loaded"), 16)
            for step in range(STEPS):
                start(0, 0, step)
            pe.wait_ge(sem("early_loaded"), 32)
            before = dict(uses)
            with pe.Fori(0, BODIES - 1) as i:
                now[0] = i
                body(i, True)
            assert all(uses[b] - before[b] == totals[b] for b in BANKS), {b: uses[b] - before[b] for b in BANKS}
            uses.update(before)
            now[0] = BODIES - 1
            body(BODIES - 1, False)

        @block.scalar
        def _(act):
            def half_out(i, s, bank, dst, h, ready, value, done, **kw):
                act.wait_ge(sem(ready), value)
                out = dst[:, h * 512:(h + 1) * 512]
                released(act.activation(out, p3[bank][0:dst.shape[0], :], ACT.Identity if kw else ACT.Copy, **kw), bank)
                act.drain().then_inc(sem(done), 1)

            def start(i, s, step):
                if step in (12, 13):
                    part = step - 11
                    act.wait_ge(sem("offs_cut"), at(i, s, 2, part))
                    act.activation(offs[s][32 * part:32 * part + NOFF, :], offcut[s][part - 1], ACT.Copy)\
                        .then_inc(sem("offs_split"), 1)

            def mid0(i, s, step):
                if step in (10, 14, 18, 22):
                    n = (step - 10) // 4
                    bank = mid0_bank(s, n)
                    bias = const(("bq1", "bk1")[n // 2])
                    cols = slice(512 * (n % 2), 512 * (n % 2) + 512)
                    act.wait_ge(sem("proj1"), at(i, s, 4, n + 1))
                    act.activation(qk1_full(s, n), p3[bank][:, :], ACT.Identity, bias=bias)
                    released(act.activation((q1, k1)[n // 2][s][:, cols], p3[bank][:, :], ACT.Identity, bias=bias), bank)
                    act.drain().then_inc(sem("qk1_high"), 1)

            def mid1(i, s, step):
                if step in (12, 14):
                    half_out(i, s, "3b", tnT[s], (step - 12) // 2, "ln2_T", at(i, s, 2, (step - 12) // 2 + 1), "ln2_tnT")
                elif step in (16, 18):
                    n = (step - 16) // 2
                    half_out(i, s, "3b", qT[s], n, "proj2", at(i, s, 4, n + 1), "qk2_kept", bias=bqs[:, 0:1],
                             scale=float(C) ** -0.5)
                elif step in (20, 22):
                    n = (step - 16) // 2
                    half_out(i, s, "3b", kT[s], n % 2, "proj2", at(i, s, 4, n + 1), "qk2_kept", bias=const("bk2"))

            def gating(i, s, inst, which, f, step):
                if step in (4, 6):
                    n = (step - 4) // 2
                    cols = slice(512 * n, 512 * n + 512)
                    act.wait_ge(sem(which + "_T"), at(i, s, 2, n + 1))
                    act.activation(tnT[s][:, cols], p3["3b"][:, :], ACT.Copy)
                    released(act.activation(tn_high[s][:, cols], p3["3b"][:, :], ACT.Copy), "3b")
                    act.drain().then_inc(sem(which + "_tnT"), 1)
                elif step == 9:
                    act.wait_ge(sem("logits"), at4(i, inst, 1, 1))
                    act.activation(lg[s][:, :, :], lg[s][:, :, :], ACT.Exp).then_inc(sem("gate_exp"), 1)

            def layer3(i, s, step):
                if step in (4, 6):
                    n = (step - 4) // 2
                    half_out(i, s, ("3a", "3b")[n], tnT[s], n, "ln3_T", at(i, s, 2, n + 1), "ln3_tnT")
                elif step in (8, 10):
                    n = (step - 8) // 2
                    half_out(i, s, "3a", qT[s], n, "q3", at(i, s, 2, n + 1), "q3_kept", bias=const("bq3"))
                elif step == 15:
                    act.wait_ge(sem("kv3_centred"), at(i, s, 1, 1))
                    act.activation(prob[:, 0:2 * N], kv[s], ACT.Square).then_inc(sem("kv3_squared"), 1)
                elif step == 17:
                    act.wait_ge(sem("kv3_sumsq"), at(i, s, 1, 1))
                    act.activation(hm[s][:, :], hm[s][:, :], ACT.Sqrt, scale=1.0 / (HEADC - 1)).then_inc(sem("kv3_std"), 1)
                elif step == 27:
                    act.wait_ge(sem("p3_biased"), at(i, s, 1, 1))
                    act.activation(tn[s][:, :, :], tn[s][:, :, :], ACT.Gelu).then_inc(sem("p3_gelu"), 1)

            def between1(i, s, step):
                if step < 30:
                    layer3(i, s, step)
                else:
                    gating(i, s, 2 + s, "lnf3", "b", step - 30)

            def finish(i, s, step):
                if step in (1, 2):
                    h = step - 1
                    act.wait_ge(sem("final_T"), at(i, s, 2, h + 1))
                    bank = ("3a", "3b")[h]
                    released(act.activation(xo[s][:, h * 512:(h + 1) * 512], p3[bank][:, :], ACT.Copy), bank)
                elif step == 3:
                    act.drain().then_inc(sem("xo_ready"), 1)
                    act.wait_ge(sem("xo_ready"), at(i, s, 1, 1))
                    act.dma_start(out[i * SLOTS + s].rearrange("c h w -> c (h w)"), xo[s][:, :])\
                        .then_inc(sem(f"stored{s}"), 16)

            def chunks(i, s):
                for g in range(0, 3 * NT, 2):
                    c, third = divmod(g, 3)
                    act.wait_ge(sem("z_ready"), at(i, s, 3 * NT, g + 1))
                    released(act.activation(z[:, c, 3 * third:3 * third + 3, :],
                                            p3["3a"][:, 0:384].rearrange("p (a b) -> p a b", a=3), ACT.Copy, scale=-1.0), "3a")
                act.drain().then_inc(sem("z_kept"), 3 * NT // 2)

            def sampling(i, s, side):
                def x_distance(k):
                    return act.activation(hx[k % 2], pair[1][:, :], ACT.Abs, bias=const("xneg"))

                def x_hat(k):
                    act.drain()
                    act.activation(hx[k % 2], hx[k % 2], ACT.Relu, bias=1.0, scale=-1.0)

                def y_distance(n, c, lo, hi):
                    return act.activation(ay[n % RING][:, 0:hi - lo], pair[2][:, lo:hi], ACT.Abs, bias=const("yneg")[:, c:c + 1])

                for n, (k, c, lo, hi) in enumerate(NEAR):
                    if n % NT == 0:
                        act.wait_ge(sem("spread"), at(i, s, 2 * TAPS, 2 * k + 1))
                        released(x_distance(k), "1")
                        x_hat(k)
                        act.wait_ge(sem("spread"), at(i, s, 2 * TAPS, 2 * k + 2))
                    if n % 2 == 0:
                        act.wait_ge(sem("even_hat_ready"), at(i, s, len(NEAR) // 2, n // 2 + 1))
                        act.wait_ge(sem("odd_hat_ready"), at(i, s, len(NEAR) // 2, n // 2 + 1))
                    if n == len(NEAR) - 1:
                        act.wait_ge(sem("far_known"), at(i, s, 1, 1))
                    y_distance(n, c, lo, hi).then_inc(sem("ay_ready"), 1)
                    if n % NT == NT - 1:
                        act.drain().then_inc(sem("free2"), 1)
                    if n % 2:
                        side(i, n // 2)
                flag = act.value_load(isfar[s][0:1, 0:1], min_val=0, max_val=1)
                with act.If(flag > 0):
                    act.wait_ge(sem("even_hat_ready"), (at(i, s, len(NEAR) // 2, len(NEAR) // 2) + RING // 2))
                    act.wait_ge(sem("odd_hat_ready"), (at(i, s, len(NEAR) // 2, len(NEAR) // 2) + RING // 2))
                    for n, (k, c, lo, hi) in enumerate(FAR):
                        if n == 0 or FAR[n - 1][0] != k:
                            act.wait_ge(sem("far_spread"), at(i, s, 2 * TAPS, 2 * k + 1))
                            x_distance(k).then_inc(sem("far_free1"), 1)
                            x_hat(k)
                            act.wait_ge(sem("far_spread"), at(i, s, 2 * TAPS, 2 * k + 2))
                        if n >= RING:
                            act.wait_ge(sem("far_hat_ready"), at(i, s, len(FAR), n - RING + 1))
                        y_distance(n, c, lo, hi).then_inc(sem("far_ay_ready"), 1)
                        if n + 1 == len(FAR) or FAR[n + 1][0] != k:
                            act.drain().then_inc(sem("far_free2"), 1)
                with act.Else():
                    act.drain().then_inc(sem("far_free1"), TAPS)
                    act.drain().then_inc(sem("far_free2"), TAPS)
                    act.drain().then_inc(sem("far_ay_ready"), len(FAR))

            def attention(i, s, inst, side):
                for j in range(NT + 3):
                    if j < NT:
                        act.wait_ge(sem("nmax"), at4(i, inst, NT, j + 1))
                        act.activation(pr[j % 3], pair[j % 2][:, :], ACT.Exp, bias=nmax[s][:, j:j + 1],
                                       accum_out=rsum[s][:, j:j + 1]).then_inc(sem(f"free{j % 2}"), 1)
                        act.drain().then_inc(sem("prob_exp"), 1)
                    side(i, 3 * j)
                    if 2 <= j < NT + 2:
                        jj = j - 2
                        act.wait_ge(sem("prob_T"), at4(i, inst, NT, jj + 1))
                        act.wait_ge(sem("pv"), at4(i, inst, NT, jj + 1))
                        released(act.activation(prT[jj % 2].rearrange("p a b -> p (a b)"), pair[2][:, :], ACT.Copy), "2")
                        act.drain().then_inc(sem("probT_kept"), 1)
                    side(i, 3 * j + 1)
                    side(i, 3 * j + 2)

            def experts(i, s, inst, which, f, side):
                def gelu(u):
                    act.wait_ge(sem("hidden"), at4(i, inst, UNITS, u + 1))
                    act.activation(hid[u % 4], pair[u % 2][:, :], ACT.Gelu, bias=const("b1" + f)[:, u:u + 1])\
                        .then_inc(sem(f"free{u % 2}"), 1)
                    act.drain().then_inc(sem("gelu"), 1)

                for u in range(HC):
                    act.wait_ge(sem("expert"), at4(i, inst, 2 * E, 4))
                    gelu(u)
                for e in range(E):
                    for n in range(8):
                        side(i, 8 * e + n)
                        if n in (1, 3) and e + 1 < E:
                            act.wait_ge(sem("expert"), at4(i, inst, 2 * E, 2 * e + 4))
                            gelu(HC * (e + 1) + n // 2)

            def body(i, more):
                chunks(i, 0)
                sampling(i, 0, woven(lambda i, n: start(i, 1, n), placed(START_PLACES["act"])))
                chunks(i, 1)
                sampling(i, 1, woven(lambda i, n: mid0(i, 0, n), placed(MID0_PLACES["act"])))
                attention(i, 0, 0, woven(lambda i, n: mid0(i, 1, n), MID0_ATTENTION_PACE))
                act.wait_ge(sem("late_loaded"), 16)
                act.mul(bqs[:, :], const("bq2"), float(C) ** -0.5)
                act.drain()
                attention(i, 1, 1, woven(lambda i, n: mid1(i, 0, n), MID1_PACE))
                attention(i, 0, 2, woven(lambda i, n: mid1(i, 1, n), MID1_PACE))
                attention(i, 1, 3, woven(lambda i, n: gating(i, 0, 0, "lnf2", "a", n), GATING_ATTENTION_PACE))
                experts(i, 0, 0, "lnf2", "a", woven(lambda i, n: gating(i, 1, 1, "lnf2", "a", n), GATING_EXPERTS_PACE))
                experts(i, 1, 1, "lnf2", "a", woven(lambda i, n: between1(i, 0, n), BETWEEN_PACE))
                experts(i, 0, 2, "lnf3", "b", woven(lambda i, n: between1(i, 1, n), BETWEEN_PACE))

                next_start = woven(lambda i, n: start(i + 1, 0, n), NEXT_START_PACE)

                def last_side(i, n):
                    if n < 4:
                        finish(i, 0, n)
                    elif more:
                        next_start(i, n)

                experts(i, 1, 3, "lnf3", "b", last_side)
                for step in range(4):
                    finish(i, 1, step)
                for s in range(SLOTS):
                    act.wait_ge(sem(f"stored{s}"), 16 * i + 16)

            act.dma_start(early_sb[:, start_cols:en], early_in[:, start_cols:en]).then_inc(sem("early_loaded"), 16)
            act.dma_start(sel[:, :], sel_in).then_inc(sem("early_loaded"), 16)
            act.wait_ge(sem("early_loaded"), 32)
            act.dma_start(late_sb[:, :], late_in).then_inc(sem("late_loaded"), 16)
            act.wait_ge(sem("pads_zero"), 1)
            act.wait_ge(sem("seeded"), 1)
            for step in range(STEPS):
                start(0, 0, step)
            with act.Fori(0, BODIES - 1) as i:
                body(i, True)
            body(BODIES - 1, False)

        @block.vector
        def _(dve):
            def over_tiles(row, n=NT):
                return row.rearrange("p (a b) -> p a b", a=1).to_broadcast([row.shape[0], n, row.shape[1]])

            def inner(col, n):
                return col.rearrange("p (a b) -> p a b", b=1).to_broadcast([P, col.shape[1], n])

            def tiled(bank, n=4):
                return p3[bank][:, :].rearrange("p (a b) -> p a b", a=n)

            def group_norm(i, s, which, src, step):
                if step == 0:
                    for h in range(2):
                        dve.bn_stats(bst[s][:, 6 * h:6 * h + 6], src[:, 512 * h:512 * h + 512])
                    dve.drain()
                    dve.bn_aggr(mv[s][:, 0, :], bst[s][:, 0:12])
                    dve.drain()
                    dve.tensor_copy(gst[s][:, 0:1], mv[s][:, 0, 0:1]).then_inc(sem(which + "_stat"), 1)
                elif step == 2:
                    dve.wait_ge(sem(which + "_group"), at(i, s, 2, 1))
                    released(dve.tensor_copy(gst[s][:, 2:3], p3["3b"][:, 0:1]), "3b")
                    dve.drain()
                    dve.tensor_tensor(gst[s][:, 3:4], mv[s][:, 0, 0:1], gst[s][:, 2:3], ALU.subtract)
                    dve.drain()
                    dve.scalar_tensor_tensor(gst[s][:, 1:2], gst[s][:, 3:4], gst[s][:, 3:4], mv[s][:, 0, 1:2],
                                             ALU.mult, ALU.add).then_inc(sem(which + "_stat"), 1)
                elif step == 4:
                    dve.wait_ge(sem(which + "_group"), at(i, s, 2, 2))
                    released(dve.tensor_scalar(var[s][:, 0:1], p3["3b"][:, 0:1], GN_EPS, None, ALU.add), "3b")
                    dve.drain().then_inc(sem(which + "_var"), 1)
                elif step == 6:
                    dve.wait_ge(sem(which + "_rstd"), at(i, s, 1, 1))
                    dve.scalar_tensor_tensor(nmr[s][:, 0:1], gst[s][:, 2:3], -1.0, rstd[s][:, 0:1], ALU.mult, ALU.mult)
                    dve.drain()
                    dve.tensor_scalar(xn[s][:, :], src, rstd[s][:, 0:1], nmr[s][:, 0:1], ALU.mult, ALU.add)\
                        .then_inc(sem(which + "_xn"), 1)

            def start(i, s, step):
                if step == 0:
                    dve.wait_ge(sem(f"x_loaded{s}"), 16 * i + 16)
                if step <= 6:
                    group_norm(i, s, "gn0", ximg[s], step)
                elif step in (8, 9):
                    h = step - 8
                    bank = ("3a", "3b")[h]
                    cols = slice(512 * h, 512 * h + 512)
                    dve.wait_ge(sem("off_ready"), at(i, s, 2, h + 1))
                    dve.scalar_tensor_tensor(pos[:, cols], p3[bank][32:32 + NOFF, :], const("offb"), const("base")[:, cols],
                                             ALU.add, ALU.add)
                    mid, left, right = (v.rearrange("p (a b) -> p a b", b=HW) for v in
                                        (pos[:, cols], p3[bank][0:NOFF, :], p3[bank][64:64 + NOFF, :]))
                    dve.drain()
                    dve.tensor_tensor(mid[:, :, 1:HW], left[:, :, 0:HW - 1], mid[:, :, 1:HW], ALU.add)
                    dve.drain()
                    released(dve.tensor_tensor(mid[:, :, 0:HW - 1], right[:, :, 1:HW], mid[:, :, 0:HW - 1], ALU.add), bank)
                    dve.drain()
                elif step == 10:
                    dve.tensor_copy(offs[s][0:NOFF, :], pos)
                    dve.drain()
                    dve.tensor_tensor(rest, pos, offs[s][0:NOFF, :], ALU.subtract)
                    dve.drain().then_inc(sem("offs_split"), 1)
                elif step == 11:
                    dve.tensor_copy(offcut[s][0], rest)
                    dve.drain().then_inc(sem("offs_cut"), 1)
                    dve.tensor_tensor(offcut[s][1], rest, offcut[s][0], ALU.subtract)
                    dve.drain().then_inc(sem("offs_cut"), 1)
                elif step == 13:
                    dve.tensor_tensor(rest, pos, const("base"), ALU.subtract)
                    dve.drain()
                    dve.tensor_reduce(dymax[:, :], rest, AX.X, ALU.max, apply_absolute_value=True)
                    dve.drain()
                    dve.tensor_scalar(dymax[:, :], dymax[:, :], const("isy"), None, ALU.mult)
                    dve.drain()
                    dve.tensor_scalar(dyok[:, :], const("ones"), dymax[:, 0:1], float(REACH), ALU.mult, ALU.is_lt)\
                        .then_inc(sem("dy_checked"), 1)
                elif step == 16:
                    dve.wait_ge(sem("dy_count"), at(i, s, 1, 1))
                    released(dve.tensor_scalar(isfar[s][:, :], p3["3a"][0:1, 0:1], NOFF - 0.5, None, ALU.is_lt), "3a")
                    dve.drain().then_inc(sem("far_known"), 1)

            def keep_v(i, s, h, bank, ready, bias, done):
                dve.wait_ge(sem(ready), at(i, s, 2, h + 1))
                released(dve.tensor_tensor(vt[s][:, 4 * h:4 * h + 4, :], tiled(bank), over_tiles(const(bias), 4), ALU.add), bank)
                dve.drain().then_inc(sem(done), 1)

            def mid0(i, s, step):
                if step <= 6:
                    group_norm(i, s, "gn1", xc[s][:, :], step)
                if step in (12, 16, 20, 24):
                    n = (step - 12) // 4
                    cols = slice(512 * (n % 2), 512 * (n % 2) + 512)
                    dve.wait_ge(sem("qk1_high"), at(i, s, 4, n + 1))
                    for lo, hi in (((64, 128),), ((32, 64), (96, 128)))[n // 2]:
                        part = (q1, k1)[n // 2][s][lo:hi, cols]
                        dve.tensor_tensor(part, qk1_full(s, n)[lo:hi, :], part.bitcast(F32), ALU.subtract)
                    dve.drain().then_inc(sem("qk1_kept"), 1)
                if step in (24, 26):
                    keep_v(i, s, (step - 24) // 2, mid0_bank(s, (step - 24) // 2), "v1", "bv1", "v1_kept")

            def layer_norm(i, s, which, step):
                if step == 0:
                    for j in range(NT):
                        dve.bn_stats(bst[s][:, 6 * j:6 * j + 6], tok[s][:, j, :])
                    dve.drain()
                    for j in range(NT):
                        dve.bn_aggr(mv[s][:, j, :], bst[s][:, 6 * j:6 * j + 6])
                    dve.drain()
                    dve.tensor_scalar(var[s][:, :], mv[s][:, :, 1], LN_EPS, None, ALU.add).then_inc(sem(which + "_var"), 1)
                elif step == 2:
                    dve.wait_ge(sem(which + "_rstd"), at(i, s, 1, 1))
                    dve.scalar_tensor_tensor(nmr[s][:, :], mv[s][:, :, 0], -1.0, rstd[s][:, :], ALU.mult, ALU.mult)
                    dve.drain()
                    for j in range(NT):
                        dve.tensor_scalar(tn[s][:, j, :], tok[s][:, j, :], rstd[s][:, j:j + 1], nmr[s][:, j:j + 1],
                                          ALU.mult, ALU.add)
                    dve.drain().then_inc(sem(which + "_tn"), 1)

            def mid1(i, s, step):
                if step in (1, 3):
                    h = step // 2
                    cols = slice(512 * h, 512 * h + 512)
                    dve.wait_ge(sem("att1_T"), at(i, s, 2, h + 1))
                    released(dve.tensor_tensor(xn[s][:, cols], p3["3b"][:, :], xn[s][:, cols], ALU.add), "3b")
                    dve.drain().then_inc(sem("y1_kept"), 1)
                elif step in (5, 7):
                    h = (step - 5) // 2
                    dve.wait_ge(sem("tok1"), at(i, s, 2, h + 1))
                    released(dve.tensor_tensor(tn[s][:, 4 * h:4 * h + 4, :], tiled("3b"), over_tiles(const("bo1"), 4),
                                               ALU.add), "3b")
                elif step == 8:
                    dve.drain()
                    dve.tensor_copy(tok[s][:, :, :], tn[s][:, :, :])
                    dve.drain()
                    layer_norm(i, s, "ln2", 0)
                elif step == 10:
                    layer_norm(i, s, "ln2", 2)
                elif step in (24, 26):
                    keep_v(i, s, (step - 24) // 2, "3b", "v2", "bv2", "v2_kept")

            def gating(i, s, inst, which, f, step):
                if step in (0, 2):
                    layer_norm(i, s, which, step)
                elif step in (5, 7):
                    n = (step - 5) // 2
                    cols = slice(512 * n, 512 * n + 512)
                    dve.wait_ge(sem(which + "_tnT"), at(i, s, 2, n + 1))
                    dve.tensor_tensor(tn_low[s][:, cols], tnT[s][:, cols], tn_high[s][:, cols].bitcast(F32), ALU.subtract)
                    dve.drain().then_inc(sem(which + "_tn_split"), 1)
                elif step == 8:
                    dve.wait_ge(sem("gate"), at4(i, inst, 1, 1))
                    released(dve.tensor_tensor(lg[s][:, :, :], p3["3b"][:, 0:NT * E].rearrange("p (a b) -> p a b", a=NT),
                                               over_tiles(const("gb" + f)), ALU.add), "3b")
                    dve.drain()
                    dve.tensor_reduce(gmx[s][:, :], lg[s][:, :, :], AX.X, ALU.max)
                    dve.drain()
                    dve.tensor_tensor(lg[s][:, :, :], lg[s][:, :, :], inner(gmx[s][:, :], E), ALU.subtract)\
                        .then_inc(sem("logits"), 1)
                elif step == 10:
                    dve.wait_ge(sem("gate_exp"), at4(i, inst, 1, 1))
                    dve.tensor_reduce(gsum[s][:, :], lg[s][:, :, :], AX.X, ALU.add)
                    dve.drain()
                    dve.reciprocal(gsum[s][:, :], gsum[s][:, :])
                    dve.drain()
                    dve.tensor_tensor(lg[s][:, :, :], lg[s][:, :, :], inner(gsum[s][:, :], E), ALU.mult)
                    dve.drain()
                elif step == 11:
                    other = lg[s][:, :, :].rearrange("p a (o b) -> p a o b", o=1).to_broadcast([P, NT, E, E])
                    own = lg[s][:, :, :].rearrange("p a (b o) -> p a b o", o=1).to_broadcast([P, NT, E, E])
                    lower = const("low").rearrange("p (o b c) -> p o b c", o=1, b=E).to_broadcast([P, NT, E, E])
                    wins, ties = (kv[s][:, r * NT * E * E:(r + 1) * NT * E * E].rearrange("p (a b c) -> p a b c", a=NT, b=E)
                                  for r in range(2))
                    dve.tensor_tensor(wins, other, own, ALU.is_gt)
                    dve.tensor_tensor(ties, other, own, ALU.is_equal)
                    dve.drain()
                    dve.tensor_tensor(ties, ties, lower, ALU.mult)
                    dve.drain()
                    dve.tensor_tensor(wins, wins, ties, ALU.add)
                    dve.drain()
                    dve.tensor_reduce(cw[s][:, :, :], wins, AX.X, ALU.add)
                    dve.drain()
                    dve.scalar_tensor_tensor(cw[s][:, :, :], cw[s][:, :, :], 1.5, lg[s][:, :, :], ALU.is_lt, ALU.mult)\
                        .then_inc(sem("cw"), 1)
                elif step == 13:
                    dve.wait_ge(sem("cw_T"), at4(i, inst, 1, 1))
                    released(dve.tensor_copy(cwT[s][:, :], p3["3b"][0:NT * E, 0:P]), "3b")
                    dve.drain().then_inc(sem("cwT_kept"), 1)
                elif step in (15, 17):
                    h = (step - 15) // 2
                    dve.wait_ge(sem("bias2"), at4(i, inst, 2, h + 1))
                    part = tok[s][:, 4 * h:4 * h + 4, :]
                    released(dve.tensor_tensor(part, tiled("3b"), part, ALU.add), "3b")
                    dve.drain()

            def layer3(i, s, step):
                kvs = kv[s].rearrange("p (a b) -> p a b", a=NT)
                heads = kv[s].rearrange("p (g d) -> p g d", d=HEADC)
                if step in (0, 2):
                    layer_norm(i, s, "ln3", step)
                elif step in (9, 11, 12, 13):
                    g = {9: 0, 11: 1, 12: 2, 13: 3}[step]
                    bank = ("3b", "3b", "3a", "3b")[g]
                    dve.wait_ge(sem("kv3"), at(i, s, 4, g + 1))
                    released(dve.tensor_tensor(kvs[:, 2 * g:2 * g + 2, :], tiled(bank, 2), over_tiles(const("bkv3"), 2),
                                               ALU.add), bank)
                    if g == 3:
                        dve.drain().then_inc(sem("kv3_centred"), 1)
                elif step == 16:
                    dve.wait_ge(sem("kv3_squared"), at(i, s, 1, 1))
                    dve.tensor_reduce(hm[s][:, :], prob[:, 0:2 * N].rearrange("p (g d) -> p g d", d=HEADC), AX.X, ALU.add)\
                        .then_inc(sem("kv3_sumsq"), 1)
                elif step == 18:
                    dve.wait_ge(sem("kv3_std"), at(i, s, 1, 1))
                    dve.tensor_scalar(hm[s][:, :], hm[s][:, :], HEAD_EPS, None, ALU.add)
                    dve.drain()
                    dve.reciprocal(hm[s][:, :], hm[s][:, :])
                    dve.drain()
                    dve.tensor_tensor(heads, heads, inner(hm[s][:, :], HEADC), ALU.mult)
                elif step == 19:
                    dve.drain()
                    dve.tensor_tensor(kvs, kvs, over_tiles(const("lnw3")), ALU.mult)
                    dve.drain()
                    dve.tensor_tensor(kvs, kvs, over_tiles(const("lnb3")), ALU.add).then_inc(sem("kv3_normed"), 1)
                elif step == 21:
                    dve.wait_ge(sem("state3"), at(i, s, 1, 1))
                    released(dve.tensor_tensor(kvm[s][:, :], p3["3a"][:, 0:P], const("kvmask"), ALU.mult), "3a")
                    dve.drain().then_inc(sem("state3_kept"), 1)
                elif step in (23, 24):
                    h = step - 23
                    cols = slice(512 * h, 512 * h + 512)
                    bank = ("3a", "3b")[h]
                    dve.wait_ge(sem("read3"), at(i, s, 2, h + 1))
                    released(dve.tensor_tensor(kT[s][:, cols], p3[bank][:, :], tnT[s][:, cols], ALU.add), bank)
                    dve.drain().then_inc(sem("ret3_kept"), 1)
                elif step in (26, 27):
                    h = step - 26
                    bank = ("3a", "3b")[h]
                    if h == 0:
                        dve.wait_ge(sem("tok3_res"), at(i, s, 1, 1))
                    dve.wait_ge(sem("proj3"), at(i, s, 2, h + 1))
                    released(dve.tensor_tensor(tn[s][:, 4 * h:4 * h + 4, :], tiled(bank), over_tiles(const("bp3"), 4), ALU.add), bank)
                    if h:
                        dve.drain().then_inc(sem("p3_biased"), 1)
                elif step == 28:
                    dve.drain().then_inc(sem(f"ximg_free{s}"), 1)
                elif step == 29:
                    dve.wait_ge(sem("p3_gelu"), at(i, s, 1, 1))
                    dve.tensor_tensor(tok[s][:, :, :], tok[s][:, :, :], tn[s][:, :, :], ALU.add)
                    dve.drain()

            def between1(i, s, step):
                if step < 30:
                    layer3(i, s, step)
                else:
                    gating(i, s, 2 + s, "lnf3", "b", step - 30)

            def chunks(i, s):
                for g in range(1, 3 * NT, 2):
                    c, third = divmod(g, 3)
                    dve.wait_ge(sem("z_ready"), at(i, s, 3 * NT, g + 1))
                    released(dve.tensor_scalar(z[:, c, 3 * third:3 * third + 3, :],
                                               p3["3b"][:, 0:384].rearrange("p (a b) -> p a b", a=3), -1.0, None, ALU.mult), "3b")
                dve.drain().then_inc(sem("z_kept"), 3 * NT // 2)

            def sampling(i, s, side):
                def y_hat(n, lo, hi):
                    dve.tensor_scalar(ay[n % RING][:, 0:hi - lo], ay[n % RING][:, 0:hi - lo], 1.0, 0.0, ALU.subtract, ALU.min)

                def product(n, k, lo, hi):
                    return dve.tensor_tensor(hat[n % RING][:, 0:hi - lo], ay[n % RING][:, 0:hi - lo], hx[k % 2][:, lo:hi],
                                             ALU.mult)

                def hats(n):
                    dve.wait_ge(sem("ay_ready"), at(i, s, len(NEAR), n + 2))
                    for m in (n, n + 1):
                        y_hat(m, *NEAR[m][2:])

                hats(0)
                dve.drain().then_inc(sem("y_hats"), 1)
                for n in range(0, len(NEAR), 2):
                    if n + 2 < len(NEAR):
                        hats(n + 2)
                        dve.drain().then_inc(sem("y_hats"), 1)
                    dve.wait_ge(sem("hat_used"), at(i, s, len(NEAR), n + 2))
                    if n == len(NEAR) - 2:
                        dve.wait_ge(sem("far_known"), at(i, s, 1, 1))
                    k, c, lo, hi = NEAR[n]
                    product(n, k, lo, hi).then_inc(sem("even_hat_ready"), 1)
                    side(i, n // 2)
                flag = dve.value_load(isfar[s][0:1, 0:1], min_val=0, max_val=1)
                with dve.If(flag > 0):
                    dve.wait_ge(sem("hat_used"), at(i, s, len(NEAR), len(NEAR)) + RING)
                    for n, (k, c, lo, hi) in enumerate(FAR):
                        dve.wait_ge(sem("far_ay_ready"), at(i, s, len(FAR), n + 1))
                        y_hat(n, lo, hi)
                        dve.drain()
                        if n >= RING:
                            dve.wait_ge(sem("far_hat_used"), at(i, s, len(FAR), n - RING + 1))
                        product(n, k, lo, hi).then_inc(sem("far_hat_ready"), 1)
                with dve.Else():
                    dve.drain().then_inc(sem("far_hat_ready"), len(FAR))
                dve.wait_ge(sem("hat_used"), at(i, s, len(NEAR), len(NEAR)) + RING)
                dve.wait_ge(sem("far_hat_used"), at(i, s, len(FAR), len(FAR)))
                released(dve.scalar_tensor_tensor(xc[s][:, :], pair[0][:, :], const("b0"), ximg[s][:, :], ALU.add, ALU.add), "0")
                dve.drain()

            def attention(i, s, inst, side):
                for j in range(NT + 3):
                    if j < NT:
                        dve.wait_ge(sem("energy"), at4(i, inst, NT, j + 1))
                        dve.tensor_reduce(nmax[s][:, j:j + 1], pair[j % 2][:, :], AX.X, ALU.max, negate=True)\
                            .then_inc(sem("nmax"), 1)
                    side(i, 3 * j)
                    if inst >= 2 and 1 <= j <= NT:
                        jj = j - 1
                        off = (NT - 1 - jj) * P
                        dve.wait_ge(sem("prob_exp"), at4(i, inst, NT, jj + 1))
                        dve.tensor_tensor_reduce(out=pr[jj % 3], in0=pr[jj % 3], in1=const("toep")[:, off:off + N],
                                                 scale=1.0, scalar=0.0, op0=ALU.mult, op1=ALU.add,
                                                 accum_out=rsum[s][:, jj:jj + 1])
                        dve.drain().then_inc(sem("prob_biased"), 1)
                    side(i, 3 * j + 1)
                    if j >= 3:
                        jj = j - 3
                        dve.wait_ge(sem("pv"), at4(i, inst, NT, jj + 1) + 2)
                        dve.reciprocal(rinv[s][:, jj:jj + 1], rsum[s][:, jj:jj + 1])
                        dve.drain()
                        if inst < 2:
                            ins = dve.tensor_scalar(tn[s][:, jj, :], p3["3a"][:, 0:P], rinv[s][:, jj:jj + 1], None, ALU.mult)
                        else:
                            ins = dve.scalar_tensor_tensor(tok[s][:, jj, :], p3["3a"][:, 0:P], rinv[s][:, jj:jj + 1],
                                                           tok[s][:, jj, :], ALU.mult, ALU.add)
                        released(ins, "3a")
                        dve.drain().then_inc(sem("o_kept"), 1)
                    side(i, 3 * j + 2)

            def experts(i, s, inst, side):
                for e in range(E):
                    for n in range(8):
                        side(i, 8 * e + n)
                        if n in (5, 7):
                            h = n // 2 - 2
                            dve.wait_ge(sem("expert"), at4(i, inst, 2 * E, 2 * e + h + 1) + 4)
                            for j in range(4 * h, 4 * h + 4):
                                ins = dve.scalar_tensor_tensor(tok[s][:, j, :], pair[2][:, j * P:(j + 1) * P],
                                                               cw[s][:, j, e:e + 1], tok[s][:, j, :], ALU.mult, ALU.add)
                            if h:
                                released(ins, "2")
                            dve.drain()

            def body(i, more):
                chunks(i, 0)
                sampling(i, 0, woven(lambda i, n: start(i, 1, n), placed(START_PLACES["dve"])))
                chunks(i, 1)
                sampling(i, 1, woven(lambda i, n: mid0(i, 0, n), placed(MID0_PLACES["dve"])))
                attention(i, 0, 0, woven(lambda i, n: mid0(i, 1, n), MID0_ATTENTION_PACE))
                dve.wait_ge(sem("late_loaded"), 16)
                attention(i, 1, 1, woven(lambda i, n: mid1(i, 0, n), MID1_PACE))
                attention(i, 0, 2, woven(lambda i, n: mid1(i, 1, n), MID1_PACE))
                attention(i, 1, 3, woven(lambda i, n: gating(i, 0, 0, "lnf2", "a", n), GATING_ATTENTION_PACE))
                experts(i, 0, 0, woven(lambda i, n: gating(i, 1, 1, "lnf2", "a", n), GATING_EXPERTS_PACE))
                experts(i, 1, 1, woven(lambda i, n: between1(i, 0, n), BETWEEN_PACE))
                experts(i, 0, 2, woven(lambda i, n: between1(i, 1, n), BETWEEN_PACE))
                dve.drain().then_inc(sem("tok_final"), 1)
                experts(i, 1, 3, woven(lambda i, n: start(i + 1, 0, n), NEXT_START_PACE if more else []))
                dve.drain().then_inc(sem("tok_final"), 1)

            for s in range(SLOTS):
                dve.memset(offs[s][:, :], 0.0)
            for name, n in (("even_hat_ready", RING // 2), ("odd_hat_ready", RING // 2), ("hat_used", RING), ("pv", 2), ("expert", 4), ("seeded", 1),
                            *(("free" + b, 1) for b in BANKS), *((f"ximg_free{s}", 1) for s in range(SLOTS))):
                dve.drain().then_inc(sem(name), n)
            dve.wait_ge(sem("start_loaded"), 16)
            dve.wait_ge(sem("pads_zero"), 1)
            for step in range(STEPS):
                start(0, 0, step)
            dve.wait_ge(sem("early_loaded"), 32)
            for name in ("wkv3", "bkv3"):
                dve.drain()
                weights = const(name).rearrange("p (g d) -> p g d", d=HEADC)
                means = hm[0][:, 0:2 * C // HEADC]
                dve.tensor_reduce(means, weights, AX.X, ALU.add)
                dve.drain()
                dve.tensor_scalar(means, means, 1.0 / HEADC, None, ALU.mult)
                dve.drain()
                dve.tensor_tensor(weights, weights, inner(means, HEADC), ALU.subtract)
            dve.drain()
            with dve.Fori(0, BODIES - 1) as i:
                body(i, True)
            body(BODIES - 1, False)


def packed(part, arrays, np):
    cols, n = columns(part)
    out = np.zeros((P, n), np.float32)
    for name, (at, p, width) in cols.items():
        out[0:p, at:at + width] = arrays[name]
    return out


def kernel(**inputs):
    import ml_dtypes
    import numpy as np
    import concourse.bacc as bacc
    from concourse.bass_utils import run_bass_kernel_spmd

    w = {k: np.asarray(v) for k, v in inputs.items()}
    f = np.float32

    def rows(v):
        return np.broadcast_to(v.reshape(1, -1), (P, v.size))

    def groups(v):
        out = np.zeros((v.shape[0], P // 32, 32), f)
        out[:, :, 0:v.shape[1]] = v[:, None, :]
        return out.reshape(-1, P)

    p, n = np.arange(P), np.arange(N)
    tap = np.arange(TAPS)
    base = np.stack([n // HW + (tap // 3)[:, None] - 1, n % HW + (tap % 3)[:, None] - 1], 1).reshape(NOFF, N)
    gap = np.abs(np.arange(TOEP)[None, :] - (NT - 1) * P - p[:, None]).astype(np.float64)
    decay = (gap + 1e-9) ** (0.1 - 1.5)
    toep = decay / 1e-9 ** (0.1 - 1.5) + 1e-9
    toep = np.where(gap == 0, 1.0 + 1e-9, toep)
    head = p // HEADC
    a = dict(ident=np.eye(P), grp=(p[:, None] // 4 == p // 4) / 4.0, kvmask=(head[:, None] == head) / float(N),
             base=base, yneg=-(ROWS * np.arange(NT)[None, :] + p[:, None] // HW), xneg=-(p[:, None] % HW), toep=toep,
             low=rows((np.arange(E)[None, :] < np.arange(E)[:, None]).astype(f)))
    offw = np.zeros((C, 3, 3, 32), f)
    offw[..., 0:NOFF] = w["L0_conv_offset_w"].transpose(1, 2, 3, 0)
    a.update(offw=offw.reshape(C, -1), isy=(np.arange(NOFF)[:, None] + 1) % 2, ones=np.ones((NOFF, P)), offb=w["L0_conv_offset_b"][:, None],
             w0=w["L0_conv_weight"].transpose(1, 2, 3, 0).reshape(C, -1), b0=w["L0_conv_bias"][:, None],
             wq1=groups(w["L1_conv_Wq"].T), wk1=groups(w["L1_conv_Wk"].T),
             bq1=groups(w["L1_conv_bq"][None, :]).T, bk1=groups(w["L1_conv_bk"][None, :]).T,
             wv1=w["L1_conv_Wv"].T, bv1=rows(w["L1_conv_bv"]), wo1=w["L1_conv_Wo"].T, bo1=rows(w["L1_conv_bo"]))
    a.update(wq2=w["L2_attn_Wq"].T, wk2=w["L2_attn_Wk"].T, bq2=w["L2_attn_bq"][:, None], bk2=w["L2_attn_bk"][:, None],
             wv2=w["L2_attn_Wv"].T, bv2=rows(w["L2_attn_bv"]))
    wqkv = w["L3_attn_W_qkv"].reshape(C // HEADC, 3, HEADC, C).transpose(1, 3, 0, 2).reshape(3, C, C)
    bqkv = w["L3_attn_b_qkv"].reshape(C // HEADC, 3, HEADC).transpose(1, 0, 2).reshape(3, C)
    a.update(wq3=wqkv[0], bq3=bqkv[0][:, None], wkv3=np.concatenate([wqkv[1], wqkv[2]], 1), bkv3=rows(bqkv[1:]),
             lnw3=rows(np.concatenate([w["L3_attn_kln_w"].reshape(-1), w["L3_attn_vln_w"].reshape(-1)])),
             lnb3=rows(np.concatenate([w["L3_attn_kln_b"].reshape(-1), w["L3_attn_vln_b"].reshape(-1)])),
             wp3=w["L3_attn_W_proj"].T, bp3=rows(w["L3_attn_b_proj"]))
    for name, layer in (("a", "L2_ffn_"), ("b", "L3_ffn_")):
        b2 = np.zeros((NT * E, NT * C), f)
        for j in range(NT):
            b2[j * E:(j + 1) * E, j * C:(j + 1) * C] = w[layer + "b2"]
        a["gw" + name] = w[layer + "gate_w"]
        a["gb" + name] = rows(w[layer + "gate_b"])
        a["w1" + name] = w[layer + "W1"].transpose(1, 0, 2).reshape(C, -1)
        a["b1" + name] = w[layer + "b1"].reshape(E * HC, P).T
        a["w2" + name] = w[layer + "W2"].reshape(E * HC, P, C).transpose(1, 0, 2).reshape(P, -1)
        a["b2" + name] = b2
    early, late = layout()
    sel = np.zeros((96, NOFF, P), ml_dtypes.bfloat16)
    for q in range(3):
        for r in range(NOFF):
            sel[32 * q + r, r, :] = 1
    arrays = dict(x=np.ascontiguousarray(w["x"]), sel=sel.reshape(96, -1), early=packed(early, a, np), late=packed(late, a, np))

    nc = bacc.Bacc("TRN2", target_bir_lowering=False, num_devices=1)
    args = [nc.dram_tensor(k, v.shape, mybir.dt.from_np(v.dtype), kind="ExternalInput").ap() for k, v in arrays.items()]
    result = nc.dram_tensor("result", (B, C, HW, HW), F32, kind="ExternalOutput").ap()
    build(nc, *args, result)
    r = run_bass_kernel_spmd(nc, [arrays], core_ids=[0])
    return r.results[0]["result"]
```
